# Optimizing a Trainium2 kernel written in Bass

```python
import numpy as np
import jax
import jax.numpy as jnp

def _softmax(x, axis=-1):
    return jax.nn.softmax(x, axis=axis)

def _gelu(x):
    return jax.nn.gelu(x, approximate=True)

def _silu(x):
    return jax.nn.silu(x)

def _sigmoid(x):
    return jax.nn.sigmoid(x)

def _layernorm(x, axis=-1, eps=1e-05):
    m = jnp.mean(x, axis=axis, keepdims=True)
    v = jnp.var(x, axis=axis, keepdims=True)
    return (x - m) / jnp.sqrt(v + eps)

def _scatter_add(tgt, idx, src, axis=0):
    return tgt.at[idx].add(src)

def _segment_sum(src, seg, n):
    return jax.ops.segment_sum(src, seg, n)
kernel_name = 'mk_lm_tower_d2_tok_ids512_r4_125ea2'

def setup_inputs(seed: int=0):
    np.random.seed(seed)
    _w = jnp.asarray

    def _rec_inputs():
        import jax
        import jax.numpy as jnp
        _rk = jax.random.key(seed)
        x = jax.random.randint(jax.random.fold_in(_rk, 1), (1, 2048), 0, 50257, jnp.int32)
        return x
    x = _rec_inputs()

    def _L0_tok_setup():
        import jax, jax.numpy as jnp
        import numpy as np
        D_MODEL = 128
        VOCAB = 50257
        BATCH = 8
        SEQ = 512

        def _positional_encoding(seq_len, d_model, dtype):
            pos = jnp.arange(1, seq_len + 1, dtype=jnp.float32)[:, None]
            i = jnp.arange(d_model)
            exponent = jnp.where(i % 2 == 0, i, i + 1).astype(jnp.float32) / d_model
            angle = pos / 10000.0 ** exponent
            pe = jnp.where(i % 2 == 0, jnp.cos(angle), jnp.sin(angle))
            return pe.astype(dtype)
        key = jax.random.key(seed)
        k1, k2, k3 = jax.random.split(key, 3)
        x = jax.random.randint(k1, (BATCH, SEQ), 0, VOCAB)
        W = jax.random.normal(k2, (D_MODEL, VOCAB), dtype=jnp.float32) * 0.02
        b = jax.random.normal(k3, (D_MODEL,), dtype=jnp.float32) * 0.02
        return {'x': x, 'W': W, 'b': b}
    _L0_tok_all = _L0_tok_setup()
    _L0_tok_in = {k: v for k, v in _L0_tok_all.items() if k in ('W', 'b')}
    del _L0_tok_all

    def _L0_attn_setup():
        import jax, jax.numpy as jnp
        import numpy as np
        B, T, D = (8, 1024, 128)
        H = 4 * D

        def _xavier(key, fan_in, fan_out):
            lim = float(np.sqrt(6.0 / (fan_in + fan_out)))
            return jax.random.uniform(key, (fan_in, fan_out), jnp.float32, -lim, lim)

        def layer_norm(x, g, b, eps=1e-05):
            m = jnp.mean(x, axis=-1, keepdims=True)
            v = jnp.var(x, axis=-1, keepdims=True)
            return (x - m) * jax.lax.rsqrt(v + eps) * g + b

        def time_shift(x, ratio):
            r = jnp.clip(ratio, 0.0, 1.0)
            xs = jnp.pad(x[:, :-1, :], ((0, 0), (1, 0), (0, 0)))
            return x * r + xs * (1.0 - r)

        def recurrence(w, u, k, v):
            decay = jax.nn.sigmoid(w)
            bonus = jnp.tanh(u)

            def step(state, kv):
                kt, vt = kv
                gate = jax.nn.sigmoid(bonus + kt)
                out = gate * vt + (1.0 - gate) * state
                new_state = decay * state + (1.0 - decay) * vt
                return (new_state, out)
            state0 = jnp.zeros((k.shape[0], k.shape[2]), k.dtype)
            _, outs = jax.lax.scan(step, state0, (k.transpose(1, 0, 2), v.transpose(1, 0, 2)))
            return outs.transpose(1, 0, 2)

        def rwkv_block(x, Wk, bk, Wv, bv, Wr, br, Wo, bo, Wck, bck, Wcv, bcv, Wcr, bcr, ln1_g, ln1_b, ln2_g, ln2_b, time_decay, time_first, tmk, tmv, tmr, cmk, cmr):
            h = layer_norm(x, ln1_g, ln1_b)
            k = time_shift(h, tmk) @ Wk + bk
            v = time_shift(h, tmv) @ Wv + bv
            r = time_shift(h, tmr) @ Wr + br
            rec = recurrence(time_decay, time_first, k, v)
            tm = jnp.tanh(r) * rec @ Wo + bo
            x = x + 0.5 * tm
            h = layer_norm(x, ln2_g, ln2_b)
            ck = time_shift(h, cmk) @ Wck + bck
            cr = time_shift(h, cmr) @ Wcr + bcr
            vv = jax.nn.gelu(ck, approximate=False) @ Wcv + bcv
            x = x + 0.5 * (jnp.tanh(cr) * vv)
            return x
        key = jax.random.key(seed)
        ks = jax.random.split(key, 9)
        inp = {'x': jax.random.normal(ks[0], (B, T, D), jnp.float32), 'Wk': _xavier(ks[1], D, D), 'bk': jnp.zeros((D,), jnp.float32), 'Wv': _xavier(ks[2], D, D), 'bv': jnp.zeros((D,), jnp.float32), 'Wr': _xavier(ks[3], D, D), 'br': jnp.zeros((D,), jnp.float32), 'Wo': _xavier(ks[4], D, D), 'bo': jnp.zeros((D,), jnp.float32), 'Wck': _xavier(ks[5], D, H), 'bck': jnp.zeros((H,), jnp.float32), 'Wcv': _xavier(ks[6], H, D), 'bcv': jnp.zeros((D,), jnp.float32), 'Wcr': _xavier(ks[7], D, D), 'bcr': jnp.zeros((D,), jnp.float32), 'ln1_g': jnp.ones((D,), jnp.float32), 'ln1_b': jnp.zeros((D,), jnp.float32), 'ln2_g': jnp.ones((D,), jnp.float32), 'ln2_b': jnp.zeros((D,), jnp.float32), 'time_decay': jnp.linspace(-0.5, -0.1, D, dtype=jnp.float32), 'time_first': jnp.full((D,), 0.5, jnp.float32), 'tmk': jnp.full((1, 1, D), 0.5, jnp.float32), 'tmv': jnp.full((1, 1, D), 0.5, jnp.float32), 'tmr': jnp.full((1, 1, D), 0.5, jnp.float32), 'cmk': jnp.full((1, 1, D), 0.5, jnp.float32), 'cmr': jnp.full((1, 1, D), 0.5, jnp.float32)}
        return inp
    _L0_attn_all = _L0_attn_setup()
    _L0_attn_in = {k: v for k, v in _L0_attn_all.items() if k in ('Wk', 'bk', 'Wv', 'bv', 'Wr', 'br', 'Wo', 'bo', 'Wck', 'bck', 'Wcv', 'bcv', 'Wcr', 'bcr', 'ln1_g', 'ln1_b', 'ln2_g', 'ln2_b', 'time_decay', 'time_first', 'tmk', 'tmv', 'tmr', 'cmk', 'cmr')}
    del _L0_attn_all

    def _L0_ffn_setup():
        import jax, jax.numpy as jnp
        import numpy as np
        B, S, D, H, E = (4, 512, 128, 8, 8)
        FF = 4 * D
        HD = D // H
        EPS = 1e-05

        def _layernorm(x, g, b):
            mu = jnp.mean(x, axis=-1, keepdims=True)
            var = jnp.mean((x - mu) ** 2, axis=-1, keepdims=True)
            return (x - mu) * jax.lax.rsqrt(var + EPS) * g + b
        key = jax.random.key(seed)
        ks = jax.random.split(key, 16)
        s = 0.02
        return {'x': jax.random.normal(ks[0], (B, S, D), dtype=jnp.float32), 'ln1_g': jnp.ones((D,), jnp.float32), 'ln1_b': jnp.zeros((D,), jnp.float32), 'Wq': jax.random.normal(ks[1], (D, D), jnp.float32) * s, 'bq': jnp.zeros((D,), jnp.float32), 'Wk': jax.random.normal(ks[2], (D, D), jnp.float32) * s, 'bk': jnp.zeros((D,), jnp.float32), 'Wv': jax.random.normal(ks[3], (D, D), jnp.float32) * s, 'bv': jnp.zeros((D,), jnp.float32), 'Wo': jax.random.normal(ks[4], (D, D), jnp.float32) * s, 'bo': jnp.zeros((D,), jnp.float32), 'gate_W': jax.random.normal(ks[5], (D, E), jnp.float32) * s, 'gate_b': jnp.zeros((E,), jnp.float32), 'W1': jax.random.normal(ks[6], (E, D, FF), jnp.float32) * s, 'b1': jnp.zeros((E, FF), jnp.float32), 'W2': jax.random.normal(ks[7], (E, FF, D), jnp.float32) * s, 'b2': jnp.zeros((E, D), jnp.float32)}
    _L0_ffn_all = _L0_ffn_setup()
    _L0_ffn_in = {k: v for k, v in _L0_ffn_all.items() if k in ('ln1_g', 'ln1_b', 'Wq', 'bq', 'Wk', 'bk', 'Wv', 'bv', 'Wo', 'bo', 'gate_W', 'gate_b', 'W1', 'b1', 'W2', 'b2')}
    del _L0_ffn_all

    def _L1_attn_setup():
        import jax, jax.numpy as jnp
        import numpy as np
        DIM = 128
        HEADS = 8
        WS = 64
        G = 32
        SPARSITY = 0.3
        key = jax.random.key(seed)
        ks = jax.random.split(key, 7)
        b, n = (4, 2048)
        x = jax.random.normal(ks[0], (b, n, DIM), dtype=jnp.float32)
        w_qkv = jax.random.normal(ks[1], (DIM, 3 * DIM), dtype=jnp.float32) * DIM ** (-0.5)
        w_out = jax.random.normal(ks[2], (DIM, DIM), dtype=jnp.float32) * DIM ** (-0.5)
        b_out = jnp.zeros((DIM,), dtype=jnp.float32)
        local_bias = jax.random.normal(ks[3], (HEADS, WS, WS), dtype=jnp.float32)
        global_param = jax.random.normal(ks[4], (HEADS, G, WS), dtype=jnp.float32)
        gate = jax.random.normal(ks[5], (HEADS,), dtype=jnp.float32)
        return {'x': x, 'w_qkv': w_qkv, 'w_out': w_out, 'b_out': b_out, 'local_bias': local_bias, 'global_param': global_param, 'gate': gate}
    _L1_attn_all = _L1_attn_setup()
    _L1_attn_in = {k: v for k, v in _L1_attn_all.items() if k in ('w_qkv', 'w_out', 'b_out', 'local_bias', 'global_param', 'gate')}
    del _L1_attn_all

    def _L1_ffn_setup():
        import jax, jax.numpy as jnp
        import numpy as np
        B, T, C = (8, 256, 128)
        H = 256
        G, EG = (2, 4)
        E = G * EG
        K = 2
        LN_EPS = 1e-05

        def _swiglu(x):
            a, b = jnp.split(x, 2, axis=-1)
            return jax.nn.silu(a) * b
        key = jax.random.key(seed)
        ks = jax.random.split(key, 8)
        n = lambda k, shape, s: jax.random.normal(k, shape, dtype=jnp.float32) * s
        return {'x': n(ks[0], (B, T, C), 1.0), 'ln_scale': jnp.ones((C,), jnp.float32), 'ln_bias': jnp.zeros((C,), jnp.float32), 'shared_in_w': n(ks[1], (2 * H, C), 0.02), 'shared_out_w': n(ks[2], (C, H), 0.02), 'shared_out_b': jnp.zeros((C,), jnp.float32), 'expert_in_w': n(ks[3], (2 * H, C), 0.02), 'expert_out_weight': n(ks[4], (E, C, H), 0.02), 'expert_out_bias': jnp.zeros((E, C), jnp.float32), 'group_gate_w': n(ks[5], (G, C), 0.02), 'expert_gate_w': n(ks[6], (E, C), 0.02), 'group_bias': jnp.zeros((G,), jnp.float32), 'expert_bias': jnp.zeros((E,), jnp.float32)}
    _L1_ffn_all = _L1_ffn_setup()
    _L1_ffn_in = {k: v for k, v in _L1_ffn_all.items() if k in ('ln_scale', 'ln_bias', 'shared_in_w', 'shared_out_w', 'shared_out_b', 'expert_in_w', 'expert_out_weight', 'expert_out_bias', 'group_gate_w', 'expert_gate_w', 'group_bias', 'expert_bias')}
    del _L1_ffn_all
    return {'x': x, 'L0_tok_W': _L0_tok_in['W'], 'L0_tok_b': _L0_tok_in['b'], 'L0_attn_Wk': _L0_attn_in['Wk'], 'L0_attn_bk': _L0_attn_in['bk'], 'L0_attn_Wv': _L0_attn_in['Wv'], 'L0_attn_bv': _L0_attn_in['bv'], 'L0_attn_Wr': _L0_attn_in['Wr'], 'L0_attn_br': _L0_attn_in['br'], 'L0_attn_Wo': _L0_attn_in['Wo'], 'L0_attn_bo': _L0_attn_in['bo'], 'L0_attn_Wck': _L0_attn_in['Wck'], 'L0_attn_bck': _L0_attn_in['bck'], 'L0_attn_Wcv': _L0_attn_in['Wcv'], 'L0_attn_bcv': _L0_attn_in['bcv'], 'L0_attn_Wcr': _L0_attn_in['Wcr'], 'L0_attn_bcr': _L0_attn_in['bcr'], 'L0_attn_ln1_g': _L0_attn_in['ln1_g'], 'L0_attn_ln1_b': _L0_attn_in['ln1_b'], 'L0_attn_ln2_g': _L0_attn_in['ln2_g'], 'L0_attn_ln2_b': _L0_attn_in['ln2_b'], 'L0_attn_time_decay': _L0_attn_in['time_decay'], 'L0_attn_time_first': _L0_attn_in['time_first'], 'L0_attn_tmk': _L0_attn_in['tmk'], 'L0_attn_tmv': _L0_attn_in['tmv'], 'L0_attn_tmr': _L0_attn_in['tmr'], 'L0_attn_cmk': _L0_attn_in['cmk'], 'L0_attn_cmr': _L0_attn_in['cmr'], 'L0_ffn_ln1_g': _L0_ffn_in['ln1_g'], 'L0_ffn_ln1_b': _L0_ffn_in['ln1_b'], 'L0_ffn_Wq': _L0_ffn_in['Wq'], 'L0_ffn_bq': _L0_ffn_in['bq'], 'L0_ffn_Wk': _L0_ffn_in['Wk'], 'L0_ffn_bk': _L0_ffn_in['bk'], 'L0_ffn_Wv': _L0_ffn_in['Wv'], 'L0_ffn_bv': _L0_ffn_in['bv'], 'L0_ffn_Wo': _L0_ffn_in['Wo'], 'L0_ffn_bo': _L0_ffn_in['bo'], 'L0_ffn_gate_W': _L0_ffn_in['gate_W'], 'L0_ffn_gate_b': _L0_ffn_in['gate_b'], 'L0_ffn_W1': _L0_ffn_in['W1'], 'L0_ffn_b1': _L0_ffn_in['b1'], 'L0_ffn_W2': _L0_ffn_in['W2'], 'L0_ffn_b2': _L0_ffn_in['b2'], 'L1_attn_w_qkv': _L1_attn_in['w_qkv'], 'L1_attn_w_out': _L1_attn_in['w_out'], 'L1_attn_b_out': _L1_attn_in['b_out'], 'L1_attn_local_bias': _L1_attn_in['local_bias'], 'L1_attn_global_param': _L1_attn_in['global_param'], 'L1_attn_gate': _L1_attn_in['gate'], 'L1_ffn_ln_scale': _L1_ffn_in['ln_scale'], 'L1_ffn_ln_bias': _L1_ffn_in['ln_bias'], 'L1_ffn_shared_in_w': _L1_ffn_in['shared_in_w'], 'L1_ffn_shared_out_w': _L1_ffn_in['shared_out_w'], 'L1_ffn_shared_out_b': _L1_ffn_in['shared_out_b'], 'L1_ffn_expert_in_w': _L1_ffn_in['expert_in_w'], 'L1_ffn_expert_out_weight': _L1_ffn_in['expert_out_weight'], 'L1_ffn_expert_out_bias': _L1_ffn_in['expert_out_bias'], 'L1_ffn_group_gate_w': _L1_ffn_in['group_gate_w'], 'L1_ffn_expert_gate_w': _L1_ffn_in['expert_gate_w'], 'L1_ffn_group_bias': _L1_ffn_in['group_bias'], 'L1_ffn_expert_bias': _L1_ffn_in['expert_bias']}

def reference(x, L0_tok_W, L0_tok_b, L0_attn_Wk, L0_attn_bk, L0_attn_Wv, L0_attn_bv, L0_attn_Wr, L0_attn_br, L0_attn_Wo, L0_attn_bo, L0_attn_Wck, L0_attn_bck, L0_attn_Wcv, L0_attn_bcv, L0_attn_Wcr, L0_attn_bcr, L0_attn_ln1_g, L0_attn_ln1_b, L0_attn_ln2_g, L0_attn_ln2_b, L0_attn_time_decay, L0_attn_time_first, L0_attn_tmk, L0_attn_tmv, L0_attn_tmr, L0_attn_cmk, L0_attn_cmr, L0_ffn_ln1_g, L0_ffn_ln1_b, L0_ffn_Wq, L0_ffn_bq, L0_ffn_Wk, L0_ffn_bk, L0_ffn_Wv, L0_ffn_bv, L0_ffn_Wo, L0_ffn_bo, L0_ffn_gate_W, L0_ffn_gate_b, L0_ffn_W1, L0_ffn_b1, L0_ffn_W2, L0_ffn_b2, L1_attn_w_qkv, L1_attn_w_out, L1_attn_b_out, L1_attn_local_bias, L1_attn_global_param, L1_attn_gate, L1_ffn_ln_scale, L1_ffn_ln_bias, L1_ffn_shared_in_w, L1_ffn_shared_out_w, L1_ffn_shared_out_b, L1_ffn_expert_in_w, L1_ffn_expert_out_weight, L1_ffn_expert_out_bias, L1_ffn_group_gate_w, L1_ffn_expert_gate_w, L1_ffn_group_bias, L1_ffn_expert_bias):
    import jax
    import jax.numpy as jnp

    def _L0_tok_ref(x, W, b):
        import jax, jax.numpy as jnp
        import numpy as np
        D_MODEL = 128
        VOCAB = 50257
        BATCH = 8
        SEQ = 512

        def _positional_encoding(seq_len, d_model, dtype):
            pos = jnp.arange(1, seq_len + 1, dtype=jnp.float32)[:, None]
            i = jnp.arange(d_model)
            exponent = jnp.where(i % 2 == 0, i, i + 1).astype(jnp.float32) / d_model
            angle = pos / 10000.0 ** exponent
            pe = jnp.where(i % 2 == 0, jnp.cos(angle), jnp.sin(angle))
            return pe.astype(dtype)
        emb = jnp.take(W.T, x, axis=0) + b
        pe = _positional_encoding(x.shape[1], W.shape[0], emb.dtype)
        return emb + pe[None, :, :]

    def _L0_attn_ref(x, Wk, bk, Wv, bv, Wr, br, Wo, bo, Wck, bck, Wcv, bcv, Wcr, bcr, ln1_g, ln1_b, ln2_g, ln2_b, time_decay, time_first, tmk, tmv, tmr, cmk, cmr):
        import jax, jax.numpy as jnp
        import numpy as np
        B, T, D = (8, 1024, 128)
        H = 4 * D

        def _xavier(key, fan_in, fan_out):
            lim = float(np.sqrt(6.0 / (fan_in + fan_out)))
            return jax.random.uniform(key, (fan_in, fan_out), jnp.float32, -lim, lim)

        def layer_norm(x, g, b, eps=1e-05):
            m = jnp.mean(x, axis=-1, keepdims=True)
            v = jnp.var(x, axis=-1, keepdims=True)
            return (x - m) * jax.lax.rsqrt(v + eps) * g + b

        def time_shift(x, ratio):
            r = jnp.clip(ratio, 0.0, 1.0)
            xs = jnp.pad(x[:, :-1, :], ((0, 0), (1, 0), (0, 0)))
            return x * r + xs * (1.0 - r)

        def recurrence(w, u, k, v):
            decay = jax.nn.sigmoid(w)
            bonus = jnp.tanh(u)

            def step(state, kv):
                kt, vt = kv
                gate = jax.nn.sigmoid(bonus + kt)
                out = gate * vt + (1.0 - gate) * state
                new_state = decay * state + (1.0 - decay) * vt
                return (new_state, out)
            state0 = jnp.zeros((k.shape[0], k.shape[2]), k.dtype)
            _, outs = jax.lax.scan(step, state0, (k.transpose(1, 0, 2), v.transpose(1, 0, 2)))
            return outs.transpose(1, 0, 2)

        def rwkv_block(x, Wk, bk, Wv, bv, Wr, br, Wo, bo, Wck, bck, Wcv, bcv, Wcr, bcr, ln1_g, ln1_b, ln2_g, ln2_b, time_decay, time_first, tmk, tmv, tmr, cmk, cmr):
            h = layer_norm(x, ln1_g, ln1_b)
            k = time_shift(h, tmk) @ Wk + bk
            v = time_shift(h, tmv) @ Wv + bv
            r = time_shift(h, tmr) @ Wr + br
            rec = recurrence(time_decay, time_first, k, v)
            tm = jnp.tanh(r) * rec @ Wo + bo
            x = x + 0.5 * tm
            h = layer_norm(x, ln2_g, ln2_b)
            ck = time_shift(h, cmk) @ Wck + bck
            cr = time_shift(h, cmr) @ Wcr + bcr
            vv = jax.nn.gelu(ck, approximate=False) @ Wcv + bcv
            x = x + 0.5 * (jnp.tanh(cr) * vv)
            return x
        return rwkv_block(x, Wk, bk, Wv, bv, Wr, br, Wo, bo, Wck, bck, Wcv, bcv, Wcr, bcr, ln1_g, ln1_b, ln2_g, ln2_b, time_decay, time_first, tmk, tmv, tmr, cmk, cmr)

    def _L0_ffn_ref(x, ln1_g, ln1_b, Wq, bq, Wk, bk, Wv, bv, Wo, bo, gate_W, gate_b, W1, b1, W2, b2):
        import jax, jax.numpy as jnp
        import numpy as np
        B, S, D, H, E = (4, 512, 128, 8, 8)
        FF = 4 * D
        HD = D // H
        EPS = 1e-05

        def _layernorm(x, g, b):
            mu = jnp.mean(x, axis=-1, keepdims=True)
            var = jnp.mean((x - mu) ** 2, axis=-1, keepdims=True)
            return (x - mu) * jax.lax.rsqrt(var + EPS) * g + b
        b, s, d = x.shape
        q = (x @ Wq + bq).reshape(b, s, H, HD)
        k = (x @ Wk + bk).reshape(b, s, H, HD)
        v = (x @ Wv + bv).reshape(b, s, H, HD)
        scores = jnp.einsum('bqhd,bkhd->bhqk', q, k) / jnp.sqrt(jnp.float32(HD))
        attn = jax.nn.softmax(scores, axis=-1)
        o = jnp.einsum('bhqk,bkhd->bqhd', attn, v).reshape(b, s, d) @ Wo + bo
        h = _layernorm(x + o, ln1_g, ln1_b)
        t = h.reshape(b * s, d)
        probs = jax.nn.softmax(t @ gate_W + gate_b, axis=-1)
        idx = jnp.argmax(probs, axis=-1)
        gw = jnp.max(probs, axis=-1)
        hid = jax.nn.gelu(jnp.einsum('nd,edf->enf', t, W1) + b1[:, None, :])
        out_all = jnp.einsum('enf,efd->end', hid, W2) + b2[:, None, :]
        onehot = jax.nn.one_hot(idx, E, dtype=t.dtype)
        out = jnp.einsum('ne,end->nd', onehot, out_all)
        out = out * gw[:, None]
        return out.reshape(b, s, d)

    def _L1_attn_ref(x, w_qkv, w_out, b_out, local_bias, global_param, gate):
        import jax, jax.numpy as jnp
        import numpy as np
        DIM = 128
        HEADS = 8
        WS = 64
        G = 32
        SPARSITY = 0.3
        b, n, _ = x.shape
        h, ws, g = (HEADS, WS, G)
        d = DIM // h
        w = n // ws
        scale = DIM ** (-0.5)
        qkv = x @ w_qkv
        q, k, v = jnp.split(qkv, 3, axis=-1)

        def to_win(t):
            return t.reshape(b, n, h, d).transpose(0, 2, 1, 3).reshape(b, h, w, ws, d)
        q, k, v = (to_win(q), to_win(k), to_win(v))
        local = jnp.einsum('bhwnd,bhwmd->bhwnm', q, k) * scale
        local = local + local_bias[None, :, None]
        q_mean = q.mean(axis=2)
        k_mean = k.mean(axis=2)
        global_q = jnp.einsum('hgn,bhnd->bhgd', global_param, q_mean)
        global_scores = jnp.einsum('bhgd,bhmd->bhgm', global_q, k_mean) * scale
        global_bias = global_scores.mean(axis=2)
        gate_h = jax.nn.sigmoid(gate)[None, :, None, None, None]
        scores = local + gate_h * global_bias[:, :, None, None, :]
        k_keep = int(ws * (1.0 - SPARSITY))
        thresh = jax.lax.top_k(scores, k_keep)[0][..., -1:]
        scores = jnp.where(scores >= thresh, scores, jnp.float32(-1000000000.0))
        attn = jax.nn.softmax(scores, axis=-1)
        out = jnp.einsum('bhwnm,bhwmd->bhwnd', attn, v)
        out = out.reshape(b, h, n, d).transpose(0, 2, 1, 3).reshape(b, n, DIM)
        return out @ w_out + b_out

    def _L1_ffn_ref(x, ln_scale, ln_bias, shared_in_w, shared_out_w, shared_out_b, expert_in_w, expert_out_weight, expert_out_bias, group_gate_w, expert_gate_w, group_bias, expert_bias):
        import jax, jax.numpy as jnp
        import numpy as np
        B, T, C = (8, 256, 128)
        H = 256
        G, EG = (2, 4)
        E = G * EG
        K = 2
        LN_EPS = 1e-05

        def _swiglu(x):
            a, b = jnp.split(x, 2, axis=-1)
            return jax.nn.silu(a) * b
        Bx, Tx, Cx = x.shape
        S = Bx * Tx
        flat = x.reshape(S, Cx)
        mu = flat.mean(-1, keepdims=True)
        var = ((flat - mu) ** 2).mean(-1, keepdims=True)
        flat = (flat - mu) * jax.lax.rsqrt(var + LN_EPS) * ln_scale + ln_bias
        h_shared = _swiglu(flat @ shared_in_w.T)
        out_shared = h_shared @ shared_out_w.T + shared_out_b
        g_logits = flat @ group_gate_w.T + group_bias
        g_idx = jnp.argmax(g_logits, axis=-1)
        e_logits = (flat @ expert_gate_w.T).reshape(S, G, EG)
        e_sel = jnp.take_along_axis(e_logits, g_idx[:, None, None], axis=1)[:, 0, :]
        e_sel = e_sel + expert_bias.reshape(G, EG)[g_idx]
        e_probs = jax.nn.softmax(e_sel, axis=-1)
        topv, topi = jax.lax.top_k(e_probs, K)
        topv = topv / (topv.sum(-1, keepdims=True) + 1e-08)
        disp = g_idx[:, None] * EG + topi
        h_expert = _swiglu(flat @ expert_in_w.T)
        rows = jnp.arange(S)[:, None]
        comb = jnp.zeros((S, E), flat.dtype).at[rows, disp].add(topv)
        cnt = jnp.zeros((S, E), flat.dtype).at[rows, disp].add(1.0)
        routed = cnt @ expert_out_bias
        for e in range(E):
            routed = routed + comb[:, e:e + 1] * (h_expert @ expert_out_weight[e].T)
        return (out_shared + routed).reshape(Bx, Tx, Cx)
    h = _L0_tok_ref(x, L0_tok_W, L0_tok_b)
    h = h + _L0_attn_ref(_layernorm(h, axis=-1), L0_attn_Wk, L0_attn_bk, L0_attn_Wv, L0_attn_bv, L0_attn_Wr, L0_attn_br, L0_attn_Wo, L0_attn_bo, L0_attn_Wck, L0_attn_bck, L0_attn_Wcv, L0_attn_bcv, L0_attn_Wcr, L0_attn_bcr, L0_attn_ln1_g, L0_attn_ln1_b, L0_attn_ln2_g, L0_attn_ln2_b, L0_attn_time_decay, L0_attn_time_first, L0_attn_tmk, L0_attn_tmv, L0_attn_tmr, L0_attn_cmk, L0_attn_cmr)
    h = h + _L0_ffn_ref(_layernorm(h, axis=-1), L0_ffn_ln1_g, L0_ffn_ln1_b, L0_ffn_Wq, L0_ffn_bq, L0_ffn_Wk, L0_ffn_bk, L0_ffn_Wv, L0_ffn_bv, L0_ffn_Wo, L0_ffn_bo, L0_ffn_gate_W, L0_ffn_gate_b, L0_ffn_W1, L0_ffn_b1, L0_ffn_W2, L0_ffn_b2)
    h = h + _L1_attn_ref(_layernorm(h, axis=-1), L1_attn_w_qkv, L1_attn_w_out, L1_attn_b_out, L1_attn_local_bias, L1_attn_global_param, L1_attn_gate)
    h = h + _L1_ffn_ref(_layernorm(h, axis=-1), L1_ffn_ln_scale, L1_ffn_ln_bias, L1_ffn_shared_in_w, L1_ffn_shared_out_w, L1_ffn_shared_out_b, L1_ffn_expert_in_w, L1_ffn_expert_out_weight, L1_ffn_expert_out_bias, L1_ffn_group_gate_w, L1_ffn_expert_gate_w, L1_ffn_group_bias, L1_ffn_expert_bias)
    return h

_drawn_inputs = setup_inputs


def setup_inputs(seed=0):
    import zlib

    import numpy as np

    out = dict(_drawn_inputs(seed))
    spreads = {'L0_attn_bk': (0.0, 0.8),
     'L0_attn_bv': (0.0, 0.35),
     'L0_attn_br': (0.0, 0.325),
     'L0_attn_bo': (0.0, 0.1),
     'L0_attn_bck': (0.0, 0.449),
     'L0_attn_bcv': (0.0, 0.358),
     'L0_attn_bcr': (0.0, 0.522),
     'L0_attn_ln1_g': (1.0, 0.2),
     'L0_attn_ln1_b': (0.0, 0.1),
     'L0_attn_ln2_g': (1.0, 0.546),
     'L0_attn_ln2_b': (0.0, 0.403),
     'L0_attn_time_first': (0.5, 0.6),
     'L0_attn_tmk': (0.5, 0.6),
     'L0_attn_tmv': (0.5, 0.6),
     'L0_attn_tmr': (0.5, 0.6),
     'L0_attn_cmk': (0.5, 0.6),
     'L0_attn_cmr': (0.5, 0.6),
     'L0_ffn_ln1_g': (1.0, 0.6),
     'L0_ffn_ln1_b': (0.0, 0.8),
     'L0_ffn_bq': (0.0, 0.8),
     'L0_ffn_bk': (0.0, 2.0),
     'L0_ffn_bv': (0.0, 0.8),
     'L0_ffn_bo': (0.0, 0.8),
     'L0_ffn_gate_b': (0.0, 0.643),
     'L0_ffn_b1': (0.0, 0.8),
     'L0_ffn_b2': (0.0, 0.569),
     'L1_attn_b_out': (0.0, 0.1),
     'L1_ffn_ln_scale': (1.0, 0.2),
     'L1_ffn_ln_bias': (0.0, 0.1),
     'L1_ffn_shared_out_b': (0.0, 0.594),
     'L1_ffn_expert_out_bias': (0.0, 0.445),
     'L1_ffn_group_bias': (0.0, 0.1),
     'L1_ffn_expert_bias': (0.0, 0.1)}
    factors = {'L0_attn_Wk': 3.92,
     'L0_attn_time_decay': 8.0,
     'L0_ffn_Wq': 8.0,
     'L0_ffn_Wk': 8.0,
     'L0_ffn_Wv': 8.0,
     'L0_ffn_Wo': 8.0,
     'L0_ffn_gate_W': 4.047,
     'L0_ffn_W1': 6.489,
     'L0_ffn_W2': 6.064,
     'L1_attn_global_param': 8.0,
     'L1_attn_gate': 55.95,
     'L1_ffn_shared_in_w': 8.0,
     'L1_ffn_shared_out_w': 8.0,
     'L1_ffn_expert_in_w': 8.0,
     'L1_ffn_expert_out_weight': 8.0}
    for name, (base, spread) in spreads.items():
        noise = np.random.default_rng([zlib.crc32(name.encode()), seed]).standard_normal(out[name].shape)
        drawn = base * np.exp(spread * noise) if base else spread * noise
        out[name] = jnp.asarray(drawn.astype(out[name].dtype))
    for name, factor in factors.items():
        out[name] = (out[name] * factor).astype(out[name].dtype)
    return out
```

```python
import concourse.bass as bass
from concourse import mybir
from contextlib import ExitStack

T = 2048
D = 128
P = 128
TILES = T // P
CT = 512
CHUNKS = T // CT
TPC = CT // P
HEADS = 8
HD = D // HEADS
PAIRS = HEADS // 2
UNITS = CHUNKS * PAIRS
AHEAD = 4
PSLOTS = 6
FF = 4 * D
FC = FF // P
E0 = 8
WS = 64
G1 = 32
KEEP = int(WS * (1.0 - 0.3))
DROP = WS - KEEP
H1 = 256
E1 = 8
EG = 4
EPS = 1e-5
NEG = -3.0e38

VECS = ["bk", "bv", "br", "bcv", "bcr", "g1", "b1", "g2", "b2", "decay", "first", "mk", "mv", "mr", "ck", "cr",
        "bq", "bkf", "gf", "bf", "ls", "lb"]
VI = {n: i for i, n in enumerate(VECS)}
NV = len(VECS)
ROWS = [("tokb", D), ("bo", D), ("bvf", D), ("bof", D), ("gateb", E0), ("bout", D), ("shb", D), ("gb", 2),
        ("eb", E1), ("prio", E0)]
RO = {}
NR = 0
for _n, _w in ROWS:
    RO[_n] = (NR, NR + _w)
    NR += _w


def build_tower(nc, A, out):
    f32, f32r, i32 = mybir.dt.float32, mybir.dt.float32r, mybir.dt.int32
    ALU, ACT, AX = mybir.AluOpType, mybir.ActivationFunctionType, mybir.AxisListType
    ctx = ExitStack()
    with ctx:
        def sb(name, shape, dt=f32):
            return ctx.enter_context(nc.sbuf_tensor("s_" + name, shape, dt))

        def sem(name):
            return ctx.enter_context(nc.semaphore(name))

        H = sb("resid", [P, TILES, D])
        X = sb("normed", [P, TILES, D])
        SW = T + 8
        S = [sb(f"scratch{i}", [P, SW]) for i in range(7)]
        V = sb("vals", [P, 4096])
        PB = sb("probs", [P, 4096])
        QHI, QLO = sb("qhi", [P, T], f32r), sb("qlo", [P, T], f32r)
        KHI, KLO = sb("khi", [P, 2, CT], f32r), sb("klo", [P, 2, CT], f32r)
        KST = sb("kstack", [P, PAIRS, T], f32r)
        SELR = sb("selr", [P, 4 * PAIRS, P], f32r)
        IDR = sb("identr", [P, P], f32r)
        QM = [KHI, sb("qmax", [P, 2, CT], f32r)]
        QE = [KLO, SELR[:, 8:16, :].rearrange("p (h a) b -> p h (a b)", h=2)]
        AM = sb("amax", [P, TPC, P], f32r)
        ID = sb("ident", [P, P])
        SELO = sb("selo", [P, 2 * (HD + 1)])
        DEC = sb("dec", [P, CT])
        vec = sb("vec", [P, NV])
        drv = sb("drv", [P, 16])
        kone = sb("kone", [P, 1])
        row = sb("rows", [P, NR])
        idx = sb("idx", [P, TILES], i32)
        wrk = sb("w_rwkv", [P, 5 * D + FF])
        wr, wck = wrk[:, 0:5 * D], wrk[:, 5 * D:5 * D + FF]
        wcv = sb("w_cv", [P, FC, D])
        wf = sb("w_ffn", [P, 3 * D + E0])
        wof = sb("w_of", [P, D])
        wl = sb("w_l1", [P, 4 * D + 2 * D])
        win = sb("w_in", [P, 2, FF])
        wso = sb("w_so", [P, 2, D])
        wg1 = sb("w_g1", [P, 2 + E1])
        eob = sb("w_eob", [E1, D])
        b1c = sb("b1c", [P, E0 * FC])
        b2r = sb("b2r", [E0, D])
        bckc = sb("bckc", [P, FC])
        nh = sb("neghalf", [P, 8])
        st6 = sb("st6", [P, TILES, 6])
        MV = [sb(f"mv{i}", [P, TILES, 2]) for i in range(6)]
        RA = [sb(f"ra{i}", [P, TILES]) for i in range(6)]
        RB = sb("rb", [P, TILES])
        VE = sb("ve", [P, TILES])
        mq = sb("mq", [P, 8, 4])
        nm = sb("nm", [P, 8])
        cw = sb("cw", [P, TILES, E0])
        gt = [sb(f"gt{i}", [P, TILES, E0]) for i in range(4)]
        gs = sb("gs", [P, 4, TILES])
        cT = S[4][0:E0, 0:T]
        gpm = sb("gpm", [P, 2, WS])
        xm = sb("xm", [P, WS])
        wcvf = wcv[:, :, :].rearrange("p f d -> p (f d)")
        qm = wcvf[:, 0:2 * WS].rearrange("p (g n) -> p g n", g=2)
        km = wcvf[:, 2 * WS:4 * WS].rearrange("p (g n) -> p g n", g=2)
        gq = sb("gq", [P, 8])
        gqb = wcvf[:, 4 * WS:4 * WS + 2 * P].rearrange("p (g n) -> p g n", g=2)
        gat = sb("gat", [P, 2])
        BT = DEC[:, :].rearrange("p (h m) -> p h m", m=WS)
        t8 = wrk[:, 0:768].rearrange("p (k r e) -> p k r e", k=3, e=8)
        mn = sb("mn", [P, 32])
        oden = sb("oden", [P, 2, 16])
        gpick = sb("gpick", [P, TILES, 2])

        def sco(i):
            return S[i][:, 0:T].rearrange("p (r m) -> p r m", m=WS)

        def tokv(i):
            return S[i][:, 0:T].rearrange("p (t d) -> p t d", d=D)

        PS = ctx.enter_context(nc.psum_tensor("banks", [P, 8, CT], f32))
        B = [PS[:, i, :] for i in range(8)]

        names = """w_rows w_idx w_pe w_vec w_rwkv w_ck w_ffn w_sel w_misc w_l1
            w_d w_moe w_gp w_lb w_gat h_ready xh_ready t1_done hT_ready mix_ready
            k_done v_done r_done gate_ready vv_ready wv_ready tr_ready z_ready woo_done x1_ready
            x0b_ready xh2_ready t2_done h2T_ready mix2_ready cr_done ck_done gelu_ready tc_ready vv2_done
            q_ready t3_done h1_ready xh3_ready t4_done x1T_ready q_done kk_done vt_done qhi_ready
            khi_ready qlo_ready klo_ready vals_ready ksel_done kst_ready xb_ready qsel_done qm_ready mxp_done
            mxr_done nm_ready qe_done qe_ready st_done p_ready av_done xev_ready dsum_done on_ready
            wo_done y_ready xh4_ready t5_done tT_ready gl_done cw_ready cT_done cT_ready acc0_done
            acc0_ready w1_done hid_ready w2_done acc_ready h2_ready xh5_ready t6_done x2T_ready xm_ready
            gm_done gq_ready gb_done bt_ready qk_done qk_ready v1_done v1_ready s_done ns_ready
            mn_ready e_in e_ready p1_ready pt_done pt_ready ov_done o_ready t7_done oT_ready
            pr_done h3_ready h3b_ready xh6_ready t8_done fT_ready in_done sil_ready hsw_ready sh_done
            ex_done g2_done cb_ready cn_done cn_ready fin_ready dve_step act_step pool_step st_out
            ot_done ot_ready zero_ready gate_sig drv_ready drv_act selr_ready c2_ready gs_ready wex_in""".split()
        s = {n: sem(n) for n in names}
        emb_in = [sem(f"emb_in{c}") for c in range(CHUNKS)]
        ln_stats = [sem(f"ln_stats{i}") for i in range(6)]
        ln_rstd = [sem(f"ln_rstd{i}") for i in range(6)]
        block = ctx.enter_context(nc.Block())

        def vc(n):
            return vec[:, VI[n]:VI[n] + 1]

        def rowv(n):
            a, b = RO[n]
            return row[:, a:b]

        def rows_over(n, k):
            a, b = RO[n]
            return row[:, a:b].unsqueeze(1).to_broadcast([P, k, b - a])

        def ch(c):
            return slice(c * CT, (c + 1) * CT)

        def tl(c):
            return slice(c * TPC, (c + 1) * TPC)

        def bt4(b):
            return B[b].rearrange("p (t d) -> p t d", d=D)

        hT, hTn = S[1], S[1][:, 1:T + 1]

        @block.sync
        def _(sp):
            sp.dma_start(idx[:, :], A["idx"]).then_inc(s["w_idx"], 16)
            sp.dma_start(row[:, :], A["rows"].to_broadcast([P, NR])).then_inc(s["w_rows"], 16)
            sp.dma_start(S[6][:, 0:T], A["pe"]).then_inc(s["w_pe"], 16)
            sp.dma_start(vec[:, :], A["vec"]).then_inc(s["w_vec"], 16)
            sp.dma_start(ID[:, :], A["ident"]).then_inc(s["w_misc"], 16)
            sp.dma_start(SELO[:, :], A["selo"]).then_inc(s["w_misc"], 16)
            sp.dma_start(bckc[:, :], A["bckc"]).then_inc(s["w_misc"], 16)
            sp.dma_start(kone[:, :], A["kone"]).then_inc(s["w_misc"], 16)
            sp.dma_start(wr, A["w_rwkv"]).then_inc(s["w_rwkv"], 16)
            sp.dma_start(PB[:, 0:T], A["sel"]).then_inc(s["w_sel"], 16)
            sp.dma_start(wck, A["w_ck"]).then_inc(s["w_ck"], 16)
            sp.dma_start(wcv[:, :, :], A["w_cv"]).then_inc(s["w_ck"], 16)
            sp.dma_start(wf[:, :], A["w_ffn"]).then_inc(s["w_ffn"], 16)
            sp.dma_start(wof[:, :], A["w_of"]).then_inc(s["w_ffn"], 16)
            sp.dma_start(wl[:, :], A["w_l1"]).then_inc(s["w_l1"], 16)
            sp.dma_start(win[:, :, :], A["w_in"]).then_inc(s["w_d"], 16)
            sp.dma_start(wso[:, :, :], A["w_so"]).then_inc(s["w_d"], 16)
            sp.dma_start(wg1[:, :], A["w_g1"]).then_inc(s["w_d"], 16)
            sp.dma_start(eob[:, :], A["eob"]).then_inc(s["w_d"], 16)
            sp.dma_start(b1c[:, :], A["b1c"]).then_inc(s["w_d"], 16)
            sp.dma_start(b2r[:, :], A["b2r"]).then_inc(s["w_d"], 16)
            sp.dma_start(gat[:, :], A["gat"]).then_inc(s["w_gat"], 16)
            sp.wait_ge(s["z_ready"], CHUNKS)
            for half in range(2):
                sp.dma_start(BT[half * WS:(half + 1) * WS, :, :], A["lb"]).then_inc(s["w_lb"], 16)
            sp.wait_ge(s["ksel_done"], PAIRS * CHUNKS)
            sp.wait_ge(s["vals_ready"], CHUNKS)
            sp.dma_start(S[0][:, 0:T], A["moe_w1"][:, 0:T]).then_inc(s["w_moe"], 16)
            sp.dma_start(S[1][:, 0:T], A["moe_w1"][:, T:2 * T]).then_inc(s["w_moe"], 16)
            sp.dma_start(S[2][:, 0:T], A["moe_w2"][:, 0:T]).then_inc(s["w_moe"], 16)
            sp.dma_start(S[3][:, 0:T], A["moe_w2"][:, T:2 * T]).then_inc(s["w_moe"], 16)
            sp.wait_ge(s["h2_ready"], CHUNKS)
            for g in range(2):
                sp.dma_start(S[2 + g][:, 0:T], A["gp"][g, :, :]).then_inc(s["w_gp"], 16)
            sp.wait_ge(s["ov_done"], CHUNKS)
            sp.dma_start(V[:, 0:2 * E1 * D], A["w_ex"]).then_inc(s["wex_in"], 16)
            for c in range(CHUNKS):
                sp.wait_ge(s["fin_ready"], c + 1)
                sp.dma_start(out[:, tl(c), :], H[:, tl(c), :]).then_inc(s["st_out"], 16)
            sp.wait_ge(s["st_out"], 16 * CHUNKS)

        @block.gpsimd
        def _(pool):
            n = [0]

            def step(ins):
                n[0] += 1
                ins.then_inc(s["pool_step"], 1)
                pool.wait_ge(s["pool_step"], n[0])

            pool.wait_ge(s["w_idx"], 16)
            for t in range(TILES):
                pool.indirect_dma_start(H[:, t, :], None, A["emb"],
                                        bass.IndirectOffsetOnAxis(ap=idx[:, t:t + 1], axis=0)).then_inc(emb_in[t // TPC], 16)
            step(pool.memset(nh[:, :], -0.5))
            pool.wait_ge(s["w_rows"], 16)
            pool.wait_ge(s["w_pe"], 16)
            step(pool.tensor_tensor(tokv(6), tokv(6), rows_over("tokb", TILES), ALU.add))
            for c in range(CHUNKS):
                pool.wait_ge(emb_in[c], 16 * TPC)
                pool.tensor_tensor(H[:, tl(c), :], H[:, tl(c), :], tokv(6)[:, tl(c), :], ALU.add).then_inc(s["h_ready"], 1)

            def rstd(k, c, double=False):
                pool.wait_ge(ln_stats[k], c + 1)
                ve, ra, var = VE[:, tl(c)], RA[k][:, tl(c)], MV[k][:, tl(c), 1]
                step(pool.tensor_scalar(ve, var, EPS, None, ALU.add))
                if not double:
                    pool.tensor_tensor(ra, ve, nh[:, 0:TPC], ALU.pow).then_inc(ln_rstd[k], 1)
                    return
                step(pool.tensor_tensor(ra, ve, nh[:, 0:TPC], ALU.pow))
                step(pool.tensor_tensor(ve, ra, ra, ALU.mult))
                step(pool.tensor_tensor(ve, ve, var, ALU.mult))
                step(pool.tensor_scalar(ve, ve, EPS, None, ALU.add))
                if k == 0:
                    pool.tensor_tensor(RB[:, tl(c)], ve, nh[:, 0:TPC], ALU.pow).then_inc(ln_rstd[k], 1)
                    return
                step(pool.tensor_tensor(RB[:, tl(c)], ve, nh[:, 0:TPC], ALU.pow))
                pool.tensor_tensor(RB[:, tl(c)], RB[:, tl(c)], ra, ALU.mult).then_inc(ln_rstd[k], 1)

            for c in range(CHUNKS):
                rstd(0, c, True)
            step(pool.tensor_scalar(rowv("bo"), rowv("bo"), 0.5, None, ALU.mult))
            for c in range(CHUNKS):
                pool.wait_ge(s["xh_ready"], c + 1)
                pool.tensor_tensor(X[:, tl(c), :], X[:, tl(c), :], rows_over("bo", TPC), ALU.add).then_inc(s["x0b_ready"], 1)
            for c in range(CHUNKS):
                rstd(1, c)
            for c in range(CHUNKS):
                rstd(2, c)
            for c in range(CHUNKS):
                pool.wait_ge(s["xh3_ready"], c + 1)
                pool.wait_ge(s["t4_done"], c + 1)
                pool.tensor_tensor(X[:, tl(c), :], X[:, tl(c), :], rows_over("bof", TPC), ALU.add).then_inc(s["xb_ready"], 1)
            for k in (3, 4):
                for c in range(CHUNKS):
                    rstd(k, c)
            for c in range(CHUNKS):
                pool.wait_ge(s["xh5_ready"], c + 1)
                pool.tensor_tensor(H[:, tl(c), :], H[:, tl(c), :], rows_over("bout", TPC), ALU.add).then_inc(s["h3b_ready"], 1)
            for c in range(CHUNKS):
                pool.wait_ge(s["mn_ready"], c + 1)
                if c >= 2:
                    pool.wait_ge(s["t7_done"], c - 1)
                pool.tensor_tensor(sco(4 + 2 * (c % 2)), sco(2 + c % 2),
                                   mn[:, :].unsqueeze(2).to_broadcast([P, 32, WS]), ALU.subtract).then_inc(s["e_in"], 1)
            for c in range(CHUNKS):
                rstd(5, c, True)

        G = PB[:, :].rearrange("p (k f t) -> p k f t", k=2, f=FC)

        def prob(m):
            k = m % PSLOTS
            home = PB[:, k * 2 * CT:(k + 1) * 2 * CT] if k < 4 else S[k + 1][:, 2 * CT:4 * CT]
            return home.rearrange("p (h q) -> p h q", h=2)

        def val(c):
            return V[:, :].rearrange("p (t h d) -> p t h d", h=HEADS, d=32)[:, tl(c), :, :]

        def valh(k, h):
            return V[:, (k * HEADS + h) * 32:(k * HEADS + h + 1) * 32]

        def vwin(c, k):
            return V[:, :].rearrange("p (c k t h d) -> p c k t h d", c=2, k=2, h=HEADS, d=32)[:, c % 2, k, :, :, :]

        def sco2(i):
            return S[i][:, 0:T]

        @block.scalar
        def _(act):
            n = [0]

            def step(ins):
                n[0] += 1
                ins.then_inc(s["act_step"], 1)
                act.wait_ge(s["act_step"], n[0])

            act.wait_ge(s["w_vec"], 16)
            act.wait_ge(s["w_gat"], 16)
            act.activation(drv[:, 0:1], vc("decay"), ACT.Sigmoid).then_inc(s["act_step"], 1)
            act.activation(gat[:, :], gat[:, :], ACT.Sigmoid).then_inc(s["gate_sig"], 1)
            act.activation(drv[:, 1:2], vc("first"), ACT.Tanh).then_inc(s["drv_act"], 1)
            n[0] = 1
            act.wait_ge(s["drv_ready"], 1)
            for c in range(CHUNKS):
                act.wait_ge(s["t1_done"], c + 1)
                act.activation(hT[:, 1 + c * CT:1 + (c + 1) * CT], B[c], ACT.Identity, bias=vc("b1"),
                               scale=vc("g1")).then_inc(s["hT_ready"], 1)
            for c in range(CHUNKS):
                act.wait_ge(s["k_done"], c + 1)
                act.activation(S[5][:, ch(c)], B[4 + c % 2], ACT.Sigmoid, bias=drv[:, 2:3]).then_inc(s["gate_ready"], 1)
                act.wait_ge(s["v_done"], c + 1)
                act.activation(S[3][:, ch(c)], B[6 + c % 2], ACT.Identity, bias=vc("bv")).then_inc(s["vv_ready"], 1)
                act.activation(S[2][:, ch(c)], B[6 + c % 2], ACT.Identity, bias=drv[:, 4:5],
                               scale=drv[:, 3:4]).then_inc(s["wv_ready"], 1)
                act.wait_ge(s["r_done"], c + 1)
                act.activation(S[4][:, ch(c)], B[c], ACT.Tanh, bias=vc("br")).then_inc(s["tr_ready"], 1)
            for c in range(CHUNKS):
                act.wait_ge(s["t2_done"], c + 1)
                act.activation(hT[:, 1 + c * CT:1 + (c + 1) * CT], B[4 + c], ACT.Identity, bias=vc("b2"),
                               scale=vc("g2")).then_inc(s["h2T_ready"], 1)
            for c in range(CHUNKS):
                for f in range(FC):
                    act.wait_ge(s["ck_done"], FC * c + f + 1)
                    if c >= 2:
                        act.wait_ge(s["vv2_done"], c - 1)
                    act.activation(G[:, c % 2, f, :], B[4 + f], ACT.Gelu, bias=bckc[:, f:f + 1]).then_inc(s["gelu_ready"], 1)
                act.wait_ge(s["cr_done"], c + 1)
                act.activation(S[2][:, ch(c)], B[c], ACT.Tanh, bias=vc("bcr")).then_inc(s["tc_ready"], 1)
            for c in range(CHUNKS):
                act.wait_ge(s["t4_done"], c + 1)
                act.activation(S[0][:, ch(c)], B[c], ACT.Copy).then_inc(s["x1T_ready"], 1)
            for c in range(CHUNKS):
                act.wait_ge(s["q_done"], c + 1)
                act.activation(QHI[:, ch(c)], B[4], ACT.Identity, bias=vc("bq")).then_inc(s["qhi_ready"], 1)
                act.wait_ge(s["kk_done"], c + 1)
                if c >= 2:
                    act.wait_ge(s["ksel_done"], PAIRS * (c - 1))
                act.activation(KHI[:, c % 2, :], B[5], ACT.Identity, bias=vc("bkf")).then_inc(s["khi_ready"], 1)
                for j in range(PAIRS):
                    act.wait_ge(s["ksel_done"], PAIRS * c + j + 1)
                    act.activation(KST[:, j, ch(c)], B[6 + j % 2], ACT.Identity, bias=kone[:, 0:1]).then_inc(s["kst_ready"], 1)

            def filled(dst, done):
                act.activation(dst[0:64, 0, :], B[7][0:64, :], ACT.Copy)
                act.activation(dst[64:128, 1, :], B[7][64:128, :], ACT.Copy).then_inc(done, 1)

            def weighed(u):
                act.wait_ge(s["av_done"], 8 * (u + 1))
                if u >= 1:
                    act.wait_ge(s["dsum_done"], u)
                act.activation(S[5][:, 0:CT], B[6], ACT.Copy).then_inc(s["xev_ready"], 1)

            def attended(q):
                act.wait_ge(s["ot_done"], q + 1)
                act.activation(S[5][:, CT:2 * CT], B[7], ACT.Copy).then_inc(s["ot_ready"], 1)

            act.wait_ge(s["qsel_done"], 1)
            filled(QM[0], s["qm_ready"])
            act.wait_ge(s["qe_done"], 1)
            filled(QE[0], s["qe_ready"])
            act.wait_ge(s["qsel_done"], 2)
            filled(QM[1], s["qm_ready"])
            for u in range(UNITS):
                for k in range(TILES):
                    m = u * TILES + k
                    if m >= PSLOTS:
                        act.wait_ge(s["av_done"], (m - PSLOTS) // 2 + 1)
                    for h in range(2):
                        act.wait_ge(s["st_done"], 2 * m + h + 1)
                        act.activation(prob(m)[:, h, :], B[3 + (2 * m + h) % 3], ACT.Exp, scale=HD ** -0.5).then_inc(s["p_ready"], 1)
                    if k == 1 and u >= 1:
                        weighed(u - 1)
                    if k == 5 and u >= 1 and u % PAIRS == 0:
                        attended(u // PAIRS - 1)
                    if k == 9 and u + 2 < UNITS:
                        act.wait_ge(s["qsel_done"], u + 3)
                        filled(QM[u % 2], s["qm_ready"])
                    if k == 13 and u + 1 < UNITS:
                        act.wait_ge(s["qe_done"], u + 2)
                        filled(QE[(u + 1) % 2], s["qe_ready"])
            weighed(UNITS - 1)
            attended(CHUNKS - 1)

            for c in range(CHUNKS):
                act.wait_ge(s["t5_done"], c + 1)
                act.activation(S[5][:, ch(c)], B[c], ACT.Identity, bias=vc("bf"), scale=vc("gf")).then_inc(s["tT_ready"], 1)
            act.wait_ge(s["gs_ready"], 1)
            act.activation(gt[1][:, :, :], gt[0][:, :, :], ACT.Exp).then_inc(s["gs_ready"], 1)
            act.wait_ge(s["cT_done"], 1)
            for k in range(4):
                ins = act.activation(cT[:, ch(k)], B[k][0:E0, :], ACT.Copy)
            ins.then_inc(s["cT_ready"], 1)
            for m in range(CHUNKS * E0):
                e = m % E0
                for f in range(FC):
                    act.wait_ge(s["w1_done"], FC * m + f + 1)
                    if m >= 2:
                        act.wait_ge(s["w2_done"], m - 1)
                    act.activation(G[:, m % 2, f, :], B[f], ACT.Gelu_apprx_tanh,
                                   bias=b1c[:, e * FC + f:e * FC + f + 1]).then_inc(s["hid_ready"], 1)

            for c in range(CHUNKS):
                act.wait_ge(s["t6_done"], c + 1)
                act.activation(S[5][:, ch(c)], B[c], ACT.Copy).then_inc(s["x2T_ready"], 1)

            def qkv_out(c):
                for k in range(4):
                    act.wait_ge(s["qk_done"], 4 * c + k + 1)
                    act.activation(S[c % 2][:, k * CT:(k + 1) * CT], B[4 + k % 2], ACT.Copy).then_inc(s["qk_ready"], 1)
                for k in range(2):
                    act.wait_ge(s["v1_done"], 2 * c + k + 1)
                    act.activation(vwin(c, k)[:, :, :, 0:HD], B[4 + k].rearrange("p (t h d) -> p t h d", t=TPC, d=HD),
                                   ACT.Copy).then_inc(s["v1_ready"], 1)

            def exp_out(c):
                act.wait_ge(s["e_in"], c + 1)
                act.activation(sco(4 + 2 * (c % 2)), sco(4 + 2 * (c % 2)), ACT.Exp, scale=-1.0).then_inc(s["e_ready"], 1)

            qkv_out(0)
            qkv_out(1)
            exp_out(0)
            for c in range(CHUNKS):
                for k in range(4):
                    act.wait_ge(s["pt_done"], 4 * c + k + 1)
                    act.activation(PB[:, (c % 2) * T + k * CT:(c % 2) * T + (k + 1) * CT], B[4 + k % 2],
                                   ACT.Copy).then_inc(s["pt_ready"], 1)
                if c + 2 < CHUNKS:
                    qkv_out(c + 2)
                if c + 1 < CHUNKS:
                    exp_out(c + 1)
                act.wait_ge(s["t7_done"], c + 1)
                act.activation(S[5][:, ch(c)], B[4], ACT.Copy).then_inc(s["oT_ready"], 1)

            for c in range(CHUNKS):
                act.wait_ge(s["t8_done"], c + 1)
                act.activation(S[5][:, ch(c)], B[c], ACT.Identity, bias=vc("lb"), scale=vc("ls")).then_inc(s["fT_ready"], 1)
            act.wait_ge(s["gs_ready"], 3)
            act.activation(gt[1][:, :, 0:EG], gt[0][:, :, 0:EG], ACT.Exp).then_inc(s["gs_ready"], 1)
            act.wait_ge(s["cn_done"], 1)
            for k in range(4):
                ins = act.activation(cT[:, ch(k)], B[k][0:E1, :], ACT.Copy)
            ins.then_inc(s["cn_ready"], 1)
            for c in range(CHUNKS):
                for k in range(4):
                    act.wait_ge(s["in_done"], 4 * c + k + 1)
                    if c >= 2:
                        act.wait_ge(s["ex_done"], TPC * (c - 1))
                    act.activation(S[c % 2][:, k * CT:(k + 1) * CT], B[2 * (k % 2)], ACT.Silu).then_inc(s["sil_ready"], 1)

        @block.vector
        def _(dve):
            n = [0]

            def did(ins):
                n[0] += 1
                ins.then_inc(s["dve_step"], 1)
                return n[0]

            def settle(back=0):
                dve.wait_ge(s["dve_step"], n[0] - back)

            def step(ins):
                did(ins)
                settle()

            step(dve.memset(V[:, :], 1.0))
            step(dve.memset(S[1][:, 0:1], 0.0))
            step(dve.memset(S[6][:, T:T + 1], 0.0))
            step(dve.memset(DEC[:, :], 0.0))
            step(dve.memset(AM[:, :, :].bitcast(f32), 0.0))
            dve.wait_ge(s["w_vec"], 16)
            a, b = VI["mk"], VI["cr"] + 1
            step(dve.tensor_scalar(vec[:, a:b], vec[:, a:b], 0.0, 1.0, ALU.max, ALU.min))
            dve.wait_ge(s["drv_act"], 1)
            step(dve.tensor_scalar(drv[:, 2:3], vc("bk"), drv[:, 1:2], None, ALU.add))
            step(dve.tensor_scalar(drv[:, 3:4], drv[:, 0:1], -1.0, 1.0, ALU.mult, ALU.add))
            step(dve.tensor_scalar(DEC[:, :], DEC[:, :], drv[:, 0:1], None, ALU.add))
            dve.tensor_scalar(drv[:, 4:5], vc("bv"), drv[:, 3:4], None, ALU.mult).then_inc(s["drv_ready"], 1)

            def stats(k, c, src):
                for t in range(c * TPC, (c + 1) * TPC):
                    did(dve.bn_stats(st6[:, t, :], src[:, t, :]))
                settle()
                for t in range(c * TPC, (c + 1) * TPC):
                    ins = dve.bn_aggr(MV[k][:, t, :], st6[:, t, :])
                ins.then_inc(ln_stats[k], 1)

            def normed(k, c, dst, src, r, sem_=None):
                for t in range(c * TPC, (c + 1) * TPC):
                    ins = dve.tensor_scalar(dst[:, t, :], src[:, t, :], MV[k][:, t, 0:1], r[:, t:t + 1],
                                            ALU.subtract, ALU.mult)
                    if sem_ and t == (c + 1) * TPC - 1:
                        ins.then_inc(sem_, 1)
                    else:
                        did(ins)

            for c in range(CHUNKS):
                dve.wait_ge(s["h_ready"], c + 1)
                stats(0, c, H)
            dve.wait_ge(s["w_sel"], 16)
            step(dve.tensor_copy(SELR[:, 0:8, :], PB[:, 0:1024].rearrange("p (a b) -> p a b", b=P)))
            dve.wait_ge(s["w_misc"], 64)
            dve.wait_ge(s["w_sel"], 16)
            step(dve.tensor_copy(SELR[:, 8:16, :], PB[:, 1024:2048].rearrange("p (a b) -> p a b", b=P)))
            dve.tensor_copy(IDR[:, :], ID[:, :]).then_inc(s["selr_ready"], 1)
            for c in range(CHUNKS):
                dve.wait_ge(ln_rstd[0], c + 1)
                normed(0, c, X, H, RA[0])
                settle()
                dve.tensor_tensor(tokv(0)[:, tl(c), :], X[:, tl(c), :], RB[:, tl(c)].unsqueeze(2).to_broadcast([P, TPC, D]),
                                  ALU.mult).then_inc(s["xh_ready"], 1)
            for c in range(CHUNKS):
                dve.wait_ge(s["hT_ready"], c + 1)
                now, before = hT[:, 1 + c * CT:1 + (c + 1) * CT], hT[:, ch(c)]
                step(dve.tensor_tensor(S[0][:, ch(c)], now, before, ALU.subtract))
                for i, m in ((2, "mk"), (3, "mv"), (4, "mr")):
                    ins = dve.scalar_tensor_tensor(S[i][:, ch(c)], S[0][:, ch(c)], vc(m), before, ALU.mult, ALU.add)
                    if i < 4:
                        did(ins)
                ins.then_inc(s["mix_ready"], 1)
            dve.wait_ge(s["h_ready"], CHUNKS)
            step(dve.memset(S[6][:, 0:1], 0.0))
            for c in range(CHUNKS):
                dve.wait_ge(s["wv_ready"], c + 1)
                step(dve.tensor_tensor_scan(S[6][:, 1 + c * CT:1 + (c + 1) * CT], DEC[:, :], S[2][:, ch(c)],
                                            S[6][:, c * CT:c * CT + 1], ALU.mult, ALU.add))
                v = S[3][:, ch(c)]
                step(dve.tensor_tensor(v, v, S[6][:, ch(c)], ALU.subtract))
                step(dve.tensor_tensor(v, v, S[5][:, ch(c)], ALU.mult))
                step(dve.tensor_tensor(v, v, S[6][:, ch(c)], ALU.add))
                dve.wait_ge(s["tr_ready"], c + 1)
                dve.tensor_tensor(S[0][:, ch(c)], v, S[4][:, ch(c)], ALU.mult).then_inc(s["z_ready"], 1)
            for c in range(CHUNKS):
                dve.wait_ge(s["woo_done"], c + 1)
                dve.wait_ge(s["x0b_ready"], c + 1)
                dve.scalar_tensor_tensor(X[:, tl(c), :], bt4(c), 0.5, X[:, tl(c), :], ALU.mult, ALU.add).then_inc(s["x1_ready"], 1)
                dve.wait_ge(s["x1_ready"], c + 1)
                stats(1, c, X)
            for c in range(CHUNKS):
                dve.wait_ge(ln_rstd[1], c + 1)
                normed(1, c, tokv(5), X, RA[1], s["xh2_ready"])
            for c in range(CHUNKS):
                dve.wait_ge(s["h2T_ready"], c + 1)
                now, before = hT[:, 1 + c * CT:1 + (c + 1) * CT], hT[:, ch(c)]
                step(dve.tensor_tensor(S[0][:, ch(c)], now, before, ALU.subtract))
                did(dve.scalar_tensor_tensor(S[4][:, ch(c)], S[0][:, ch(c)], vc("cr"), before, ALU.mult, ALU.add))
                dve.scalar_tensor_tensor(S[3][:, ch(c)], S[0][:, ch(c)], vc("ck"), before, ALU.mult,
                                         ALU.add).then_inc(s["mix2_ready"], 1)
            for c in range(CHUNKS):
                dve.wait_ge(s["vv2_done"], c + 1)
                dve.wait_ge(s["tc_ready"], c + 1)
                dve.scalar_tensor_tensor(S[6][:, ch(c)], B[c], vc("bcv"), S[2][:, ch(c)], ALU.add,
                                         ALU.mult).then_inc(s["q_ready"], 1)
            for c in range(CHUNKS):
                dve.wait_ge(s["t3_done"], c + 1)
                step(dve.scalar_tensor_tensor(X[:, tl(c), :], bt4(4 + c), 0.5, X[:, tl(c), :], ALU.mult, ALU.add))
                dve.tensor_tensor(H[:, tl(c), :], H[:, tl(c), :], X[:, tl(c), :], ALU.add).then_inc(s["h1_ready"], 1)
                dve.wait_ge(s["h1_ready"], c + 1)
                stats(2, c, H)
            for c in range(CHUNKS):
                dve.wait_ge(ln_rstd[2], c + 1)
                normed(2, c, X, H, RA[2], s["xh3_ready"])
            for c in range(CHUNKS):
                dve.wait_ge(s["qhi_ready"], c + 1)
                dve.scalar_tensor_tensor(QLO[:, ch(c)], B[4], vc("bq"), QHI[:, ch(c)].bitcast(f32), ALU.add,
                                         ALU.subtract).then_inc(s["qlo_ready"], 1)
                dve.wait_ge(s["khi_ready"], c + 1)
                dve.scalar_tensor_tensor(KLO[:, c % 2, :], B[5], vc("bkf"), KHI[:, c % 2, :].bitcast(f32), ALU.add,
                                         ALU.subtract).then_inc(s["klo_ready"], 1)
                dve.wait_ge(s["vt_done"], c + 1)
                dve.tensor_tensor(val(c)[:, :, :, 0:HD], B[c].rearrange("p (t h d) -> p t h d", t=TPC, d=HD),
                                  rowv("bvf").rearrange("p (h d) -> p h d", d=HD).unsqueeze(1).to_broadcast([P, TPC, HEADS, HD]),
                                  ALU.add).then_inc(s["vals_ready"], 1)

            dve.wait_ge(s["ksel_done"], CHUNKS * PAIRS)
            for stack in (QM[0], QM[1], QE[0], QE[1]):
                did(dve.memset(stack[64:128, 0, :].bitcast(f32), 0.0))
                did(dve.memset(stack[0:64, 1, :].bitcast(f32), 0.0))
            settle()
            dve.memset(nm[:, :], 0.0).then_inc(s["zero_ready"], 1)
            dve.wait_ge(s["zero_ready"], 1)
            ON = tokv(6)

            def maxes(u, a, b):
                for i in range(a, b):
                    for h in range(2):
                        m = u * 32 + 2 * i + h
                        dve.wait_ge(s["mxp_done"], m + 1)
                        dve.tensor_reduce(mq[:, 2 * (i // 4) + h, i % 4:i % 4 + 1], B[m % 3], AX.X,
                                          ALU.max).then_inc(s["mxr_done"], 1)

            def negated(u):
                dve.wait_ge(s["mxr_done"], 32 * (u + 1))
                step(dve.tensor_reduce(nm[:, :], mq[:, :, :], AX.X, ALU.max, negate=True))
                if u >= 1:
                    dve.wait_ge(s["qe_done"], u)
                nmv = nm[:, :].rearrange("p (t h) -> p t h", h=2)
                step(dve.tensor_copy(AM[:, :, 48::64], nmv))
                dve.tensor_tensor(AM[:, :, 49::64], nmv, AM[:, :, 48::64].bitcast(f32), ALU.subtract).then_inc(s["nm_ready"], 1)

            def normalize(u):
                dve.wait_ge(s["dsum_done"], u + 1)
                o = B[7][:, 0:TPC * 2 * (HD + 1)].rearrange("p (t h e) -> p t h e", t=TPC, h=2)
                den = oden[:, 0, 0:2 * TPC].rearrange("p (t h) -> p t h", h=2)
                step(dve.reciprocal(den, o[:, :, :, HD]))
                j = u % PAIRS
                dve.tensor_tensor(ON[:, 0:TPC, 2 * j * HD:2 * (j + 1) * HD].rearrange("p t (h d) -> p t h d", h=2),
                                  o[:, :, :, 0:HD], den.unsqueeze(3).to_broadcast([P, TPC, 2, HD]),
                                  ALU.mult).then_inc(s["on_ready"], 1)

            def projected(q):
                dve.wait_ge(s["wo_done"], q + 1)
                dve.wait_ge(s["xb_ready"], q + 1)
                dve.tensor_tensor(tokv(4)[:, tl(q), :], bt4(7), X[:, tl(q), :], ALU.add).then_inc(s["y_ready"], 1)

            maxes(0, 0, 16)
            negated(0)
            maxes(1, 0, AHEAD)
            for u in range(UNITS):
                more = u + 1 < UNITS
                if more:
                    maxes(u + 1, AHEAD, AHEAD + 3)
                if u >= 1:
                    normalize(u - 1)
                if more:
                    maxes(u + 1, AHEAD + 3, AHEAD + 8)
                if u >= 1 and u % PAIRS == 0:
                    projected(u // PAIRS - 1)
                if more:
                    maxes(u + 1, AHEAD + 8, 16)
                    negated(u + 1)
                if u + 2 < UNITS:
                    maxes(u + 2, 0, AHEAD)
            normalize(UNITS - 1)
            projected(CHUNKS - 1)

            for c in range(CHUNKS):
                dve.wait_ge(s["y_ready"], c + 1)
                stats(3, c, tokv(4))
            for c in range(CHUNKS):
                dve.wait_ge(ln_rstd[3], c + 1)
                normed(3, c, X, tokv(4), RA[3], s["xh4_ready"])

            def over(x, k):
                return x.unsqueeze(2).to_broadcast([P, TILES, k])

            def prio(k):
                a0, _ = RO["prio"]
                return row[:, a0 + E0 - k:a0 + E0].unsqueeze(1).to_broadcast([P, TILES, k])

            def first_max(dst, src, mx, k, tmp):
                step(dve.tensor_reduce(mx, src, AX.X, ALU.max))
                step(dve.tensor_tensor(tmp, src, over(mx, k), ALU.is_equal))
                step(dve.tensor_tensor(tmp, tmp, prio(k), ALU.mult))
                step(dve.tensor_reduce(gs[:, 3, :], tmp, AX.X, ALU.max))
                step(dve.tensor_tensor(dst, tmp, over(gs[:, 3, :], k), ALU.is_equal))

            def softmaxed(src, k, ready, back):
                step(dve.tensor_reduce(gs[:, 0, :], src, AX.X, ALU.max))
                dve.tensor_tensor(gt[0][:, :, 0:k], src, over(gs[:, 0, :], k), ALU.subtract).then_inc(ready, 1)
                dve.wait_ge(ready, back)
                step(dve.tensor_reduce(gs[:, 1, :], gt[1][:, :, 0:k], AX.X, ALU.add))
                step(dve.reciprocal(gs[:, 1, :], gs[:, 1, :]))
                step(dve.tensor_tensor(gt[1][:, :, 0:k], gt[1][:, :, 0:k], over(gs[:, 1, :], k), ALU.mult))

            dve.wait_ge(s["gl_done"], 1)
            step(dve.tensor_tensor(gt[2][:, :, :], B[4][:, 0:TILES * E0].rearrange("p (t e) -> p t e", e=E0),
                                   rows_over("gateb", TILES), ALU.add))
            softmaxed(gt[2][:, :, :], E0, s["gs_ready"], 2)
            first_max(cw[:, :, :], gt[1][:, :, :], gs[:, 0, :], E0, gt[3][:, :, :])
            dve.tensor_tensor(cw[:, :, :], cw[:, :, :], over(gs[:, 0, :], E0), ALU.mult).then_inc(s["cw_ready"], 1)
            dve.wait_ge(s["cw_ready"], 1)
            ACC = tokv(6)
            for c in range(CHUNKS):
                dve.wait_ge(s["acc0_done"], c + 1)
                dve.tensor_copy(ACC[:, tl(c), :], bt4(4 + c)).then_inc(s["acc0_ready"], 1)
            for m in range(CHUNKS * E0):
                c, e = divmod(m, E0)
                dve.wait_ge(s["w2_done"], m + 1)
                dve.wait_ge(s["acc0_ready"] if m == 0 else s["acc_ready"], CHUNKS if m == 0 else m)
                for t in range(TPC):
                    g = c * TPC + t
                    ins = dve.scalar_tensor_tensor(ACC[:, g, :], bt4(4 + m % 2)[:, t, :], cw[:, g, e:e + 1], ACC[:, g, :],
                                                   ALU.mult, ALU.add)
                    if t < TPC - 1:
                        did(ins)
                ins.then_inc(s["acc_ready"], 1)
                if e == E0 - 1:
                    dve.wait_ge(s["acc_ready"], m + 1)
                    dve.tensor_tensor(H[:, tl(c), :], H[:, tl(c), :], ACC[:, tl(c), :], ALU.add).then_inc(s["h2_ready"], 1)
                    dve.wait_ge(s["h2_ready"], c + 1)
                    stats(4, c, H)
            for c in range(CHUNKS):
                dve.wait_ge(ln_rstd[4], c + 1)
                normed(4, c, X, H, RA[4], s["xh5_ready"])

            dve.wait_ge(s["w_gp"], 32)
            for g in range(2):
                did(dve.tensor_reduce(gpm[:, g, :], S[2 + g][:, 0:T].rearrange("p (g n) -> p n g", n=WS), AX.X, ALU.add))
            dve.wait_ge(s["x2T_ready"], CHUNKS)
            dve.tensor_reduce(xm[:, :], S[5][:, 0:T].rearrange("p (w n) -> p n w", n=WS), AX.X, ALU.add).then_inc(s["xm_ready"], 1)
            dve.wait_ge(s["gm_done"], 1)
            did(dve.tensor_scalar(qm[:, :, :], B[4][:, 0:2 * WS].rearrange("p (g n) -> p g n", g=2), WS / T, None, ALU.mult))
            did(dve.tensor_scalar(km[:, :, :], B[4][:, 2 * WS:4 * WS].rearrange("p (g n) -> p g n", g=2), WS / T, None, ALU.mult))
            step(dve.tensor_scalar(gpm[:, :, :], gpm[:, :, :], 1.0 / G1, None, ALU.mult))
            step(dve.tensor_tensor(qm[:, :, :], qm[:, :, :], gpm[:, :, :], ALU.mult))
            step(dve.tensor_reduce(gq[:, 0:2], qm[:, :, :], AX.X, ALU.add))
            dve.wait_ge(s["gate_sig"], 1)
            step(dve.scalar_tensor_tensor(gq[:, 2:4], gq[:, 0:2], D ** -0.5, gat[:, :], ALU.mult, ALU.mult))
            dve.tensor_copy(gqb[:, :, :], gq[:, 2:4].unsqueeze(2).to_broadcast([P, 2, P])).then_inc(s["gq_ready"], 1)
            dve.wait_ge(s["gb_done"], 1)
            btv = BT[:, :, :].rearrange("p h m -> p (h m)")
            dve.wait_ge(s["w_lb"], 32)
            for j in range(4):
                ins = dve.tensor_tensor(btv[:, j * P:(j + 1) * P], btv[:, j * P:(j + 1) * P], B[j][:, 0:P], ALU.add)
                if j < 3:
                    did(ins)
            ins.then_inc(s["bt_ready"], 1)
            dve.wait_ge(s["bt_ready"], 1)

            W = X[:, :, :].rearrange("p t d -> p (t d)").rearrange("p (r m) -> p r m", m=WS)

            def window_out(c):
                dve.wait_ge(s["ov_done"], c + 1)
                ob = tokv(4 + 2 * (c % 2))[:, 0:TPC, :].rearrange("p t (g j d) -> p t g j d", g=2, d=HD)
                for g in range(2):
                    o = B[6 + g].rearrange("p (t j e) -> p t j e", t=TPC, j=4)
                    den = oden[:, g, :].rearrange("p (t j) -> p t j", j=4)
                    step(dve.reciprocal(den, o[:, :, :, HD]))
                    ins = dve.tensor_tensor(ob[:, :, g, :, :], o[:, :, :, 0:HD],
                                            den.unsqueeze(3).to_broadcast([P, TPC, 4, HD]), ALU.mult)
                    if g == 0:
                        did(ins)
                ins.then_inc(s["o_ready"], 1)

            def residual3(c):
                dve.wait_ge(s["pr_done"], c + 1)
                dve.wait_ge(s["h3b_ready"], c + 1)
                dve.tensor_tensor(H[:, tl(c), :], H[:, tl(c), :], bt4(5), ALU.add).then_inc(s["h3_ready"], 1)
                dve.wait_ge(s["h3_ready"], c + 1)
                stats(5, c, H)

            for c in range(CHUNKS):
                ns, ex = sco(2 + c % 2), sco(4 + 2 * (c % 2))
                for j in range(4):
                    dve.wait_ge(s["s_done"], 4 * c + j + 1)
                    if c >= 2:
                        dve.wait_ge(s["e_in"], c - 1)
                    ins = dve.scalar_tensor_tensor(S[2 + c % 2][:, j * CT:(j + 1) * CT].rearrange("p (t x) -> p t x", t=TPC),
                                                   B[j].rearrange("p (t x) -> p t x", t=TPC), -(D ** -0.5),
                                                   btv[:, j * P:(j + 1) * P].unsqueeze(1).to_broadcast([P, TPC, P]),
                                                   ALU.mult, ALU.subtract)
                    ins.then_inc(s["ns_ready"], 1)
                dve.wait_ge(s["ns_ready"], 4 * (c + 1))
                if c >= 1:
                    dve.wait_ge(s["e_in"], c)
                dve.tensor_reduce(mn[:, :], ns, AX.X, ALU.min).then_inc(s["mn_ready"], 1)
                for r in range(32):
                    did(dve.max(t8[:, 0, r, :], ns[:, r, :]))
                for r in range(32):
                    settle(31)
                    did(dve.match_replace(W[:, r, :], t8[:, 0, r, :], ns[:, r, :], NEG))
                for r in range(32):
                    settle(31)
                    did(dve.max(t8[:, 1, r, :], W[:, r, :]))
                for r in range(32):
                    settle(31)
                    did(dve.match_replace(W[:, r, :], t8[:, 1, r, :], W[:, r, :], NEG))
                for r in range(32):
                    settle(31)
                    did(dve.max(t8[:, 2, r, :], W[:, r, :]))
                settle()
                if c >= 1:
                    window_out(c - 1)
                dve.wait_ge(s["e_in"], c + 1)
                step(dve.tensor_tensor(ns, ns, t8[:, 2, :, DROP - 16:DROP - 15].to_broadcast([P, 32, WS]), ALU.is_le))
                dve.wait_ge(s["e_ready"], c + 1)
                dve.tensor_tensor(ex, ex, ns, ALU.mult).then_inc(s["p1_ready"], 1)
                if c >= 1:
                    residual3(c - 1)
            window_out(CHUNKS - 1)
            residual3(CHUNKS - 1)

            for c in range(CHUNKS):
                dve.wait_ge(ln_rstd[5], c + 1)
                normed(5, c, X, H, RB, s["xh6_ready"])
            dve.wait_ge(s["g2_done"], 1)
            g2 = B[5][:, 0:TILES * (2 + E1)].rearrange("p (t e) -> p t e", e=2 + E1)
            step(dve.tensor_tensor(gt[2][:, :, 0:2], g2[:, :, 0:2], rows_over("gb", TILES), ALU.add))
            step(dve.tensor_tensor(gt[3][:, :, :], g2[:, :, 2:2 + E1], rows_over("eb", TILES), ALU.add))
            v = gs[:, 2, :]
            step(dve.tensor_tensor(v, gt[2][:, :, 1], gt[2][:, :, 0], ALU.is_gt))
            grp = gpick
            step(dve.tensor_copy(grp[:, :, 1], v))
            step(dve.tensor_scalar(grp[:, :, 0], v, -1.0, 1.0, ALU.mult, ALU.add))
            did(dve.tensor_tensor(gt[3][:, :, 0:EG], gt[3][:, :, 0:EG], over(grp[:, :, 0], EG), ALU.mult))
            step(dve.tensor_tensor(gt[3][:, :, EG:E1], gt[3][:, :, EG:E1], over(grp[:, :, 1], EG), ALU.mult))
            step(dve.tensor_tensor(gt[2][:, :, 0:EG], gt[3][:, :, 0:EG], gt[3][:, :, EG:E1], ALU.add))
            softmaxed(gt[2][:, :, 0:EG], EG, s["gs_ready"], 4)
            pr, o1, o2, tmp = gt[1][:, :, 0:EG], gt[2][:, :, 0:EG], gt[2][:, :, EG:E1], gt[3][:, :, 0:EG]
            first_max(o1, pr, gs[:, 0, :], EG, tmp)
            step(dve.scalar_tensor_tensor(pr, o1, -4.0, pr, ALU.mult, ALU.add))
            first_max(o2, pr, gs[:, 1, :], EG, tmp)
            step(dve.tensor_tensor(gs[:, 2, :], gs[:, 0, :], gs[:, 1, :], ALU.add))
            step(dve.tensor_scalar(gs[:, 2, :], gs[:, 2, :], 1e-8, None, ALU.add))
            step(dve.reciprocal(gs[:, 2, :], gs[:, 2, :]))
            did(dve.tensor_tensor(gs[:, 0, :], gs[:, 0, :], gs[:, 2, :], ALU.mult))
            step(dve.tensor_tensor(gs[:, 1, :], gs[:, 1, :], gs[:, 2, :], ALU.mult))
            did(dve.tensor_tensor(tmp, o1, over(gs[:, 0, :], EG), ALU.mult))
            did(dve.tensor_tensor(pr, o2, over(gs[:, 1, :], EG), ALU.mult))
            step(dve.tensor_tensor(o1, o1, o2, ALU.add))
            step(dve.tensor_tensor(tmp, tmp, pr, ALU.add))
            for g in range(2):
                did(dve.tensor_tensor(gt[0][:, :, g * EG:(g + 1) * EG], o1, over(grp[:, :, g], EG), ALU.mult))
                ins = dve.tensor_tensor(cw[:, :, g * EG:(g + 1) * EG], tmp, over(grp[:, :, g], EG), ALU.mult)
                if g == 0:
                    did(ins)
            ins.then_inc(s["c2_ready"], 1)
            dve.wait_ge(s["c2_ready"], 1)
            OA, OBB = tokv(2), tokv(3)
            for c in range(CHUNKS):
                for k in range(4):
                    dve.wait_ge(s["sil_ready"], 4 * c + k + 1)
                    sl = S[c % 2][:, k * CT:(k + 1) * CT]
                    dve.tensor_tensor(sl, sl, B[2 * (k % 2) + 1], ALU.mult).then_inc(s["hsw_ready"], 1)
                dve.wait_ge(s["sh_done"], c + 1)
                step(dve.tensor_tensor(H[:, tl(c), :], H[:, tl(c), :], rows_over("shb", TPC), ALU.add))
                dve.tensor_tensor(H[:, tl(c), :], H[:, tl(c), :], bt4(4), ALU.add).then_inc(s["xev_ready"], 1)
                dve.wait_ge(s["xev_ready"], UNITS + c + 1)
                for t in range(TPC):
                    g = c * TPC + t
                    dve.wait_ge(s["ex_done"], g + 1)
                    b0 = 6 if t % 2 == 0 else 2
                    for e in range(E1):
                        dst = (OA if e % 2 == 0 else OBB)[:, g, :]
                        src = PS[:, b0 + e // 4, (e % 4) * D:(e % 4 + 1) * D]
                        if e < 2:
                            did(dve.tensor_scalar(dst, src, cw[:, g, e:e + 1], None, ALU.mult))
                            continue
                        settle(1)
                        ins = dve.scalar_tensor_tensor(dst, src, cw[:, g, e:e + 1], dst, ALU.mult, ALU.add)
                        if e < E1 - 1:
                            did(ins)
                    ins.then_inc(s["cb_ready"], 1)
                    dve.wait_ge(s["cb_ready"], g + 1)
                step(dve.tensor_tensor(OA[:, tl(c), :], OA[:, tl(c), :], OBB[:, tl(c), :], ALU.add))
                dve.tensor_tensor(H[:, tl(c), :], H[:, tl(c), :], OA[:, tl(c), :], ALU.add).then_inc(s["fin_ready"], 1)

        @block.tensor
        def _(pe):
            def transposes(dst, src, done):
                for t in range(TPC):
                    ins = pe.transpose(dst[:, t * P:(t + 1) * P], src(t), ID[:, :])
                ins.then_inc(done, 1)

            def w(i):
                return wr[:, i * D:(i + 1) * D]

            pe.wait_ge(s["w_misc"], 64)
            for c in range(CHUNKS):
                pe.wait_ge(s["xh_ready"], c + 1)
                transposes(B[c], lambda t: tokv(0)[:, c * TPC + t, :], s["t1_done"])
            pe.wait_ge(s["w_rwkv"], 16)
            for c in range(CHUNKS):
                pe.wait_ge(s["mix_ready"], c + 1)
                if c >= 2:
                    pe.wait_ge(s["gate_ready"], c - 1)
                pe.matmul(B[4 + c % 2], w(0), S[2][:, ch(c)], start=True, stop=True).then_inc(s["k_done"], 1)
                if c >= 2:
                    pe.wait_ge(s["wv_ready"], c - 1)
                pe.matmul(B[6 + c % 2], w(1), S[3][:, ch(c)], start=True, stop=True).then_inc(s["v_done"], 1)
                pe.matmul(B[c], w(2), S[4][:, ch(c)], start=True, stop=True).then_inc(s["r_done"], 1)
            for c in range(CHUNKS):
                pe.wait_ge(s["z_ready"], c + 1)
                for t in range(TPC):
                    g = (c * TPC + t) * P
                    ins = pe.matmul(B[c][:, t * D:(t + 1) * D], S[0][:, g:g + P], w(3), start=True, stop=True)
                ins.then_inc(s["woo_done"], 1)
            for c in range(CHUNKS):
                pe.wait_ge(s["xh2_ready"], c + 1)
                transposes(B[4 + c], lambda t: tokv(5)[:, c * TPC + t, :], s["t2_done"])
            pe.wait_ge(s["w_ck"], 32)

            def ckr(c):
                pe.wait_ge(s["mix2_ready"], c + 1)
                if c == 0:
                    pe.wait_ge(s["h2T_ready"], CHUNKS)
                for f in range(FC):
                    if c >= 1:
                        pe.wait_ge(s["gelu_ready"], FC * (c - 1) + f + 1)
                    pe.matmul(B[4 + f], wck[:, f * P:(f + 1) * P], S[3][:, ch(c)], start=True, stop=True).then_inc(s["ck_done"], 1)
                pe.wait_ge(s["x1_ready"], c + 1)
                pe.matmul(B[c], w(4), S[4][:, ch(c)], start=True, stop=True).then_inc(s["cr_done"], 1)

            ckr(0)
            for c in range(CHUNKS):
                if c + 1 < CHUNKS:
                    ckr(c + 1)
                pe.wait_ge(s["gelu_ready"], FC * (c + 1))
                pe.wait_ge(s["tc_ready"], c + 1)
                for f in range(FC):
                    ins = pe.matmul(B[c], wcv[:, f, :], G[:, c % 2, f, :], start=f == 0, stop=f == FC - 1)
                ins.then_inc(s["vv2_done"], 1)
            for c in range(CHUNKS):
                pe.wait_ge(s["q_ready"], c + 1)
                transposes(B[4 + c], lambda t: S[6][:, (c * TPC + t) * P:(c * TPC + t + 1) * P], s["t3_done"])
            for c in range(CHUNKS):
                pe.wait_ge(s["xh3_ready"], c + 1)
                transposes(B[c], lambda t: X[:, c * TPC + t, :], s["t4_done"])
            pe.wait_ge(s["w_ffn"], 32)
            pe.wait_ge(s["selr_ready"], 1)
            pe.wait_ge(s["h1_ready"], CHUNKS)
            for c in range(CHUNKS):
                pe.wait_ge(s["x1T_ready"], c + 1)
                if c >= 1:
                    pe.wait_ge(s["qlo_ready"], c)
                pe.matmul(B[4], wf[:, 0:D], S[0][:, ch(c)], start=True, stop=True).then_inc(s["q_done"], 1)
                if c >= 1:
                    pe.wait_ge(s["klo_ready"], c)
                pe.matmul(B[5], wf[:, D:2 * D], S[0][:, ch(c)], start=True, stop=True).then_inc(s["kk_done"], 1)
                for t in range(TPC):
                    g = (c * TPC + t) * P
                    ins = pe.matmul(B[c][:, t * D:(t + 1) * D], S[0][:, g:g + P], wf[:, 2 * D:3 * D], start=True, stop=True)
                ins.then_inc(s["vt_done"], 1)
                pe.wait_ge(s["klo_ready"], c + 1)
                for j in range(PAIRS):
                    i = PAIRS * c + j
                    if i >= 2:
                        pe.wait_ge(s["kst_ready"], i - 1)
                    pe.matmul(B[6 + j % 2], SELR[:, 8 + j, :], KHI[:, c % 2, :], start=True, stop=False)
                    pe.matmul(B[6 + j % 2], SELR[:, 12 + j, :], KLO[:, c % 2, :], start=False, stop=True).then_inc(s["ksel_done"], 1)

            def qsel(u, last):
                q, j = divmod(u, PAIRS)
                pe.matmul(B[7], SELR[:, j, :], QHI[:, ch(q)], start=True, stop=False)
                return pe.matmul(B[7], SELR[:, 4 + j, :], QLO[:, ch(q)], start=False, stop=last)

            def maxes(u, i):
                j = u % PAIRS
                t, kq = divmod(i, 4)
                for h in range(2):
                    m = 32 * u + 2 * i + h
                    if m >= 3:
                        pe.wait_ge(s["mxr_done"], m - 2)
                    pe.matmul(B[m % 3], QM[u % 2][:, h, t * P:(t + 1) * P], KST[:, j, kq * CT:(kq + 1) * CT],
                              start=True, stop=True).then_inc(s["mxp_done"], 1)

            def scores(u, k):
                m, j = u * TILES + k, u % PAIRS
                for h in range(2):
                    b = 2 * m + h
                    if b >= 3:
                        pe.wait_ge(s["p_ready"], b - 2)
                    pe.matmul(B[3 + b % 3], KST[:, j, k * P:(k + 1) * P], QE[u % 2][:, h, :], start=True,
                              stop=True).then_inc(s["st_done"], 1)

            def weigh(u, kp):
                j = u % PAIRS
                pe.wait_ge(s["p_ready"], 2 * (u * TILES + 2 * kp + 2))
                if kp == 0 and u >= 1:
                    pe.wait_ge(s["xev_ready"], u)
                for h in range(2):
                    for par in range(2):
                        k = 2 * kp + par
                        q = 32 * (2 * h + par)
                        ins = pe.matmul(B[6][q:q + 32, :], valh(k, 2 * j + h), prob(u * TILES + k)[:, h, :],
                                        start=kp == 0, stop=kp == TILES // 2 - 1, tile_position=(0, q))
                ins.then_inc(s["av_done"], 1)

            def attended(q):
                pe.wait_ge(s["on_ready"], PAIRS * (q + 1))
                transposes(B[7], lambda t: tokv(6)[:, t, :], s["ot_done"])

            def project(q):
                pe.wait_ge(s["ot_ready"], q + 1)
                for t in range(TPC):
                    ins = pe.matmul(B[7][:, t * D:(t + 1) * D], S[5][:, CT + t * P:CT + (t + 1) * P], wof[:, :],
                                    start=True, stop=True)
                ins.then_inc(s["wo_done"], 1)

            def dsum(u):
                pe.wait_ge(s["xev_ready"], u + 1)
                n = 2 * (HD + 1)
                for t in range(TPC):
                    ins = pe.matmul(B[7][:, t * n:(t + 1) * n], S[5][:, t * P:(t + 1) * P], SELO[:, :], start=True, stop=True)
                ins.then_inc(s["dsum_done"], 1)

            def with_max(u):
                pe.wait_ge(s["nm_ready"], u + 1)
                qsel(u, False)
                for t in range(TPC):
                    ins = pe.matmul(B[7][:, t * P:(t + 1) * P], AM[:, t, :], IDR[:, :], start=False, stop=t == TPC - 1)
                ins.then_inc(s["qe_done"], 1)

            pe.wait_ge(s["vals_ready"], CHUNKS)
            pe.wait_ge(s["kst_ready"], CHUNKS * PAIRS)
            pe.wait_ge(s["qlo_ready"], CHUNKS)
            qsel(0, True).then_inc(s["qsel_done"], 1)
            pe.wait_ge(s["zero_ready"], 1)
            pe.wait_ge(s["qm_ready"], 1)
            for i in range(16):
                maxes(0, i)
            with_max(0)
            pe.wait_ge(s["qe_ready"], 1)
            qsel(1, True).then_inc(s["qsel_done"], 1)
            pe.wait_ge(s["qm_ready"], 2)
            for i in range(AHEAD):
                maxes(1, i)
            for u in range(UNITS):
                q = u // PAIRS
                for k in range(TILES):
                    scores(u, k)
                    v, i = divmod(16 * (u + 1) + k + AHEAD, 16)
                    if v < UNITS:
                        if i == 0:
                            pe.wait_ge(s["qm_ready"], v + 1)
                        maxes(v, i)
                    if k == 2 and u >= 1:
                        dsum(u - 1)
                    if k == 5 and u >= 1 and u % PAIRS == 0:
                        attended(q - 1)
                    if k == 7 and u >= 1 and u % PAIRS == 0:
                        project(q - 1)
                    if k == 9:
                        if u >= 1:
                            pe.wait_ge(s["on_ready"], u)
                        if u >= 1 and u % PAIRS == 0:
                            pe.wait_ge(s["y_ready"], q)
                        if u + 2 < UNITS:
                            qsel(u + 2, True).then_inc(s["qsel_done"], 1)
                    if k == 13 and u + 1 < UNITS:
                        if u + 2 < UNITS:
                            pe.wait_ge(s["qm_ready"], u + 3)
                        with_max(u + 1)
                    if k % 4 == 1:
                        g = u * 4 + (k - 5) // 4
                        if g >= 0:
                            weigh(g // 4, 2 * (g % 4))
                            weigh(g // 4, 2 * (g % 4) + 1)
                if u + 1 < UNITS:
                    pe.wait_ge(s["qe_ready"], u + 2)
            weigh(UNITS - 1, TILES // 2 - 2)
            weigh(UNITS - 1, TILES // 2 - 1)
            pe.wait_ge(s["on_ready"], UNITS - 1)
            dsum(UNITS - 1)
            attended(CHUNKS - 1)
            project(CHUNKS - 1)

            for c in range(CHUNKS):
                pe.wait_ge(s["xh4_ready"], c + 1)
                transposes(B[c], lambda t: X[:, c * TPC + t, :], s["t5_done"])
            pe.wait_ge(s["tT_ready"], CHUNKS)
            for t in range(TILES):
                ins = pe.matmul(B[4][:, t * E0:(t + 1) * E0], S[5][:, t * P:(t + 1) * P], wf[:, 3 * D:3 * D + E0],
                                start=True, stop=True)
            ins.then_inc(s["gl_done"], 1)
            pe.wait_ge(s["cw_ready"], 1)
            for t in range(TILES):
                ins = pe.transpose(B[t // TPC][0:E0, (t % TPC) * P:(t % TPC + 1) * P], cw[:, t, :], ID[:, :])
            ins.then_inc(s["cT_done"], 1)
            pe.wait_ge(s["cT_ready"], 1)
            pe.wait_ge(s["w_d"], 96)
            for c in range(CHUNKS):
                for t in range(TPC):
                    ins = pe.matmul(B[4 + c][:, t * D:(t + 1) * D], cT[:, (c * TPC + t) * P:(c * TPC + t + 1) * P], b2r[:, :],
                                    start=True, stop=True)
                ins.then_inc(s["acc0_done"], 1)
            pe.wait_ge(s["w_moe"], 64)

            def up(m):
                c, e = divmod(m, E0)
                for f in range(FC):
                    if m >= 1:
                        pe.wait_ge(s["hid_ready"], FC * (m - 1) + f + 1)
                    o = (e % 4) * FF + f * P
                    pe.matmul(B[f], S[e // 4][:, o:o + P], S[5][:, ch(c)], start=True, stop=True).then_inc(s["w1_done"], 1)

            def down(m):
                e = m % E0
                pe.wait_ge(s["hid_ready"], FC * (m + 1))
                if m < 2:
                    pe.wait_ge(s["acc0_ready"], m + 1)
                else:
                    pe.wait_ge(s["acc_ready"], m - 1)
                for t in range(TPC):
                    for f in range(FC):
                        o = (e % 4) * FF + f * D
                        ins = pe.matmul(B[4 + m % 2][:, t * D:(t + 1) * D], G[:, m % 2, f, t * P:(t + 1) * P],
                                        S[2 + e // 4][:, o:o + D], start=f == 0, stop=f == FC - 1)
                ins.then_inc(s["w2_done"], 1)

            up(0)
            for m in range(CHUNKS * E0):
                if m + 1 < CHUNKS * E0:
                    up(m + 1)
                down(m)

            for c in range(CHUNKS):
                pe.wait_ge(s["xh5_ready"], c + 1)
                if c == 0:
                    pe.wait_ge(s["hid_ready"], FC * CHUNKS * E0)
                transposes(B[c], lambda t: X[:, c * TPC + t, :], s["t6_done"])
            pe.wait_ge(s["w_l1"], 16)
            pe.wait_ge(s["xm_ready"], 1)
            for k in range(4):
                ins = pe.matmul(B[4][:, k * WS:(k + 1) * WS], wl[:, k * P:(k + 1) * P], xm[:, :], start=True, stop=True)
            ins.then_inc(s["gm_done"], 1)
            pe.wait_ge(s["gq_ready"], 1)
            for g in range(2):
                for j in range(4):
                    r = slice(32 * j, 32 * j + 32)
                    ins = pe.matmul(B[j][:, g * WS:(g + 1) * WS], gqb[r, g, :], km[r, g, :], start=True, stop=True,
                                    tile_position=(32 * j, 0))
            ins.then_inc(s["gb_done"], 1)

            def window_scores(c):
                for k in range(4):
                    if k < 2:
                        if c >= 1:
                            pe.wait_ge(s["v1_ready"], 2 * (c - 1) + k + 1)
                        if c >= 2:
                            pe.wait_ge(s["pt_ready"], 4 * (c - 2) + 4)
                    else:
                        pe.wait_ge(s["qk_ready"], 4 * c + k - 1)
                    pe.matmul(B[4 + k % 2], wl[:, k * P:(k + 1) * P], S[5][:, ch(c)], start=True, stop=True).then_inc(s["qk_done"], 1)
                wv = wl[:, 4 * P:5 * P]
                pe.wait_ge(s["qk_ready"], 4 * c + 3)
                for t in range(TPC):
                    g = (c * TPC + t) * P
                    ins = pe.matmul(B[4][:, t * D:(t + 1) * D], S[5][:, g:g + P], wv, start=True, stop=True)
                ins.then_inc(s["v1_done"], 1)
                pe.wait_ge(s["qk_ready"], 4 * c + 4)
                for t in range(TPC):
                    for par in range(2):
                        g = (c * TPC + t) * P + WS * par
                        o = WS * (1 - par)
                        ins = pe.matmul(B[5][o:o + WS, t * D:(t + 1) * D], S[5][:, g:g + WS], wv, start=True, stop=True,
                                        tile_position=(0, o))
                ins.then_inc(s["v1_done"], 1)
                for j in range(4):
                    if c == 0:
                        pe.wait_ge(s["bt_ready"], 1)
                    else:
                        pe.wait_ge(s["ns_ready"], 4 * (c - 1) + j + 1)
                for j in range(4):
                    r = slice(32 * j, 32 * j + 32)
                    for t in range(TPC):
                        for g in range(2):
                            for par in range(2):
                                x = t * P + WS * par
                                o = (2 * t + g) * WS
                                ins = pe.matmul(B[j][WS * par:WS * par + WS, o:o + WS],
                                                S[c % 2][r, g * CT + x:g * CT + x + WS],
                                                S[c % 2][r, (2 + g) * CT + x:(2 + g) * CT + x + WS],
                                                start=True, stop=True, tile_position=(32 * j, WS * par))
                    ins.then_inc(s["s_done"], 1)

            window_scores(0)
            window_scores(1)
            for c in range(CHUNKS):
                pe.wait_ge(s["p1_ready"], c + 1)
                for k in range(4):
                    if k < 2:
                        pe.wait_ge(s["v1_ready"], 2 * min(c + 2, CHUNKS))
                        if c >= 1:
                            pe.wait_ge(s["oT_ready"] if k == 0 else s["h3_ready"], c)
                    else:
                        pe.wait_ge(s["pt_ready"], 4 * c + k - 1)
                    transposes(B[4 + k % 2], lambda t: sco2(4 + 2 * (c % 2))[:, (k * TPC + t) * P:(k * TPC + t + 1) * P], s["pt_done"])
                pe.wait_ge(s["pt_ready"], 4 * (c + 1))
                if c >= 1:
                    pe.wait_ge(s["o_ready"], c)
                for g in range(2):
                    r = slice(WS * g, WS * g + WS)
                    for t in range(TPC):
                        for j in range(4):
                            for par in range(2):
                                o = (c % 2) * T + (j * TPC + t) * P + WS * par
                                ins = pe.matmul(B[6 + g][WS * par:WS * par + WS, (t * 4 + j) * 32:(t * 4 + j + 1) * 32],
                                                PB[r, o:o + WS], vwin(c, 0 if g == par else 1)[r, t, 4 * g + j, :],
                                                start=True, stop=True, tile_position=(WS * g, WS * par))
                ins.then_inc(s["ov_done"], 1)
                if c + 2 < CHUNKS:
                    window_scores(c + 2)
                pe.wait_ge(s["o_ready"], c + 1)
                if c + 2 < CHUNKS:
                    pe.wait_ge(s["v1_ready"], 2 * (c + 3))
                transposes(B[4], lambda t: tokv(4 + 2 * (c % 2))[:, t, :], s["t7_done"])
                pe.wait_ge(s["oT_ready"], c + 1)
                for t in range(TPC):
                    g = (c * TPC + t) * P
                    ins = pe.matmul(B[5][:, t * D:(t + 1) * D], S[5][:, g:g + P], wl[:, 5 * P:6 * P], start=True, stop=True)
                ins.then_inc(s["pr_done"], 1)

            for c in range(CHUNKS):
                pe.wait_ge(s["xh6_ready"], c + 1)
                transposes(B[c], lambda t: X[:, c * TPC + t, :], s["t8_done"])
            pe.wait_ge(s["fT_ready"], CHUNKS)
            for t in range(TILES):
                ins = pe.matmul(B[5][:, t * (2 + E1):(t + 1) * (2 + E1)], S[5][:, t * P:(t + 1) * P], wg1[:, :],
                                start=True, stop=True)
            ins.then_inc(s["g2_done"], 1)
            pe.wait_ge(s["c2_ready"], 1)
            for t in range(TILES):
                ins = pe.transpose(B[t // TPC][0:E1, (t % TPC) * P:(t % TPC + 1) * P], gt[0][:, t, :], ID[:, :])
            ins.then_inc(s["cn_done"], 1)
            pe.wait_ge(s["cn_ready"], 1)
            pe.wait_ge(s["wex_in"], 16)
            wex = V[:, 0:2 * E1 * D].rearrange("p (k n) -> p k n", k=2)
            for c in range(CHUNKS):
                for k in range(4):
                    if 4 * c + k >= 2:
                        pe.wait_ge(s["hsw_ready"], 4 * c + k - 1)
                    if k % 2 == 1 and c >= 1:
                        pe.wait_ge(s["cb_ready"], TPC * c)
                    m, half = divmod(k, 2)
                    x = S[5][:, ch(c)]
                    b0 = 2 * (k % 2)
                    pe.matmul(B[b0], win[:, m, half * P:(half + 1) * P], x, start=True, stop=True)
                    pe.matmul(B[b0 + 1], win[:, m, H1 + half * P:H1 + (half + 1) * P], x, start=True,
                              stop=True).then_inc(s["in_done"], 1)
                pe.wait_ge(s["hsw_ready"], 4 * c + 4)
                if c >= 1:
                    pe.wait_ge(s["xev_ready"], UNITS + c)
                for t in range(TPC):
                    dst = B[4][:, t * D:(t + 1) * D]
                    for k in range(2):
                        pe.matmul(dst, S[c % 2][:, k * CT + t * P:k * CT + (t + 1) * P], wso[:, k, :], start=k == 0, stop=False)
                    ins = pe.matmul(dst, cT[:, (c * TPC + t) * P:(c * TPC + t + 1) * P], eob[:, :], start=False, stop=True)
                ins.then_inc(s["sh_done"], 1)
                for t in range(TPC):
                    g = c * TPC + t
                    b0 = 6 if t % 2 == 0 else 2
                    if g >= 2:
                        pe.wait_ge(s["cb_ready"], g - 1)
                    for half in range(2):
                        for k in range(2):
                            ins = pe.matmul(B[b0 + half], S[c % 2][:, (2 + k) * CT + t * P:(2 + k) * CT + (t + 1) * P],
                                            wex[:, k, half * CT:(half + 1) * CT], start=k == 0, stop=k == 1)
                    ins.then_inc(s["ex_done"], 1)


def kernel(**inputs):
    import numpy as np
    import concourse.bacc as bacc
    from concourse.bass_utils import run_bass_kernel_spmd

    g = {k: np.asarray(v) for k, v in inputs.items()}

    def col(a):
        return np.ascontiguousarray(a).reshape(D, 1)

    f = np.float32
    pos = np.arange(1, T + 1, dtype=f)[:, None]
    i = np.arange(D)
    exponent = np.where(i % 2 == 0, i, i + 1).astype(f) / f(D)
    angle = (pos / np.power(f(10000.0), exponent)).astype(f)
    pe = np.where(i % 2 == 0, np.cos(angle), np.sin(angle)).astype(f)

    a = {}
    a["idx"] = np.ascontiguousarray(g["x"].reshape(TILES, P).T)
    a["emb"] = np.ascontiguousarray(g["L0_tok_W"].T)
    a["pe"] = np.ascontiguousarray(pe.reshape(TILES, P, D).transpose(1, 0, 2)).reshape(P, T)
    r = "L0_attn_"
    a["vec"] = np.concatenate([col(g[n]) for n in (
        r + "bk", r + "bv", r + "br", r + "bcv", r + "bcr", r + "ln1_g", r + "ln1_b", r + "ln2_g", r + "ln2_b",
        r + "time_decay", r + "time_first", r + "tmk", r + "tmv", r + "tmr", r + "cmk", r + "cmr",
        "L0_ffn_bq", "L0_ffn_bk", "L0_ffn_ln1_g", "L0_ffn_ln1_b", "L1_ffn_ln_scale", "L1_ffn_ln_bias")], 1)
    a["rows"] = np.concatenate([g["L0_tok_b"], g[r + "bo"], g["L0_ffn_bv"], g["L0_ffn_bo"], g["L0_ffn_gate_b"],
                                g["L1_attn_b_out"], g["L1_ffn_shared_out_b"], g["L1_ffn_group_bias"],
                                g["L1_ffn_expert_bias"], np.arange(E0, 0, -1).astype(f)]).reshape(1, NR)
    a["w_rwkv"] = np.concatenate([g[r + n] for n in ("Wk", "Wv", "Wr", "Wo", "Wcr")], 1)
    a["w_ck"] = g[r + "Wck"]
    a["w_cv"] = np.ascontiguousarray(g[r + "Wcv"].reshape(FC, P, D).transpose(1, 0, 2))
    a["bckc"] = np.ascontiguousarray(g[r + "bck"].reshape(FC, P).T)
    q = "L0_ffn_"
    a["w_ffn"] = np.concatenate([g[q + "Wq"], g[q + "Wk"], g[q + "Wv"], g[q + "gate_W"]], 1)
    a["w_of"] = g[q + "Wo"]
    a["ident"] = np.eye(P, dtype=f)
    rr = np.arange(P)
    cc = np.arange(2 * (HD + 1))
    a["selo"] = ((rr[:, None] // 64 == cc[None, :] // (HD + 1)) & (rr[:, None] % 32 == cc[None, :] % (HD + 1))).astype(f)
    sel = np.zeros((P, 16, P), f)
    for j in range(PAIRS):
        for dst in range(P):
            src = (2 * j + dst // 64) * HD + dst % HD
            part = dst % 64 // HD
            if part < 3:
                sel[src, (4 if part == 1 else 0) + j, dst] = 1
                sel[src, (12 if part == 2 else 8) + j, dst] = 1
    a["sel"] = sel.reshape(P, 16 * P)
    kone = np.zeros((P, 1), f)
    kone[[48, 49, 112, 113]] = 1
    a["kone"] = kone
    a["b1c"] = np.ascontiguousarray(g[q + "b1"].reshape(E0, FC, P).transpose(2, 0, 1)).reshape(P, E0 * FC)
    a["b2r"] = g[q + "b2"]
    a["moe_w1"] = np.ascontiguousarray(g[q + "W1"].transpose(1, 0, 2)).reshape(P, E0 * FF)
    a["moe_w2"] = np.ascontiguousarray(g[q + "W2"].reshape(E0, FC, P, D).transpose(2, 0, 1, 3)).reshape(P, E0 * FF)
    w = g["L1_attn_w_qkv"]
    pads = np.zeros((D, 4, 4, 32), f)
    for k in range(4):
        part = w[:, (k // 2) * D:(k // 2 + 1) * D].reshape(D, 2, 4, HD)
        pads[:, k, :, :HD] = part[:, k % 2]
    a["w_l1"] = np.concatenate([pads.reshape(D, 4 * P), w[:, 2 * D:], g["L1_attn_w_out"]], 1)
    gt = g["L1_attn_gate"].reshape(2, 4, 1)
    a["gat"] = np.ascontiguousarray(np.broadcast_to(gt, (2, 4, 32)).reshape(2, P).T)
    gp = g["L1_attn_global_param"].reshape(2, 4, 1, G1 * WS)
    a["gp"] = np.ascontiguousarray(np.broadcast_to(gp, (2, 4, 32, G1 * WS))).reshape(2, P, G1 * WS)
    a["lb"] = np.ascontiguousarray(g["L1_attn_local_bias"].reshape(2, 4, WS, WS).transpose(2, 1, 0, 3)).reshape(WS, HEADS, WS)
    d = "L1_ffn_"
    a["w_in"] = np.ascontiguousarray(np.stack([g[d + "shared_in_w"].T, g[d + "expert_in_w"].T], 1))
    a["w_so"] = np.ascontiguousarray(g[d + "shared_out_w"].T.reshape(2, P, D).transpose(1, 0, 2))
    a["w_ex"] = np.ascontiguousarray(g[d + "expert_out_weight"].transpose(2, 0, 1).reshape(2, P, E1 * D).transpose(1, 0, 2)).reshape(P, 2 * E1 * D)
    a["w_g1"] = np.ascontiguousarray(np.concatenate([g[d + "group_gate_w"], g[d + "expert_gate_w"]], 0).T)
    a["eob"] = g[d + "expert_out_bias"]

    nc = bacc.Bacc("TRN2", target_bir_lowering=False, num_devices=1)
    arrays, args = {}, {}
    for n, v in a.items():
        v = np.ascontiguousarray(v)
        arrays["in_" + n] = v
        args[n] = nc.dram_tensor("in_" + n, v.shape, mybir.dt.from_np(v.dtype), kind="ExternalInput").ap()
    out = nc.dram_tensor("out_h", (T, D), mybir.dt.float32, kind="ExternalOutput").ap()
    build_tower(nc, args, out.rearrange("(t p) d -> p t d", p=P))
    res = run_bass_kernel_spmd(nc, [arrays], core_ids=[0])
    return res.results[0]["out_h"].reshape(1, T, D)
```

```python
import concourse.bass as bass
from concourse import mybir
from contextlib import ExitStack

T = 2048
D = 128
P = 128
TILES = T // P
CT = 512
CHUNKS = T // CT
TPC = CT // P
HEADS = 8
HD = D // HEADS
PAIRS = HEADS // 2
UNITS = CHUNKS * PAIRS
AHEAD = 6
PSLOTS = 6
FF = 4 * D
FC = FF // P
E0 = 8
XT = (T + E0 * (P - 1)) // P
XS = XT * P
WSLOTS = 4
WS = 64
G1 = 32
KEEP = int(WS * (1.0 - 0.3))
DROP = WS - KEEP
H1 = 256
E1 = 8
EG = 4
EPS = 1e-5
NEG = -3.0e38

VECS = ["bk", "bv", "br", "bcv", "bcr", "g1", "b1", "g2", "b2", "decay", "first", "mk", "mv", "mr", "ck", "cr",
        "bq", "bkf", "gf", "bf", "ls", "lb"]
VI = {n: i for i, n in enumerate(VECS)}
NV = len(VECS)
ROWS = [("tokb", D), ("bo", D), ("bvf", D), ("bof", D), ("gateb", E0), ("bout", D), ("shb", D), ("gb", 2),
        ("eb", E1), ("prio", E0),
        ("full", TILES), ("tileno", XT)]
RO = {}
NR = 0
for _n, _w in ROWS:
    RO[_n] = (NR, NR + _w)
    NR += _w


def build_tower(nc, A, out, xs, ys):
    f32, f32r, i32 = mybir.dt.float32, mybir.dt.float32r, mybir.dt.int32
    ALU, ACT, AX = mybir.AluOpType, mybir.ActivationFunctionType, mybir.AxisListType
    ctx = ExitStack()
    with ctx:
        def sb(name, shape, dt=f32):
            return ctx.enter_context(nc.sbuf_tensor("s_" + name, shape, dt))

        def sem(name):
            return ctx.enter_context(nc.semaphore(name))

        H = sb("resid", [P, TILES, D])
        X = sb("normed", [P, TILES, D])
        SW = T + 8
        SS = sb("scratch", [P, 7 * SW])
        S = [SS[:, i * SW:(i + 1) * SW] for i in range(7)]
        V = sb("vals", [P, 4096])
        PB = sb("probs", [P, 4096])
        QHI, QLO = sb("qhi", [P, T], f32r), sb("qlo", [P, T], f32r)
        KHI, KLO = sb("khi", [P, 2, CT], f32r), sb("klo", [P, 2, CT], f32r)
        KST = sb("kstack", [P, PAIRS, T], f32r)
        SELR = sb("selr", [P, 4 * PAIRS, P], f32r)
        IDR = sb("identr", [P, P], f32r)
        QM = [KHI, sb("qmax", [P, 2, CT], f32r)]
        QE = [KLO, SELR[:, 8:16, :].rearrange("p (h a) b -> p h (a b)", h=2)]
        AM = sb("amax", [P, TPC, P], f32r)
        ID = sb("ident", [P, P])
        SELO = sb("selo", [P, 2 * (HD + 1)])
        DEC = sb("dec", [P, CT])
        vec = sb("vec", [P, NV])
        drv = sb("drv", [P, 16])
        kone = sb("kone", [P, 1])
        row = sb("rows", [P, NR])
        idx = sb("idx", [P, TILES], i32)
        wrk = sb("w_rwkv", [P, 5 * D + FF])
        wr, wck = wrk[:, 0:5 * D], wrk[:, 5 * D:5 * D + FF]
        wcv = sb("w_cv", [P, FC, D])
        wf = sb("w_ffn", [P, 3 * D + E0])
        wof = sb("w_of", [P, D])
        wl = sb("w_l1", [P, 4 * D + 2 * D])
        win = sb("w_in", [P, 2, FF])
        wso = sb("w_so", [P, 2, D])
        wg1 = sb("w_g1", [P, 2 + E1])
        eob = sb("w_eob", [E1, D])
        b1c = sb("b1c", [P, E0 * FC])
        b2r = sb("b2r", [E0, D])
        bckc = sb("bckc", [P, FC])
        nh = sb("neghalf", [P, 8])
        st6 = sb("st6", [P, TILES, 6])
        MV = [sb(f"mv{i}", [P, TILES, 2]) for i in range(6)]
        RA = [sb(f"ra{i}", [P, TILES]) for i in range(6)]
        RB = sb("rb", [P, TILES])
        VE = sb("ve", [P, TILES])
        mq = sb("mq", [P, 8, 4])
        nm = sb("nm", [P, 8])
        cw = sb("cw", [P, TILES, E0])
        gt = [sb(f"gt{i}", [P, TILES, E0]) for i in range(4)]
        gs = sb("gs", [P, 4, TILES])
        cT = S[4][0:E0, 0:T]
        tri = sb("tri", [P, 2 * P])
        slot = sb("slot", [P, TILES], i32)
        tex = sb("tex", [P, XT], i32)
        b1w = sb("b1w", [P, WSLOTS, FC])
        gpm = sb("gpm", [P, 2, WS])
        xm = sb("xm", [P, WS])
        wcvf = wcv[:, :, :].rearrange("p f d -> p (f d)")
        qm = wcvf[:, 0:2 * WS].rearrange("p (g n) -> p g n", g=2)
        km = wcvf[:, 2 * WS:4 * WS].rearrange("p (g n) -> p g n", g=2)
        gq = sb("gq", [P, 8])
        gqb = wcvf[:, 4 * WS:4 * WS + 2 * P].rearrange("p (g n) -> p g n", g=2)
        gat = sb("gat", [P, 2])
        BT = DEC[:, :].rearrange("p (h m) -> p h m", m=WS)
        t8 = wrk[:, 0:768].rearrange("p (k r e) -> p k r e", k=3, e=8)
        mn = sb("mn", [P, 32])
        oden = sb("oden", [P, 2, 16])
        gpick = sb("gpick", [P, TILES, 2])

        def sco(i):
            return S[i][:, 0:T].rearrange("p (r m) -> p r m", m=WS)

        def tokv(i):
            return S[i][:, 0:T].rearrange("p (t d) -> p t d", d=D)

        PS = ctx.enter_context(nc.psum_tensor("banks", [P, 8, CT], f32))
        B = [PS[:, i, :] for i in range(8)]

        names = """w_rows w_idx w_pe w_vec w_rwkv w_ck w_ffn w_sel w_misc w_l1
            w_d w_moe w_gp w_lb w_gat h_ready xh_ready t1_done hT_ready mix_ready
            k_done v_done r_done gate_ready vv_ready wv_ready tr_ready z_ready woo_done x1_ready
            x0b_ready xh2_ready t2_done h2T_ready mix2_ready cr_done ck_done gelu_ready tc_ready vv2_done
            q_ready t3_done h1_ready xh3_ready t4_done x1T_ready q_done kk_done vt_done qhi_ready
            khi_ready qlo_ready klo_ready vals_ready ksel_done kst_ready xb_ready qsel_done qm_ready mxp_done
            mxr_done nm_ready qe_done qe_ready st_done p_ready av_done xev_ready dsum_done on_ready
            wo_done y_ready xh4_ready t5_done tT_ready gl_done cw_ready cT_done cT_ready acc0_done
            acc0_ready w1_done hid_ready w2_done acc_ready h2_ready xh5_ready t6_done x2T_ready xm_ready
            gm_done gq_ready gb_done bt_ready qk_done qk_ready v1_done v1_ready s_done ns_ready
            mn_ready e_in e_ready p1_ready pt_done pt_ready ov_done o_ready t7_done oT_ready
            pr_done h3_ready h3b_ready xh6_ready t8_done fT_ready in_done sil_ready hsw_ready sh_done
            ex_done g2_done cb_ready cn_done cn_ready fin_ready dve_step act_step pool_step st_out
            ot_done ot_ready zero_ready ln_stats ln_rstd rank_done slot_ready xs_zero sc_in xs_in0 xs_in1
            wc_ready ys_out gate_sig drv_ready drv_act selr_ready c2_ready gs_ready wex_in""".split()
        s = {n: sem(n) for n in names}
        emb_in = [sem(f"emb_in{c}") for c in range(CHUNKS)]
        block = ctx.enter_context(nc.Block())

        def vc(n):
            return vec[:, VI[n]:VI[n] + 1]

        def rowv(n):
            a, b = RO[n]
            return row[:, a:b]

        def rows_over(n, k):
            a, b = RO[n]
            return row[:, a:b].unsqueeze(1).to_broadcast([P, k, b - a])

        def ch(c):
            return slice(c * CT, (c + 1) * CT)

        def tl(c):
            return slice(c * TPC, (c + 1) * TPC)

        def bt4(b):
            return B[b].rearrange("p (t d) -> p t d", d=D)

        hT = S[1]

        def ytile(j, n=1):
            return S[5 + j // TILES][:, (j % TILES) * D:(j % TILES + n) * D]

        def xT(j):
            return PB[:, j * P:(j + 1) * P]

        def hid(j):
            k = XT + 1 + (j % 2) * FC
            return PB[:, k * P:(k + FC) * P]

        def wexp(j):
            k, half = j % WSLOTS // 2, j % 2
            home = X[:, :, :].rearrange("p t d -> p (t d)") if k == 0 else S[4]
            return home[:, half * 2 * FF:(half + 1) * 2 * FF]

        @block.sync
        def _(sp):
            sp.dma_start(idx[:, :], A["idx"]).then_inc(s["w_idx"], 16)
            sp.dma_start(row[:, :], A["rows"].to_broadcast([P, NR])).then_inc(s["w_rows"], 16)
            sp.dma_start(S[6][:, 0:T], A["pe"]).then_inc(s["w_pe"], 16)
            sp.dma_start(vec[:, :], A["vec"]).then_inc(s["w_vec"], 16)
            sp.dma_start(ID[:, :], A["ident"]).then_inc(s["w_misc"], 16)
            sp.dma_start(SELO[:, :], A["selo"]).then_inc(s["w_misc"], 16)
            sp.dma_start(bckc[:, :], A["bckc"]).then_inc(s["w_misc"], 16)
            sp.dma_start(kone[:, :], A["kone"]).then_inc(s["w_misc"], 16)
            sp.dma_start(wr, A["w_rwkv"]).then_inc(s["w_rwkv"], 16)
            sp.dma_start(PB[:, 0:T], A["sel"]).then_inc(s["w_sel"], 16)
            sp.dma_start(wck, A["w_ck"]).then_inc(s["w_ck"], 16)
            sp.dma_start(wcv[:, :, :], A["w_cv"]).then_inc(s["w_ck"], 16)
            sp.dma_start(wf[:, :], A["w_ffn"]).then_inc(s["w_ffn"], 16)
            sp.dma_start(wof[:, :], A["w_of"]).then_inc(s["w_ffn"], 16)
            sp.dma_start(wl[:, :], A["w_l1"]).then_inc(s["w_l1"], 16)
            sp.dma_start(win[:, :, :], A["w_in"]).then_inc(s["w_d"], 16)
            sp.dma_start(wso[:, :, :], A["w_so"]).then_inc(s["w_d"], 16)
            sp.dma_start(wg1[:, :], A["w_g1"]).then_inc(s["w_d"], 16)
            sp.dma_start(eob[:, :], A["eob"]).then_inc(s["w_d"], 16)
            sp.dma_start(b1c[:, :], A["b1c"]).then_inc(s["w_d"], 16)
            sp.dma_start(b2r[:, :], A["b2r"]).then_inc(s["w_d"], 16)
            sp.dma_start(gat[:, :], A["gat"]).then_inc(s["w_gat"], 16)
            sp.dma_start(tri[:, :], A["tri"]).then_inc(s["w_d"], 16)
            sp.dma_start(xs, A["zrow"].to_broadcast([XS, D])).then_inc(s["xs_zero"], 16)
            sp.wait_ge(s["z_ready"], CHUNKS)
            for half in range(2):
                sp.dma_start(BT[half * WS:(half + 1) * WS, :, :], A["lb"]).then_inc(s["w_lb"], 16)
            sp.wait_ge(s["ksel_done"], PAIRS * CHUNKS)
            sp.wait_ge(s["vals_ready"], CHUNKS)
            sp.dma_start(SS[:, 0:E0 * FF], A["moe_w1"]).then_inc(s["w_moe"], 16)
            sp.dma_start(SS[:, 2 * SW:2 * SW + E0 * FF], A["moe_w2"]).then_inc(s["w_moe"], 16)
            xsv, ysv = xs.rearrange("(j p) d -> p j d", p=P), ys.rearrange("(j p) d -> p j d", p=P)
            sp.wait_ge(s["sc_in"], 16 * TILES)
            sp.dma_start(V[:, 0:8 * D].rearrange("p (j d) -> p j d", d=D), xsv[:, 0:8, :]).then_inc(s["xs_in0"], 16)
            sp.dma_start(V[:, 8 * D:XT * D].rearrange("p (j d) -> p j d", d=D), xsv[:, 8:XT, :]).then_inc(s["xs_in1"], 16)
            for j in range(0, XT, 2):
                n = min(2, XT - j)
                sp.wait_ge(s["acc_ready"], j + n)
                sp.dma_start(ysv[:, j:j + n, :], ytile(j, n).rearrange("p (j d) -> p j d", d=D)).then_inc(s["ys_out"], 16)
            sp.wait_ge(s["h2_ready"], CHUNKS)
            for g in range(2):
                sp.dma_start(S[2 + g][:, 0:T], A["gp"][g, :, :]).then_inc(s["w_gp"], 16)
            sp.wait_ge(s["ov_done"], CHUNKS)
            sp.dma_start(V[:, 0:2 * E1 * D], A["w_ex"]).then_inc(s["wex_in"], 16)
            for c in range(CHUNKS):
                sp.wait_ge(s["fin_ready"], c + 1)
                sp.dma_start(out[:, tl(c), :], H[:, tl(c), :]).then_inc(s["st_out"], 16)
            sp.wait_ge(s["st_out"], 16 * CHUNKS)

        @block.gpsimd
        def _(pool):
            n = [0]

            def step(ins):
                n[0] += 1
                ins.then_inc(s["pool_step"], 1)
                pool.wait_ge(s["pool_step"], n[0])

            pool.wait_ge(s["w_idx"], 16)
            for t in range(TILES):
                pool.indirect_dma_start(H[:, t, :], None, A["emb"],
                                        bass.IndirectOffsetOnAxis(ap=idx[:, t:t + 1], axis=0)).then_inc(emb_in[t // TPC], 16)
            step(pool.memset(nh[:, :], -0.5))
            pool.wait_ge(s["w_rows"], 16)
            pool.wait_ge(s["w_pe"], 16)
            step(pool.tensor_tensor(tokv(6), tokv(6), rows_over("tokb", TILES), ALU.add))
            for c in range(CHUNKS):
                pool.wait_ge(emb_in[c], 16 * TPC)
                pool.tensor_tensor(H[:, tl(c), :], H[:, tl(c), :], tokv(6)[:, tl(c), :], ALU.add).then_inc(s["h_ready"], 1)

            def rstd(k, c, double=False):
                pool.wait_ge(s["ln_stats"], CHUNKS * k + c + 1)
                ve, ra, var = VE[:, tl(c)], RA[k][:, tl(c)], MV[k][:, tl(c), 1]
                step(pool.tensor_scalar(ve, var, EPS, None, ALU.add))
                if not double:
                    pool.tensor_tensor(ra, ve, nh[:, 0:TPC], ALU.pow).then_inc(s["ln_rstd"], 1)
                    return
                step(pool.tensor_tensor(ra, ve, nh[:, 0:TPC], ALU.pow))
                step(pool.tensor_tensor(ve, ra, ra, ALU.mult))
                step(pool.tensor_tensor(ve, ve, var, ALU.mult))
                step(pool.tensor_scalar(ve, ve, EPS, None, ALU.add))
                if k == 0:
                    pool.tensor_tensor(RB[:, tl(c)], ve, nh[:, 0:TPC], ALU.pow).then_inc(s["ln_rstd"], 1)
                    return
                step(pool.tensor_tensor(RB[:, tl(c)], ve, nh[:, 0:TPC], ALU.pow))
                pool.tensor_tensor(RB[:, tl(c)], RB[:, tl(c)], ra, ALU.mult).then_inc(s["ln_rstd"], 1)

            for c in range(CHUNKS):
                rstd(0, c, True)
            step(pool.tensor_scalar(rowv("bo"), rowv("bo"), 0.5, None, ALU.mult))
            for c in range(CHUNKS):
                pool.wait_ge(s["xh_ready"], c + 1)
                pool.tensor_tensor(X[:, tl(c), :], X[:, tl(c), :], rows_over("bo", TPC), ALU.add).then_inc(s["x0b_ready"], 1)
            for c in range(CHUNKS):
                rstd(1, c)
            for c in range(CHUNKS):
                rstd(2, c)
            for c in range(CHUNKS):
                pool.wait_ge(s["xh3_ready"], c + 1)
                pool.wait_ge(s["t4_done"], c + 1)
                pool.tensor_tensor(X[:, tl(c), :], X[:, tl(c), :], rows_over("bof", TPC), ALU.add).then_inc(s["xb_ready"], 1)
            for c in range(CHUNKS):
                rstd(3, c)
            pool.wait_ge(s["xs_zero"], 16)
            pool.wait_ge(s["slot_ready"], 1)
            for t in range(TILES):
                pool.indirect_dma_start(xs, bass.IndirectOffsetOnAxis(ap=slot[:, t:t + 1], axis=0), X[:, t, :],
                                        None).then_inc(s["sc_in"], 16)
            pool.wait_ge(s["ys_out"], 16 * ((XT + 1) // 2))
            for c in range(CHUNKS):
                for t in range(c * TPC, (c + 1) * TPC):
                    pool.indirect_dma_start(V[:, t * D:(t + 1) * D], None, ys,
                                            bass.IndirectOffsetOnAxis(ap=slot[:, t:t + 1], axis=0)).then_inc(emb_in[c], 16)
                if c >= 1:
                    rstd(4, c - 1)
            rstd(4, CHUNKS - 1)
            for c in range(CHUNKS):
                pool.wait_ge(s["xh5_ready"], c + 1)
                pool.tensor_tensor(H[:, tl(c), :], H[:, tl(c), :], rows_over("bout", TPC), ALU.add).then_inc(s["h3b_ready"], 1)
            for c in range(CHUNKS):
                pool.wait_ge(s["mn_ready"], c + 1)
                if c >= 2:
                    pool.wait_ge(s["t7_done"], c - 1)
                pool.tensor_tensor(sco(4 + 2 * (c % 2)), sco(2 + c % 2),
                                   mn[:, :].unsqueeze(2).to_broadcast([P, 32, WS]), ALU.subtract).then_inc(s["e_in"], 1)
            for c in range(CHUNKS):
                rstd(5, c, True)

        G = PB[:, :].rearrange("p (k f t) -> p k f t", k=2, f=FC)

        def prob(m):
            k = m % PSLOTS
            home = PB[:, k * 2 * CT:(k + 1) * 2 * CT] if k < 4 else S[k + 1][:, 2 * CT:4 * CT]
            return home.rearrange("p (h q) -> p h q", h=2)

        def val(c):
            return V[:, :].rearrange("p (t h d) -> p t h d", h=HEADS, d=32)[:, tl(c), :, :]

        def valh(k, h):
            return V[:, (k * HEADS + h) * 32:(k * HEADS + h + 1) * 32]

        def vwin(c, k):
            return V[:, :].rearrange("p (c k t h d) -> p c k t h d", c=2, k=2, h=HEADS, d=32)[:, c % 2, k, :, :, :]

        def sco2(i):
            return S[i][:, 0:T]

        @block.scalar
        def _(act):
            n = [0]

            def step(ins):
                n[0] += 1
                ins.then_inc(s["act_step"], 1)
                act.wait_ge(s["act_step"], n[0])

            act.wait_ge(s["w_vec"], 16)
            act.wait_ge(s["w_gat"], 16)
            act.activation(drv[:, 0:1], vc("decay"), ACT.Sigmoid).then_inc(s["act_step"], 1)
            act.activation(gat[:, :], gat[:, :], ACT.Sigmoid).then_inc(s["gate_sig"], 1)
            act.activation(drv[:, 1:2], vc("first"), ACT.Tanh).then_inc(s["drv_act"], 1)
            n[0] = 1
            act.wait_ge(s["drv_ready"], 1)
            for c in range(CHUNKS):
                act.wait_ge(s["t1_done"], c + 1)
                act.activation(hT[:, 1 + c * CT:1 + (c + 1) * CT], B[c], ACT.Identity, bias=vc("b1"),
                               scale=vc("g1")).then_inc(s["hT_ready"], 1)
            for c in range(CHUNKS):
                act.wait_ge(s["k_done"], c + 1)
                act.activation(S[5][:, ch(c)], B[4 + c % 2], ACT.Sigmoid, bias=drv[:, 2:3]).then_inc(s["gate_ready"], 1)
                act.wait_ge(s["v_done"], c + 1)
                act.activation(S[3][:, ch(c)], B[6 + c % 2], ACT.Identity, bias=vc("bv")).then_inc(s["vv_ready"], 1)
                act.activation(S[2][:, ch(c)], B[6 + c % 2], ACT.Identity, bias=drv[:, 4:5],
                               scale=drv[:, 3:4]).then_inc(s["wv_ready"], 1)
                act.wait_ge(s["r_done"], c + 1)
                act.activation(S[4][:, ch(c)], B[c], ACT.Tanh, bias=vc("br")).then_inc(s["tr_ready"], 1)
            for c in range(CHUNKS):
                act.wait_ge(s["t2_done"], c + 1)
                act.activation(hT[:, 1 + c * CT:1 + (c + 1) * CT], B[4 + c], ACT.Identity, bias=vc("b2"),
                               scale=vc("g2")).then_inc(s["h2T_ready"], 1)
            for c in range(CHUNKS):
                for f in range(FC):
                    act.wait_ge(s["ck_done"], FC * c + f + 1)
                    if c >= 2:
                        act.wait_ge(s["vv2_done"], c - 1)
                    act.activation(G[:, c % 2, f, :], B[4 + f], ACT.Gelu, bias=bckc[:, f:f + 1]).then_inc(s["gelu_ready"], 1)
                act.wait_ge(s["cr_done"], c + 1)
                act.activation(S[2][:, ch(c)], B[c], ACT.Tanh, bias=vc("bcr")).then_inc(s["tc_ready"], 1)
            for c in range(CHUNKS):
                act.wait_ge(s["t4_done"], c + 1)
                act.activation(S[0][:, ch(c)], B[c], ACT.Copy).then_inc(s["x1T_ready"], 1)
            for c in range(CHUNKS):
                act.wait_ge(s["q_done"], c + 1)
                act.activation(QHI[:, ch(c)], B[4], ACT.Identity, bias=vc("bq")).then_inc(s["qhi_ready"], 1)
                act.wait_ge(s["kk_done"], c + 1)
                if c >= 2:
                    act.wait_ge(s["ksel_done"], PAIRS * (c - 1))
                act.activation(KHI[:, c % 2, :], B[5], ACT.Identity, bias=vc("bkf")).then_inc(s["khi_ready"], 1)
                for j in range(PAIRS):
                    act.wait_ge(s["ksel_done"], PAIRS * c + j + 1)
                    act.activation(KST[:, j, ch(c)], B[6 + j % 2], ACT.Identity, bias=kone[:, 0:1]).then_inc(s["kst_ready"], 1)

            def filled(dst, done):
                act.activation(dst[0:64, 0, :], B[7][0:64, :], ACT.Copy)
                act.activation(dst[64:128, 1, :], B[7][64:128, :], ACT.Copy).then_inc(done, 1)

            def weighed(u):
                act.wait_ge(s["av_done"], 8 * (u + 1))
                if u >= 1:
                    act.wait_ge(s["dsum_done"], u)
                act.activation(S[5][:, 0:CT], B[6], ACT.Copy).then_inc(s["xev_ready"], 1)

            def attended(q):
                act.wait_ge(s["ot_done"], q + 1)
                act.activation(S[5][:, CT:2 * CT], B[7], ACT.Copy).then_inc(s["ot_ready"], 1)

            act.wait_ge(s["qsel_done"], 1)
            filled(QM[0], s["qm_ready"])
            act.wait_ge(s["qe_done"], 1)
            filled(QE[0], s["qe_ready"])
            act.wait_ge(s["qsel_done"], 2)
            filled(QM[1], s["qm_ready"])
            for u in range(UNITS):
                for k in range(TILES):
                    m = u * TILES + k
                    if m >= PSLOTS:
                        act.wait_ge(s["av_done"], (m - PSLOTS) // 2 + 1)
                    for h in range(2):
                        act.wait_ge(s["st_done"], 2 * m + h + 1)
                        act.activation(prob(m)[:, h, :], B[3 + (2 * m + h) % 3], ACT.Exp, scale=HD ** -0.5).then_inc(s["p_ready"], 1)
                    if k == 1 and u >= 1:
                        weighed(u - 1)
                    if k == 5 and u >= 1 and u % PAIRS == 0:
                        attended(u // PAIRS - 1)
                    if k == 9 and u + 2 < UNITS:
                        act.wait_ge(s["qsel_done"], u + 3)
                        filled(QM[u % 2], s["qm_ready"])
                    if k == 13 and u + 1 < UNITS:
                        act.wait_ge(s["qe_done"], u + 2)
                        filled(QE[(u + 1) % 2], s["qe_ready"])
            weighed(UNITS - 1)
            attended(CHUNKS - 1)

            for c in range(CHUNKS):
                act.wait_ge(s["t5_done"], c + 1)
                act.activation(S[5][:, ch(c)], B[c], ACT.Identity, bias=vc("bf"), scale=vc("gf")).then_inc(s["tT_ready"], 1)
            act.wait_ge(s["gs_ready"], 1)
            act.activation(gt[1][:, :, :], gt[0][:, :, :], ACT.Exp).then_inc(s["gs_ready"], 1)
            act.wait_ge(s["cT_done"], 1)
            for k in range(4):
                ins = act.activation(cT[:, ch(k)], B[k][0:E0, :], ACT.Copy)
            ins.then_inc(s["cT_ready"], 1)
            for g in range((XT + 3) // 4):
                n = min(4, XT - 4 * g)
                act.wait_ge(s["t5_done"], CHUNKS + g + 1)
                act.activation(PB[:, 4 * g * P:(4 * g + n) * P], B[6 + g % 2][:, 0:n * P], ACT.Identity, bias=vc("bf"),
                               scale=vc("gf")).then_inc(s["tT_ready"], 1)
                for j in range(4 * g, 4 * g + n):
                    act.wait_ge(s["w1_done"], j + 1)
                    if j >= 2:
                        act.wait_ge(s["w2_done"], j - 1)
                    for f in range(FC):
                        act.activation(hid(j)[:, f * P:(f + 1) * P], B[4 + j % 2][:, f * P:(f + 1) * P],
                                       ACT.Gelu_apprx_tanh, bias=b1w[:, j % WSLOTS, f:f + 1]).then_inc(s["hid_ready"], 1)
                    if j >= 1:
                        act.wait_ge(s["w2_done"], j)
                        act.activation(ytile(j - 1), B[(j - 1) % 2][:, 0:D], ACT.Copy).then_inc(s["acc_ready"], 1)
            act.wait_ge(s["w2_done"], XT)
            act.activation(ytile(XT - 1), B[(XT - 1) % 2][:, 0:D], ACT.Copy).then_inc(s["acc_ready"], 1)

            for c in range(CHUNKS):
                act.wait_ge(s["t6_done"], c + 1)
                act.activation(S[5][:, ch(c)], B[c], ACT.Copy).then_inc(s["x2T_ready"], 1)

            def qkv_out(c):
                for k in range(4):
                    act.wait_ge(s["qk_done"], 4 * c + k + 1)
                    act.activation(S[c % 2][:, k * CT:(k + 1) * CT], B[4 + k % 2], ACT.Copy).then_inc(s["qk_ready"], 1)
                for k in range(2):
                    act.wait_ge(s["v1_done"], 2 * c + k + 1)
                    act.activation(vwin(c, k)[:, :, :, 0:HD], B[4 + k].rearrange("p (t h d) -> p t h d", t=TPC, d=HD),
                                   ACT.Copy).then_inc(s["v1_ready"], 1)

            def exp_out(c):
                act.wait_ge(s["e_in"], c + 1)
                act.activation(sco(4 + 2 * (c % 2)), sco(4 + 2 * (c % 2)), ACT.Exp, scale=-1.0).then_inc(s["e_ready"], 1)

            qkv_out(0)
            qkv_out(1)
            exp_out(0)
            for c in range(CHUNKS):
                for k in range(4):
                    act.wait_ge(s["pt_done"], 4 * c + k + 1)
                    act.activation(PB[:, (c % 2) * T + k * CT:(c % 2) * T + (k + 1) * CT], B[4 + k % 2],
                                   ACT.Copy).then_inc(s["pt_ready"], 1)
                if c + 2 < CHUNKS:
                    qkv_out(c + 2)
                if c + 1 < CHUNKS:
                    exp_out(c + 1)
                act.wait_ge(s["t7_done"], c + 1)
                act.activation(S[5][:, ch(c)], B[4], ACT.Copy).then_inc(s["oT_ready"], 1)

            for c in range(CHUNKS):
                act.wait_ge(s["t8_done"], c + 1)
                act.activation(S[5][:, ch(c)], B[c], ACT.Identity, bias=vc("lb"), scale=vc("ls")).then_inc(s["fT_ready"], 1)
            act.wait_ge(s["gs_ready"], 3)
            act.activation(gt[1][:, :, 0:EG], gt[0][:, :, 0:EG], ACT.Exp).then_inc(s["gs_ready"], 1)
            act.wait_ge(s["cn_done"], 1)
            for k in range(4):
                ins = act.activation(cT[:, ch(k)], B[k][0:E1, :], ACT.Copy)
            ins.then_inc(s["cn_ready"], 1)
            for c in range(CHUNKS):
                for k in range(4):
                    act.wait_ge(s["in_done"], 4 * c + k + 1)
                    if c >= 2:
                        act.wait_ge(s["ex_done"], TPC * (c - 1))
                    act.activation(S[c % 2][:, k * CT:(k + 1) * CT], B[2 * (k % 2)], ACT.Silu).then_inc(s["sil_ready"], 1)

        @block.vector
        def _(dve):
            n = [0]

            def did(ins):
                n[0] += 1
                ins.then_inc(s["dve_step"], 1)
                return n[0]

            def settle(back=0):
                dve.wait_ge(s["dve_step"], n[0] - back)

            def step(ins):
                did(ins)
                settle()

            step(dve.memset(V[:, :], 1.0))
            step(dve.memset(S[1][:, 0:1], 0.0))
            step(dve.memset(S[6][:, T:T + 1], 0.0))
            step(dve.memset(DEC[:, :], 0.0))
            step(dve.memset(AM[:, :, :].bitcast(f32), 0.0))
            dve.wait_ge(s["w_vec"], 16)
            a, b = VI["mk"], VI["cr"] + 1
            step(dve.tensor_scalar(vec[:, a:b], vec[:, a:b], 0.0, 1.0, ALU.max, ALU.min))
            dve.wait_ge(s["drv_act"], 1)
            step(dve.tensor_scalar(drv[:, 2:3], vc("bk"), drv[:, 1:2], None, ALU.add))
            step(dve.tensor_scalar(drv[:, 3:4], drv[:, 0:1], -1.0, 1.0, ALU.mult, ALU.add))
            step(dve.tensor_scalar(DEC[:, :], DEC[:, :], drv[:, 0:1], None, ALU.add))
            dve.tensor_scalar(drv[:, 4:5], vc("bv"), drv[:, 3:4], None, ALU.mult).then_inc(s["drv_ready"], 1)

            def stats(k, c, src):
                for t in range(c * TPC, (c + 1) * TPC):
                    did(dve.bn_stats(st6[:, t, :], src[:, t, :]))
                settle()
                for t in range(c * TPC, (c + 1) * TPC):
                    ins = dve.bn_aggr(MV[k][:, t, :], st6[:, t, :])
                ins.then_inc(s["ln_stats"], 1)

            def normed(k, c, dst, src, r, sem_=None):
                for t in range(c * TPC, (c + 1) * TPC):
                    ins = dve.tensor_scalar(dst[:, t, :], src[:, t, :], MV[k][:, t, 0:1], r[:, t:t + 1],
                                            ALU.subtract, ALU.mult)
                    if sem_ and t == (c + 1) * TPC - 1:
                        ins.then_inc(sem_, 1)
                    else:
                        did(ins)

            for c in range(CHUNKS):
                dve.wait_ge(s["h_ready"], c + 1)
                stats(0, c, H)
            dve.wait_ge(s["w_sel"], 16)
            step(dve.tensor_copy(SELR[:, 0:8, :], PB[:, 0:1024].rearrange("p (a b) -> p a b", b=P)))
            dve.wait_ge(s["w_misc"], 64)
            dve.wait_ge(s["w_sel"], 16)
            step(dve.tensor_copy(SELR[:, 8:16, :], PB[:, 1024:2048].rearrange("p (a b) -> p a b", b=P)))
            dve.tensor_copy(IDR[:, :], ID[:, :]).then_inc(s["selr_ready"], 1)
            for c in range(CHUNKS):
                dve.wait_ge(s["ln_rstd"], c + 1)
                normed(0, c, X, H, RA[0])
                settle()
                dve.tensor_tensor(tokv(0)[:, tl(c), :], X[:, tl(c), :], RB[:, tl(c)].unsqueeze(2).to_broadcast([P, TPC, D]),
                                  ALU.mult).then_inc(s["xh_ready"], 1)
            for c in range(CHUNKS):
                dve.wait_ge(s["hT_ready"], c + 1)
                now, before = hT[:, 1 + c * CT:1 + (c + 1) * CT], hT[:, ch(c)]
                step(dve.tensor_tensor(S[0][:, ch(c)], now, before, ALU.subtract))
                for i, m in ((2, "mk"), (3, "mv"), (4, "mr")):
                    ins = dve.scalar_tensor_tensor(S[i][:, ch(c)], S[0][:, ch(c)], vc(m), before, ALU.mult, ALU.add)
                    if i < 4:
                        did(ins)
                ins.then_inc(s["mix_ready"], 1)
            dve.wait_ge(s["h_ready"], CHUNKS)
            step(dve.memset(S[6][:, 0:1], 0.0))
            for c in range(CHUNKS):
                dve.wait_ge(s["wv_ready"], c + 1)
                step(dve.tensor_tensor_scan(S[6][:, 1 + c * CT:1 + (c + 1) * CT], DEC[:, :], S[2][:, ch(c)],
                                            S[6][:, c * CT:c * CT + 1], ALU.mult, ALU.add))
                v = S[3][:, ch(c)]
                step(dve.tensor_tensor(v, v, S[6][:, ch(c)], ALU.subtract))
                step(dve.tensor_tensor(v, v, S[5][:, ch(c)], ALU.mult))
                step(dve.tensor_tensor(v, v, S[6][:, ch(c)], ALU.add))
                dve.wait_ge(s["tr_ready"], c + 1)
                dve.tensor_tensor(S[0][:, ch(c)], v, S[4][:, ch(c)], ALU.mult).then_inc(s["z_ready"], 1)
            for c in range(CHUNKS):
                dve.wait_ge(s["woo_done"], c + 1)
                dve.wait_ge(s["x0b_ready"], c + 1)
                dve.scalar_tensor_tensor(X[:, tl(c), :], bt4(c), 0.5, X[:, tl(c), :], ALU.mult, ALU.add).then_inc(s["x1_ready"], 1)
                dve.wait_ge(s["x1_ready"], c + 1)
                stats(1, c, X)
            for c in range(CHUNKS):
                dve.wait_ge(s["ln_rstd"], 1 * CHUNKS + c + 1)
                normed(1, c, tokv(5), X, RA[1], s["xh2_ready"])
            for c in range(CHUNKS):
                dve.wait_ge(s["h2T_ready"], c + 1)
                now, before = hT[:, 1 + c * CT:1 + (c + 1) * CT], hT[:, ch(c)]
                step(dve.tensor_tensor(S[0][:, ch(c)], now, before, ALU.subtract))
                did(dve.scalar_tensor_tensor(S[4][:, ch(c)], S[0][:, ch(c)], vc("cr"), before, ALU.mult, ALU.add))
                dve.scalar_tensor_tensor(S[3][:, ch(c)], S[0][:, ch(c)], vc("ck"), before, ALU.mult,
                                         ALU.add).then_inc(s["mix2_ready"], 1)
            for c in range(CHUNKS):
                dve.wait_ge(s["vv2_done"], c + 1)
                dve.wait_ge(s["tc_ready"], c + 1)
                dve.scalar_tensor_tensor(S[6][:, ch(c)], B[c], vc("bcv"), S[2][:, ch(c)], ALU.add,
                                         ALU.mult).then_inc(s["q_ready"], 1)
            for c in range(CHUNKS):
                dve.wait_ge(s["t3_done"], c + 1)
                step(dve.scalar_tensor_tensor(X[:, tl(c), :], bt4(4 + c), 0.5, X[:, tl(c), :], ALU.mult, ALU.add))
                dve.tensor_tensor(H[:, tl(c), :], H[:, tl(c), :], X[:, tl(c), :], ALU.add).then_inc(s["h1_ready"], 1)
                dve.wait_ge(s["h1_ready"], c + 1)
                stats(2, c, H)
            for c in range(CHUNKS):
                dve.wait_ge(s["ln_rstd"], 2 * CHUNKS + c + 1)
                normed(2, c, X, H, RA[2], s["xh3_ready"])
            for c in range(CHUNKS):
                dve.wait_ge(s["qhi_ready"], c + 1)
                dve.scalar_tensor_tensor(QLO[:, ch(c)], B[4], vc("bq"), QHI[:, ch(c)].bitcast(f32), ALU.add,
                                         ALU.subtract).then_inc(s["qlo_ready"], 1)
                dve.wait_ge(s["khi_ready"], c + 1)
                dve.scalar_tensor_tensor(KLO[:, c % 2, :], B[5], vc("bkf"), KHI[:, c % 2, :].bitcast(f32), ALU.add,
                                         ALU.subtract).then_inc(s["klo_ready"], 1)
                dve.wait_ge(s["vt_done"], c + 1)
                dve.tensor_tensor(val(c)[:, :, :, 0:HD], B[c].rearrange("p (t h d) -> p t h d", t=TPC, d=HD),
                                  rowv("bvf").rearrange("p (h d) -> p h d", d=HD).unsqueeze(1).to_broadcast([P, TPC, HEADS, HD]),
                                  ALU.add).then_inc(s["vals_ready"], 1)

            dve.wait_ge(s["ksel_done"], CHUNKS * PAIRS)
            for stack in (QM[0], QM[1], QE[0], QE[1]):
                did(dve.memset(stack[64:128, 0, :].bitcast(f32), 0.0))
                did(dve.memset(stack[0:64, 1, :].bitcast(f32), 0.0))
            settle()
            dve.memset(nm[:, :], 0.0).then_inc(s["zero_ready"], 1)
            dve.wait_ge(s["zero_ready"], 1)
            ON = tokv(6)

            def maxes(u, a, b):
                for i in range(a, b):
                    for h in range(2):
                        m = u * 32 + 2 * i + h
                        dve.wait_ge(s["mxp_done"], m + 1)
                        dve.tensor_reduce(mq[:, 2 * (i // 4) + h, i % 4:i % 4 + 1], B[m % 3], AX.X,
                                          ALU.max).then_inc(s["mxr_done"], 1)

            def negated(u):
                dve.wait_ge(s["mxr_done"], 32 * (u + 1))
                step(dve.tensor_reduce(nm[:, :], mq[:, :, :], AX.X, ALU.max, negate=True))
                if u >= 1:
                    dve.wait_ge(s["qe_done"], u)
                nmv = nm[:, :].rearrange("p (t h) -> p t h", h=2)
                step(dve.tensor_copy(AM[:, :, 48::64], nmv))
                dve.tensor_tensor(AM[:, :, 49::64], nmv, AM[:, :, 48::64].bitcast(f32), ALU.subtract).then_inc(s["nm_ready"], 1)

            def normalize(u):
                dve.wait_ge(s["dsum_done"], u + 1)
                o = B[7][:, 0:TPC * 2 * (HD + 1)].rearrange("p (t h e) -> p t h e", t=TPC, h=2)
                den = oden[:, 0, 0:2 * TPC].rearrange("p (t h) -> p t h", h=2)
                step(dve.reciprocal(den, o[:, :, :, HD]))
                j = u % PAIRS
                dve.tensor_tensor(ON[:, 0:TPC, 2 * j * HD:2 * (j + 1) * HD].rearrange("p t (h d) -> p t h d", h=2),
                                  o[:, :, :, 0:HD], den.unsqueeze(3).to_broadcast([P, TPC, 2, HD]),
                                  ALU.mult).then_inc(s["on_ready"], 1)

            def projected(q):
                dve.wait_ge(s["wo_done"], q + 1)
                dve.wait_ge(s["xb_ready"], q + 1)
                dve.tensor_tensor(tokv(4)[:, tl(q), :], bt4(7), X[:, tl(q), :], ALU.add).then_inc(s["y_ready"], 1)

            maxes(0, 0, 16)
            negated(0)
            maxes(1, 0, AHEAD)
            for u in range(UNITS):
                more = u + 1 < UNITS
                if more:
                    maxes(u + 1, AHEAD, AHEAD + 3)
                if u >= 1:
                    normalize(u - 1)
                if more:
                    maxes(u + 1, AHEAD + 3, AHEAD + 8)
                if u >= 1 and u % PAIRS == 0:
                    projected(u // PAIRS - 1)
                if more:
                    maxes(u + 1, AHEAD + 8, 16)
                    negated(u + 1)
                if u + 2 < UNITS:
                    maxes(u + 2, 0, AHEAD)
            normalize(UNITS - 1)
            projected(CHUNKS - 1)

            for c in range(CHUNKS):
                dve.wait_ge(s["y_ready"], c + 1)
                stats(3, c, tokv(4))
            for c in range(CHUNKS):
                dve.wait_ge(s["ln_rstd"], 3 * CHUNKS + c + 1)
                normed(3, c, X, tokv(4), RA[3], s["xh4_ready"])

            def over(x, k):
                return x.unsqueeze(2).to_broadcast([P, TILES, k])

            def prio(k):
                a0, _ = RO["prio"]
                return row[:, a0 + E0 - k:a0 + E0].unsqueeze(1).to_broadcast([P, TILES, k])

            def first_max(dst, src, mx, k, tmp):
                step(dve.tensor_reduce(mx, src, AX.X, ALU.max))
                step(dve.tensor_tensor(tmp, src, over(mx, k), ALU.is_equal))
                step(dve.tensor_tensor(tmp, tmp, prio(k), ALU.mult))
                step(dve.tensor_reduce(gs[:, 3, :], tmp, AX.X, ALU.max))
                step(dve.tensor_tensor(dst, tmp, over(gs[:, 3, :], k), ALU.is_equal))

            def softmaxed(src, k, ready, back):
                step(dve.tensor_reduce(gs[:, 0, :], src, AX.X, ALU.max))
                dve.tensor_tensor(gt[0][:, :, 0:k], src, over(gs[:, 0, :], k), ALU.subtract).then_inc(ready, 1)
                dve.wait_ge(ready, back)
                step(dve.tensor_reduce(gs[:, 1, :], gt[1][:, :, 0:k], AX.X, ALU.add))
                step(dve.reciprocal(gs[:, 1, :], gs[:, 1, :]))
                step(dve.tensor_tensor(gt[1][:, :, 0:k], gt[1][:, :, 0:k], over(gs[:, 1, :], k), ALU.mult))

            dve.wait_ge(s["gl_done"], 1)
            step(dve.tensor_tensor(gt[2][:, :, :], B[4][:, 0:TILES * E0].rearrange("p (t e) -> p t e", e=E0),
                                   rows_over("gateb", TILES), ALU.add))
            softmaxed(gt[2][:, :, :], E0, s["gs_ready"], 2)
            first_max(cw[:, :, :], gt[1][:, :, :], gs[:, 0, :], E0, gt[3][:, :, :])
            dve.tensor_copy(RA[3][:, :], gs[:, 0, :]).then_inc(s["cw_ready"], 1)
            dve.wait_ge(s["cw_ready"], 1)
            dve.tensor_tensor(gt[0][:, :, :], cw[:, :, :], over(gs[:, 0, :], E0), ALU.mult).then_inc(s["cw_ready"], 1)
            before = B[5][:, 0:TILES * E0].rearrange("p (t e) -> p t e", e=E0)
            count = B[5][:, TILES * E0:2 * TILES * E0].rearrange("p (t e) -> p t e", e=E0)
            dve.wait_ge(s["rank_done"], 1)
            step(dve.tensor_copy(gt[1][:, :, :], count))
            a, b = gt[1], gt[2]
            for k in (1, 2, 4, 8):
                did(dve.tensor_copy(b[:, 0:k, :], a[:, 0:k, :]))
                step(dve.tensor_tensor(b[:, k:TILES, :], a[:, k:TILES, :], a[:, 0:TILES - k, :], ALU.add))
                a, b = b, a
            total = a[:, TILES - 1, :]
            need, run, tmp = nm[:, 0:E0], mn[:, 0:E0], mn[:, E0:2 * E0]
            full = gt[3][:, :, :].rearrange("p t e -> p (t e)").rearrange("p (e k) -> p e k", k=TILES)
            step(dve.tensor_tensor(full, total.unsqueeze(2).to_broadcast([P, E0, TILES]),
                                   rowv("full").unsqueeze(1).to_broadcast([P, E0, TILES]), ALU.is_gt))
            step(dve.tensor_reduce(need, full, AX.X, ALU.add))
            step(dve.tensor_tensor(a[:, :, :], a[:, :, :], count, ALU.subtract))
            did(dve.tensor_tensor(a[:, :, :], a[:, :, :], before, ALU.add))
            step(dve.tensor_copy(run, need))
            for k in (1, 2, 4):
                did(dve.tensor_copy(tmp[:, 0:k], run[:, 0:k]))
                step(dve.tensor_tensor(tmp[:, k:E0], run[:, k:E0], run[:, 0:E0 - k], ALU.add))
                run, tmp = tmp, run
            step(dve.tensor_tensor(tmp, run, need, ALU.subtract))
            step(dve.tensor_scalar(tmp, tmp, float(P), None, ALU.mult))
            step(dve.tensor_tensor(a[:, :, :], a[:, :, :], tmp.unsqueeze(1).to_broadcast([P, TILES, E0]), ALU.add))
            step(dve.tensor_tensor(a[:, :, :], a[:, :, :], cw[:, :, :], ALU.mult))
            step(dve.tensor_reduce(gs[:, 1, :], a[:, :, :], AX.X, ALU.add))
            dve.tensor_copy(slot[:, :], gs[:, 1, :]).then_inc(s["slot_ready"], 1)
            ends = xm[:, 0:XT]
            past = S[6][:, 0:XT * E0].rearrange("p (j e) -> p j e", e=E0)
            step(dve.tensor_tensor(past, rowv("tileno").unsqueeze(2).to_broadcast([P, XT, E0]),
                                   run.unsqueeze(1).to_broadcast([P, XT, E0]), ALU.is_ge))
            step(dve.tensor_reduce(ends, past, AX.X, ALU.add))
            step(dve.tensor_scalar(ends, ends, float(E0 - 1), None, ALU.min))
            step(dve.tensor_copy(tex[:, :], ends))
            for c in range(CHUNKS):
                dve.wait_ge(s["acc0_done"], c + 1)
                dve.tensor_tensor(H[:, tl(c), :], H[:, tl(c), :], bt4(c), ALU.add).then_inc(s["acc0_ready"], 1)
            dve.wait_ge(s["w_moe"], 32)
            dve.wait_ge(s["sc_in"], 16 * TILES)
            for j in range(XT):
                e = dve.value_load(tex[0:1, j:j + 1], min_val=0, max_val=E0 - 1)
                if j >= WSLOTS:
                    dve.wait_ge(s["w2_done"], j - WSLOTS + 1)
                did(dve.tensor_copy(wexp(j)[:, 0:FF], SS[:, bass.ds(e * FF, FF)]))
                did(dve.tensor_copy(wexp(j)[:, FF:2 * FF], SS[:, bass.ds(e * FF + 2 * SW, FF)]))
                settle()
                dve.tensor_copy(b1w[:, j % WSLOTS, :], b1c[:, bass.ds(e * FC, FC)]).then_inc(s["wc_ready"], 1)
            for c in range(CHUNKS):
                dve.wait_ge(emb_in[c], 2 * 16 * TPC)
                dve.wait_ge(s["acc0_ready"], CHUNKS)
                for t in range(c * TPC, (c + 1) * TPC):
                    ins = dve.scalar_tensor_tensor(H[:, t, :], V[:, t * D:(t + 1) * D], RA[3][:, t:t + 1], H[:, t, :],
                                                   ALU.mult, ALU.add)
                    if t < (c + 1) * TPC - 1:
                        did(ins)
                ins.then_inc(s["h2_ready"], 1)
                dve.wait_ge(s["h2_ready"], c + 1)
                settle()
                stats(4, c, H)
            for c in range(CHUNKS):
                dve.wait_ge(s["ln_rstd"], 4 * CHUNKS + c + 1)
                normed(4, c, X, H, RA[4], s["xh5_ready"])

            did(dve.memset(V[:, :].rearrange("p (x d) -> p x d", d=32)[:, :, HD:HD + 1], 1.0))
            dve.wait_ge(s["w_gp"], 32)
            for g in range(2):
                did(dve.tensor_reduce(gpm[:, g, :], S[2 + g][:, 0:T].rearrange("p (g n) -> p n g", n=WS), AX.X, ALU.add))
            dve.wait_ge(s["x2T_ready"], CHUNKS)
            dve.tensor_reduce(xm[:, :], S[5][:, 0:T].rearrange("p (w n) -> p n w", n=WS), AX.X, ALU.add).then_inc(s["xm_ready"], 1)
            dve.wait_ge(s["gm_done"], 1)
            did(dve.tensor_scalar(qm[:, :, :], B[4][:, 0:2 * WS].rearrange("p (g n) -> p g n", g=2), WS / T, None, ALU.mult))
            did(dve.tensor_scalar(km[:, :, :], B[4][:, 2 * WS:4 * WS].rearrange("p (g n) -> p g n", g=2), WS / T, None, ALU.mult))
            step(dve.tensor_scalar(gpm[:, :, :], gpm[:, :, :], 1.0 / G1, None, ALU.mult))
            step(dve.tensor_tensor(qm[:, :, :], qm[:, :, :], gpm[:, :, :], ALU.mult))
            step(dve.tensor_reduce(gq[:, 0:2], qm[:, :, :], AX.X, ALU.add))
            dve.wait_ge(s["gate_sig"], 1)
            step(dve.scalar_tensor_tensor(gq[:, 2:4], gq[:, 0:2], D ** -0.5, gat[:, :], ALU.mult, ALU.mult))
            dve.tensor_copy(gqb[:, :, :], gq[:, 2:4].unsqueeze(2).to_broadcast([P, 2, P])).then_inc(s["gq_ready"], 1)
            dve.wait_ge(s["gb_done"], 1)
            btv = BT[:, :, :].rearrange("p h m -> p (h m)")
            dve.wait_ge(s["w_lb"], 32)
            for j in range(4):
                ins = dve.tensor_tensor(btv[:, j * P:(j + 1) * P], btv[:, j * P:(j + 1) * P], B[j][:, 0:P], ALU.add)
                if j < 3:
                    did(ins)
            ins.then_inc(s["bt_ready"], 1)
            dve.wait_ge(s["bt_ready"], 1)

            W = X[:, :, :].rearrange("p t d -> p (t d)").rearrange("p (r m) -> p r m", m=WS)

            def window_out(c):
                dve.wait_ge(s["ov_done"], c + 1)
                ob = tokv(4 + 2 * (c % 2))[:, 0:TPC, :].rearrange("p t (g j d) -> p t g j d", g=2, d=HD)
                for g in range(2):
                    o = B[6 + g].rearrange("p (t j e) -> p t j e", t=TPC, j=4)
                    den = oden[:, g, :].rearrange("p (t j) -> p t j", j=4)
                    step(dve.reciprocal(den, o[:, :, :, HD]))
                    ins = dve.tensor_tensor(ob[:, :, g, :, :], o[:, :, :, 0:HD],
                                            den.unsqueeze(3).to_broadcast([P, TPC, 4, HD]), ALU.mult)
                    if g == 0:
                        did(ins)
                ins.then_inc(s["o_ready"], 1)

            def residual3(c):
                dve.wait_ge(s["pr_done"], c + 1)
                dve.wait_ge(s["h3b_ready"], c + 1)
                dve.tensor_tensor(H[:, tl(c), :], H[:, tl(c), :], bt4(5), ALU.add).then_inc(s["h3_ready"], 1)
                dve.wait_ge(s["h3_ready"], c + 1)
                stats(5, c, H)

            for c in range(CHUNKS):
                ns, ex = sco(2 + c % 2), sco(4 + 2 * (c % 2))
                for j in range(4):
                    dve.wait_ge(s["s_done"], 4 * c + j + 1)
                    if c >= 2:
                        dve.wait_ge(s["e_in"], c - 1)
                    ins = dve.scalar_tensor_tensor(S[2 + c % 2][:, j * CT:(j + 1) * CT].rearrange("p (t x) -> p t x", t=TPC),
                                                   B[j].rearrange("p (t x) -> p t x", t=TPC), -(D ** -0.5),
                                                   btv[:, j * P:(j + 1) * P].unsqueeze(1).to_broadcast([P, TPC, P]),
                                                   ALU.mult, ALU.subtract)
                    ins.then_inc(s["ns_ready"], 1)
                dve.wait_ge(s["ns_ready"], 4 * (c + 1))
                if c >= 1:
                    dve.wait_ge(s["e_in"], c)
                dve.tensor_reduce(mn[:, :], ns, AX.X, ALU.min).then_inc(s["mn_ready"], 1)
                for r in range(32):
                    did(dve.max(t8[:, 0, r, :], ns[:, r, :]))
                for r in range(32):
                    settle(31)
                    did(dve.match_replace(W[:, r, :], t8[:, 0, r, :], ns[:, r, :], NEG))
                for r in range(32):
                    settle(31)
                    did(dve.max(t8[:, 1, r, :], W[:, r, :]))
                for r in range(32):
                    settle(31)
                    did(dve.match_replace(W[:, r, :], t8[:, 1, r, :], W[:, r, :], NEG))
                for r in range(32):
                    settle(31)
                    did(dve.max(t8[:, 2, r, :], W[:, r, :]))
                settle()
                if c >= 1:
                    window_out(c - 1)
                dve.wait_ge(s["e_in"], c + 1)
                step(dve.tensor_tensor(ns, ns, t8[:, 2, :, DROP - 16:DROP - 15].to_broadcast([P, 32, WS]), ALU.is_le))
                dve.wait_ge(s["e_ready"], c + 1)
                dve.tensor_tensor(ex, ex, ns, ALU.mult).then_inc(s["p1_ready"], 1)
                if c >= 1:
                    residual3(c - 1)
            window_out(CHUNKS - 1)
            residual3(CHUNKS - 1)

            for c in range(CHUNKS):
                dve.wait_ge(s["ln_rstd"], 5 * CHUNKS + c + 1)
                normed(5, c, X, H, RB, s["xh6_ready"])
            dve.wait_ge(s["g2_done"], 1)
            g2 = B[5][:, 0:TILES * (2 + E1)].rearrange("p (t e) -> p t e", e=2 + E1)
            step(dve.tensor_tensor(gt[2][:, :, 0:2], g2[:, :, 0:2], rows_over("gb", TILES), ALU.add))
            step(dve.tensor_tensor(gt[3][:, :, :], g2[:, :, 2:2 + E1], rows_over("eb", TILES), ALU.add))
            v = gs[:, 2, :]
            step(dve.tensor_tensor(v, gt[2][:, :, 1], gt[2][:, :, 0], ALU.is_gt))
            grp = gpick
            step(dve.tensor_copy(grp[:, :, 1], v))
            step(dve.tensor_scalar(grp[:, :, 0], v, -1.0, 1.0, ALU.mult, ALU.add))
            did(dve.tensor_tensor(gt[3][:, :, 0:EG], gt[3][:, :, 0:EG], over(grp[:, :, 0], EG), ALU.mult))
            step(dve.tensor_tensor(gt[3][:, :, EG:E1], gt[3][:, :, EG:E1], over(grp[:, :, 1], EG), ALU.mult))
            step(dve.tensor_tensor(gt[2][:, :, 0:EG], gt[3][:, :, 0:EG], gt[3][:, :, EG:E1], ALU.add))
            softmaxed(gt[2][:, :, 0:EG], EG, s["gs_ready"], 4)
            pr, o1, o2, tmp = gt[1][:, :, 0:EG], gt[2][:, :, 0:EG], gt[2][:, :, EG:E1], gt[3][:, :, 0:EG]
            first_max(o1, pr, gs[:, 0, :], EG, tmp)
            step(dve.scalar_tensor_tensor(pr, o1, -4.0, pr, ALU.mult, ALU.add))
            first_max(o2, pr, gs[:, 1, :], EG, tmp)
            step(dve.tensor_tensor(gs[:, 2, :], gs[:, 0, :], gs[:, 1, :], ALU.add))
            step(dve.tensor_scalar(gs[:, 2, :], gs[:, 2, :], 1e-8, None, ALU.add))
            step(dve.reciprocal(gs[:, 2, :], gs[:, 2, :]))
            did(dve.tensor_tensor(gs[:, 0, :], gs[:, 0, :], gs[:, 2, :], ALU.mult))
            step(dve.tensor_tensor(gs[:, 1, :], gs[:, 1, :], gs[:, 2, :], ALU.mult))
            did(dve.tensor_tensor(tmp, o1, over(gs[:, 0, :], EG), ALU.mult))
            did(dve.tensor_tensor(pr, o2, over(gs[:, 1, :], EG), ALU.mult))
            step(dve.tensor_tensor(o1, o1, o2, ALU.add))
            step(dve.tensor_tensor(tmp, tmp, pr, ALU.add))
            for g in range(2):
                did(dve.tensor_tensor(gt[0][:, :, g * EG:(g + 1) * EG], o1, over(grp[:, :, g], EG), ALU.mult))
                ins = dve.tensor_tensor(cw[:, :, g * EG:(g + 1) * EG], tmp, over(grp[:, :, g], EG), ALU.mult)
                if g == 0:
                    did(ins)
            ins.then_inc(s["c2_ready"], 1)
            dve.wait_ge(s["c2_ready"], 1)
            OA, OBB = tokv(2), tokv(3)
            for c in range(CHUNKS):
                for k in range(4):
                    dve.wait_ge(s["sil_ready"], 4 * c + k + 1)
                    sl = S[c % 2][:, k * CT:(k + 1) * CT]
                    dve.tensor_tensor(sl, sl, B[2 * (k % 2) + 1], ALU.mult).then_inc(s["hsw_ready"], 1)
                dve.wait_ge(s["sh_done"], c + 1)
                step(dve.tensor_tensor(H[:, tl(c), :], H[:, tl(c), :], rows_over("shb", TPC), ALU.add))
                dve.tensor_tensor(H[:, tl(c), :], H[:, tl(c), :], bt4(4), ALU.add).then_inc(s["xev_ready"], 1)
                dve.wait_ge(s["xev_ready"], UNITS + c + 1)
                for t in range(TPC):
                    g = c * TPC + t
                    dve.wait_ge(s["ex_done"], g + 1)
                    b0 = 6 if t % 2 == 0 else 2
                    for e in range(E1):
                        dst = (OA if e % 2 == 0 else OBB)[:, g, :]
                        src = PS[:, b0 + e // 4, (e % 4) * D:(e % 4 + 1) * D]
                        if e < 2:
                            did(dve.tensor_scalar(dst, src, cw[:, g, e:e + 1], None, ALU.mult))
                            continue
                        settle(1)
                        ins = dve.scalar_tensor_tensor(dst, src, cw[:, g, e:e + 1], dst, ALU.mult, ALU.add)
                        if e < E1 - 1:
                            did(ins)
                    ins.then_inc(s["cb_ready"], 1)
                    dve.wait_ge(s["cb_ready"], g + 1)
                step(dve.tensor_tensor(OA[:, tl(c), :], OA[:, tl(c), :], OBB[:, tl(c), :], ALU.add))
                dve.tensor_tensor(H[:, tl(c), :], H[:, tl(c), :], OA[:, tl(c), :], ALU.add).then_inc(s["fin_ready"], 1)

        @block.tensor
        def _(pe):
            def transposes(dst, src, done):
                for t in range(TPC):
                    ins = pe.transpose(dst[:, t * P:(t + 1) * P], src(t), ID[:, :])
                ins.then_inc(done, 1)

            def w(i):
                return wr[:, i * D:(i + 1) * D]

            pe.wait_ge(s["w_misc"], 64)
            for c in range(CHUNKS):
                pe.wait_ge(s["xh_ready"], c + 1)
                transposes(B[c], lambda t: tokv(0)[:, c * TPC + t, :], s["t1_done"])
            pe.wait_ge(s["w_rwkv"], 16)
            for c in range(CHUNKS):
                pe.wait_ge(s["mix_ready"], c + 1)
                if c >= 2:
                    pe.wait_ge(s["gate_ready"], c - 1)
                pe.matmul(B[4 + c % 2], w(0), S[2][:, ch(c)], start=True, stop=True).then_inc(s["k_done"], 1)
                if c >= 2:
                    pe.wait_ge(s["wv_ready"], c - 1)
                pe.matmul(B[6 + c % 2], w(1), S[3][:, ch(c)], start=True, stop=True).then_inc(s["v_done"], 1)
                pe.matmul(B[c], w(2), S[4][:, ch(c)], start=True, stop=True).then_inc(s["r_done"], 1)
            for c in range(CHUNKS):
                pe.wait_ge(s["z_ready"], c + 1)
                for t in range(TPC):
                    g = (c * TPC + t) * P
                    ins = pe.matmul(B[c][:, t * D:(t + 1) * D], S[0][:, g:g + P], w(3), start=True, stop=True)
                ins.then_inc(s["woo_done"], 1)
            for c in range(CHUNKS):
                pe.wait_ge(s["xh2_ready"], c + 1)
                transposes(B[4 + c], lambda t: tokv(5)[:, c * TPC + t, :], s["t2_done"])
            pe.wait_ge(s["w_ck"], 32)

            def ckr(c):
                pe.wait_ge(s["mix2_ready"], c + 1)
                if c == 0:
                    pe.wait_ge(s["h2T_ready"], CHUNKS)
                for f in range(FC):
                    if c >= 1:
                        pe.wait_ge(s["gelu_ready"], FC * (c - 1) + f + 1)
                    pe.matmul(B[4 + f], wck[:, f * P:(f + 1) * P], S[3][:, ch(c)], start=True, stop=True).then_inc(s["ck_done"], 1)
                pe.wait_ge(s["x1_ready"], c + 1)
                pe.matmul(B[c], w(4), S[4][:, ch(c)], start=True, stop=True).then_inc(s["cr_done"], 1)

            ckr(0)
            for c in range(CHUNKS):
                if c + 1 < CHUNKS:
                    ckr(c + 1)
                pe.wait_ge(s["gelu_ready"], FC * (c + 1))
                pe.wait_ge(s["tc_ready"], c + 1)
                for f in range(FC):
                    ins = pe.matmul(B[c], wcv[:, f, :], G[:, c % 2, f, :], start=f == 0, stop=f == FC - 1)
                ins.then_inc(s["vv2_done"], 1)
            for c in range(CHUNKS):
                pe.wait_ge(s["q_ready"], c + 1)
                transposes(B[4 + c], lambda t: S[6][:, (c * TPC + t) * P:(c * TPC + t + 1) * P], s["t3_done"])
            for c in range(CHUNKS):
                pe.wait_ge(s["xh3_ready"], c + 1)
                transposes(B[c], lambda t: X[:, c * TPC + t, :], s["t4_done"])
            pe.wait_ge(s["w_ffn"], 32)
            pe.wait_ge(s["selr_ready"], 1)
            pe.wait_ge(s["h1_ready"], CHUNKS)
            for c in range(CHUNKS):
                pe.wait_ge(s["x1T_ready"], c + 1)
                if c >= 1:
                    pe.wait_ge(s["qlo_ready"], c)
                pe.matmul(B[4], wf[:, 0:D], S[0][:, ch(c)], start=True, stop=True).then_inc(s["q_done"], 1)
                if c >= 1:
                    pe.wait_ge(s["klo_ready"], c)
                pe.matmul(B[5], wf[:, D:2 * D], S[0][:, ch(c)], start=True, stop=True).then_inc(s["kk_done"], 1)
                for t in range(TPC):
                    g = (c * TPC + t) * P
                    ins = pe.matmul(B[c][:, t * D:(t + 1) * D], S[0][:, g:g + P], wf[:, 2 * D:3 * D], start=True, stop=True)
                ins.then_inc(s["vt_done"], 1)
                pe.wait_ge(s["klo_ready"], c + 1)
                for j in range(PAIRS):
                    i = PAIRS * c + j
                    if i >= 2:
                        pe.wait_ge(s["kst_ready"], i - 1)
                    pe.matmul(B[6 + j % 2], SELR[:, 8 + j, :], KHI[:, c % 2, :], start=True, stop=False)
                    pe.matmul(B[6 + j % 2], SELR[:, 12 + j, :], KLO[:, c % 2, :], start=False, stop=True).then_inc(s["ksel_done"], 1)

            def qsel(u, last):
                q, j = divmod(u, PAIRS)
                pe.matmul(B[7], SELR[:, j, :], QHI[:, ch(q)], start=True, stop=False)
                return pe.matmul(B[7], SELR[:, 4 + j, :], QLO[:, ch(q)], start=False, stop=last)

            def maxes(u, i):
                j = u % PAIRS
                t, kq = divmod(i, 4)
                for h in range(2):
                    m = 32 * u + 2 * i + h
                    if m >= 3:
                        pe.wait_ge(s["mxr_done"], m - 2)
                    pe.matmul(B[m % 3], QM[u % 2][:, h, t * P:(t + 1) * P], KST[:, j, kq * CT:(kq + 1) * CT],
                              start=True, stop=True).then_inc(s["mxp_done"], 1)

            def scores(u, k):
                m, j = u * TILES + k, u % PAIRS
                for h in range(2):
                    b = 2 * m + h
                    if b >= 3:
                        pe.wait_ge(s["p_ready"], b - 2)
                    pe.matmul(B[3 + b % 3], KST[:, j, k * P:(k + 1) * P], QE[u % 2][:, h, :], start=True,
                              stop=True).then_inc(s["st_done"], 1)

            def weigh(u, kp):
                j = u % PAIRS
                pe.wait_ge(s["p_ready"], 2 * (u * TILES + 2 * kp + 2))
                if kp == 0 and u >= 1:
                    pe.wait_ge(s["xev_ready"], u)
                for h in range(2):
                    for par in range(2):
                        k = 2 * kp + par
                        q = 32 * (2 * h + par)
                        ins = pe.matmul(B[6][q:q + 32, :], valh(k, 2 * j + h), prob(u * TILES + k)[:, h, :],
                                        start=kp == 0, stop=kp == TILES // 2 - 1, tile_position=(0, q))
                ins.then_inc(s["av_done"], 1)

            def attended(q):
                pe.wait_ge(s["on_ready"], PAIRS * (q + 1))
                transposes(B[7], lambda t: tokv(6)[:, t, :], s["ot_done"])

            def project(q):
                pe.wait_ge(s["ot_ready"], q + 1)
                for t in range(TPC):
                    ins = pe.matmul(B[7][:, t * D:(t + 1) * D], S[5][:, CT + t * P:CT + (t + 1) * P], wof[:, :],
                                    start=True, stop=True)
                ins.then_inc(s["wo_done"], 1)

            def dsum(u):
                pe.wait_ge(s["xev_ready"], u + 1)
                n = 2 * (HD + 1)
                for t in range(TPC):
                    ins = pe.matmul(B[7][:, t * n:(t + 1) * n], S[5][:, t * P:(t + 1) * P], SELO[:, :], start=True, stop=True)
                ins.then_inc(s["dsum_done"], 1)

            def with_max(u):
                pe.wait_ge(s["nm_ready"], u + 1)
                qsel(u, False)
                for t in range(TPC):
                    ins = pe.matmul(B[7][:, t * P:(t + 1) * P], AM[:, t, :], IDR[:, :], start=False, stop=t == TPC - 1)
                ins.then_inc(s["qe_done"], 1)

            pe.wait_ge(s["vals_ready"], CHUNKS)
            pe.wait_ge(s["kst_ready"], CHUNKS * PAIRS)
            pe.wait_ge(s["qlo_ready"], CHUNKS)
            qsel(0, True).then_inc(s["qsel_done"], 1)
            pe.wait_ge(s["zero_ready"], 1)
            pe.wait_ge(s["qm_ready"], 1)
            for i in range(16):
                maxes(0, i)
            with_max(0)
            pe.wait_ge(s["qe_ready"], 1)
            qsel(1, True).then_inc(s["qsel_done"], 1)
            pe.wait_ge(s["qm_ready"], 2)
            for i in range(AHEAD):
                maxes(1, i)
            for u in range(UNITS):
                q = u // PAIRS
                for k in range(TILES):
                    scores(u, k)
                    v, i = divmod(16 * (u + 1) + k + AHEAD, 16)
                    if v < UNITS:
                        if i == 0:
                            pe.wait_ge(s["qm_ready"], v + 1)
                        maxes(v, i)
                    if k == 2 and u >= 1:
                        dsum(u - 1)
                    if k == 5 and u >= 1 and u % PAIRS == 0:
                        attended(q - 1)
                    if k == 7 and u >= 1 and u % PAIRS == 0:
                        project(q - 1)
                    if k == 9:
                        if u >= 1:
                            pe.wait_ge(s["on_ready"], u)
                        if u >= 1 and u % PAIRS == 0:
                            pe.wait_ge(s["y_ready"], q)
                        if u + 2 < UNITS:
                            qsel(u + 2, True).then_inc(s["qsel_done"], 1)
                    if k == 13 and u + 1 < UNITS:
                        if u + 2 < UNITS:
                            pe.wait_ge(s["qm_ready"], u + 3)
                        with_max(u + 1)
                    if k % 4 == 1:
                        g = u * 4 + (k - 5) // 4
                        if g >= 0:
                            weigh(g // 4, 2 * (g % 4))
                            weigh(g // 4, 2 * (g % 4) + 1)
                if u + 1 < UNITS:
                    pe.wait_ge(s["qe_ready"], u + 2)
            weigh(UNITS - 1, TILES // 2 - 2)
            weigh(UNITS - 1, TILES // 2 - 1)
            pe.wait_ge(s["on_ready"], UNITS - 1)
            dsum(UNITS - 1)
            attended(CHUNKS - 1)
            project(CHUNKS - 1)

            for c in range(CHUNKS):
                pe.wait_ge(s["xh4_ready"], c + 1)
                transposes(B[c], lambda t: X[:, c * TPC + t, :], s["t5_done"])
            pe.wait_ge(s["tT_ready"], CHUNKS)
            for t in range(TILES):
                ins = pe.matmul(B[4][:, t * E0:(t + 1) * E0], S[5][:, t * P:(t + 1) * P], wf[:, 3 * D:3 * D + E0],
                                start=True, stop=True)
            ins.then_inc(s["gl_done"], 1)
            pe.wait_ge(s["w_d"], 112)
            pe.wait_ge(s["cw_ready"], 1)
            chosen = cw[:, :, :].rearrange("p t e -> p (t e)")
            for k in range(2):
                ins = pe.matmul(B[5][:, k * TILES * E0:(k + 1) * TILES * E0], tri[:, k * P:(k + 1) * P], chosen,
                                start=True, stop=True)
            ins.then_inc(s["rank_done"], 1)
            pe.wait_ge(s["cw_ready"], 2)
            for t in range(TILES):
                ins = pe.transpose(B[t // TPC][0:E0, (t % TPC) * P:(t % TPC + 1) * P], gt[0][:, t, :], ID[:, :])
            ins.then_inc(s["cT_done"], 1)
            pe.wait_ge(s["cT_ready"], 1)
            for c in range(CHUNKS):
                for t in range(TPC):
                    ins = pe.matmul(B[c][:, t * D:(t + 1) * D], cT[:, (c * TPC + t) * P:(c * TPC + t + 1) * P], b2r[:, :],
                                    start=True, stop=True)
                ins.then_inc(s["acc0_done"], 1)

            def slots_over(g):
                n = min(4, XT - 4 * g)
                if g == 0:
                    pe.wait_ge(s["xs_in0"], 16)
                if g == 2:
                    pe.wait_ge(s["xs_in1"], 16)
                if g >= 2:
                    pe.wait_ge(s["tT_ready"], CHUNKS + g - 1)
                for t in range(n):
                    j = 4 * g + t
                    ins = pe.transpose(B[6 + g % 2][:, t * P:(t + 1) * P], V[:, j * D:(j + 1) * D], ID[:, :])
                ins.then_inc(s["t5_done"], 1)

            def up(j):
                pe.wait_ge(s["wc_ready"], j + 1)
                pe.wait_ge(s["tT_ready"], CHUNKS + j // 4 + 1)
                if j >= 2:
                    pe.wait_ge(s["hid_ready"], FC * (j - 1))
                for f in range(FC):
                    ins = pe.matmul(B[4 + j % 2][:, f * P:(f + 1) * P], wexp(j)[:, f * P:(f + 1) * P], xT(j), start=True,
                                    stop=True)
                ins.then_inc(s["w1_done"], 1)

            def down(j):
                if j >= 2:
                    pe.wait_ge(s["acc_ready"], j - 1)
                for f in range(FC):
                    pe.wait_ge(s["hid_ready"], FC * j + f + 1)
                    ins = pe.matmul(B[j % 2][:, 0:D], hid(j)[:, f * P:(f + 1) * P], wexp(j)[:, FF + f * D:FF + (f + 1) * D],
                                    start=f == 0, stop=f == FC - 1)
                ins.then_inc(s["w2_done"], 1)

            pe.wait_ge(s["acc0_ready"], CHUNKS)
            slots_over(0)
            up(0)
            for j in range(XT):
                if j % 4 == 1 and 4 * (j // 4 + 1) < XT:
                    slots_over(j // 4 + 1)
                if j + 1 < XT:
                    up(j + 1)
                down(j)

            for c in range(CHUNKS):
                pe.wait_ge(s["xh5_ready"], c + 1)
                transposes(B[c], lambda t: X[:, c * TPC + t, :], s["t6_done"])
            pe.wait_ge(s["w_l1"], 16)
            pe.wait_ge(s["xm_ready"], 1)
            for k in range(4):
                ins = pe.matmul(B[4][:, k * WS:(k + 1) * WS], wl[:, k * P:(k + 1) * P], xm[:, :], start=True, stop=True)
            ins.then_inc(s["gm_done"], 1)
            pe.wait_ge(s["gq_ready"], 1)
            for g in range(2):
                for j in range(4):
                    r = slice(32 * j, 32 * j + 32)
                    ins = pe.matmul(B[j][:, g * WS:(g + 1) * WS], gqb[r, g, :], km[r, g, :], start=True, stop=True,
                                    tile_position=(32 * j, 0))
            ins.then_inc(s["gb_done"], 1)

            def window_scores(c):
                for k in range(4):
                    if k < 2:
                        if c >= 1:
                            pe.wait_ge(s["v1_ready"], 2 * (c - 1) + k + 1)
                        if c >= 2:
                            pe.wait_ge(s["pt_ready"], 4 * (c - 2) + 4)
                    else:
                        pe.wait_ge(s["qk_ready"], 4 * c + k - 1)
                    pe.matmul(B[4 + k % 2], wl[:, k * P:(k + 1) * P], S[5][:, ch(c)], start=True, stop=True).then_inc(s["qk_done"], 1)
                wv = wl[:, 4 * P:5 * P]
                pe.wait_ge(s["qk_ready"], 4 * c + 3)
                for t in range(TPC):
                    g = (c * TPC + t) * P
                    ins = pe.matmul(B[4][:, t * D:(t + 1) * D], S[5][:, g:g + P], wv, start=True, stop=True)
                ins.then_inc(s["v1_done"], 1)
                pe.wait_ge(s["qk_ready"], 4 * c + 4)
                for t in range(TPC):
                    for par in range(2):
                        g = (c * TPC + t) * P + WS * par
                        o = WS * (1 - par)
                        ins = pe.matmul(B[5][o:o + WS, t * D:(t + 1) * D], S[5][:, g:g + WS], wv, start=True, stop=True,
                                        tile_position=(0, o))
                ins.then_inc(s["v1_done"], 1)
                for j in range(4):
                    if c == 0:
                        pe.wait_ge(s["bt_ready"], 1)
                    else:
                        pe.wait_ge(s["ns_ready"], 4 * (c - 1) + j + 1)
                for j in range(4):
                    r = slice(32 * j, 32 * j + 32)
                    for t in range(TPC):
                        for g in range(2):
                            for par in range(2):
                                x = t * P + WS * par
                                o = (2 * t + g) * WS
                                ins = pe.matmul(B[j][WS * par:WS * par + WS, o:o + WS],
                                                S[c % 2][r, g * CT + x:g * CT + x + WS],
                                                S[c % 2][r, (2 + g) * CT + x:(2 + g) * CT + x + WS],
                                                start=True, stop=True, tile_position=(32 * j, WS * par))
                    ins.then_inc(s["s_done"], 1)

            window_scores(0)
            window_scores(1)
            for c in range(CHUNKS):
                pe.wait_ge(s["p1_ready"], c + 1)
                for k in range(4):
                    if k < 2:
                        pe.wait_ge(s["v1_ready"], 2 * min(c + 2, CHUNKS))
                        if c >= 1:
                            pe.wait_ge(s["oT_ready"] if k == 0 else s["h3_ready"], c)
                    else:
                        pe.wait_ge(s["pt_ready"], 4 * c + k - 1)
                    transposes(B[4 + k % 2], lambda t: sco2(4 + 2 * (c % 2))[:, (k * TPC + t) * P:(k * TPC + t + 1) * P], s["pt_done"])
                pe.wait_ge(s["pt_ready"], 4 * (c + 1))
                if c >= 1:
                    pe.wait_ge(s["o_ready"], c)
                for g in range(2):
                    r = slice(WS * g, WS * g + WS)
                    for t in range(TPC):
                        for j in range(4):
                            for par in range(2):
                                o = (c % 2) * T + (j * TPC + t) * P + WS * par
                                ins = pe.matmul(B[6 + g][WS * par:WS * par + WS, (t * 4 + j) * 32:(t * 4 + j + 1) * 32],
                                                PB[r, o:o + WS], vwin(c, 0 if g == par else 1)[r, t, 4 * g + j, :],
                                                start=True, stop=True, tile_position=(WS * g, WS * par))
                ins.then_inc(s["ov_done"], 1)
                if c + 2 < CHUNKS:
                    window_scores(c + 2)
                pe.wait_ge(s["o_ready"], c + 1)
                if c + 2 < CHUNKS:
                    pe.wait_ge(s["v1_ready"], 2 * (c + 3))
                transposes(B[4], lambda t: tokv(4 + 2 * (c % 2))[:, t, :], s["t7_done"])
                pe.wait_ge(s["oT_ready"], c + 1)
                for t in range(TPC):
                    g = (c * TPC + t) * P
                    ins = pe.matmul(B[5][:, t * D:(t + 1) * D], S[5][:, g:g + P], wl[:, 5 * P:6 * P], start=True, stop=True)
                ins.then_inc(s["pr_done"], 1)

            for c in range(CHUNKS):
                pe.wait_ge(s["xh6_ready"], c + 1)
                transposes(B[c], lambda t: X[:, c * TPC + t, :], s["t8_done"])
            pe.wait_ge(s["fT_ready"], CHUNKS)
            for t in range(TILES):
                ins = pe.matmul(B[5][:, t * (2 + E1):(t + 1) * (2 + E1)], S[5][:, t * P:(t + 1) * P], wg1[:, :],
                                start=True, stop=True)
            ins.then_inc(s["g2_done"], 1)
            pe.wait_ge(s["c2_ready"], 1)
            for t in range(TILES):
                ins = pe.transpose(B[t // TPC][0:E1, (t % TPC) * P:(t % TPC + 1) * P], gt[0][:, t, :], ID[:, :])
            ins.then_inc(s["cn_done"], 1)
            pe.wait_ge(s["cn_ready"], 1)
            pe.wait_ge(s["wex_in"], 16)
            wex = V[:, 0:2 * E1 * D].rearrange("p (k n) -> p k n", k=2)
            for c in range(CHUNKS):
                for k in range(4):
                    if 4 * c + k >= 2:
                        pe.wait_ge(s["hsw_ready"], 4 * c + k - 1)
                    if k % 2 == 1 and c >= 1:
                        pe.wait_ge(s["cb_ready"], TPC * c)
                    m, half = divmod(k, 2)
                    x = S[5][:, ch(c)]
                    b0 = 2 * (k % 2)
                    pe.matmul(B[b0], win[:, m, half * P:(half + 1) * P], x, start=True, stop=True)
                    pe.matmul(B[b0 + 1], win[:, m, H1 + half * P:H1 + (half + 1) * P], x, start=True,
                              stop=True).then_inc(s["in_done"], 1)
                pe.wait_ge(s["hsw_ready"], 4 * c + 4)
                if c >= 1:
                    pe.wait_ge(s["xev_ready"], UNITS + c)
                for t in range(TPC):
                    dst = B[4][:, t * D:(t + 1) * D]
                    for k in range(2):
                        pe.matmul(dst, S[c % 2][:, k * CT + t * P:k * CT + (t + 1) * P], wso[:, k, :], start=k == 0, stop=False)
                    ins = pe.matmul(dst, cT[:, (c * TPC + t) * P:(c * TPC + t + 1) * P], eob[:, :], start=False, stop=True)
                ins.then_inc(s["sh_done"], 1)
                for t in range(TPC):
                    g = c * TPC + t
                    b0 = 6 if t % 2 == 0 else 2
                    if g >= 2:
                        pe.wait_ge(s["cb_ready"], g - 1)
                    for half in range(2):
                        for k in range(2):
                            ins = pe.matmul(B[b0 + half], S[c % 2][:, (2 + k) * CT + t * P:(2 + k) * CT + (t + 1) * P],
                                            wex[:, k, half * CT:(half + 1) * CT], start=k == 0, stop=k == 1)
                    ins.then_inc(s["ex_done"], 1)


def kernel(**inputs):
    import numpy as np
    import concourse.bacc as bacc
    from concourse.bass_utils import run_bass_kernel_spmd

    g = {k: np.asarray(v) for k, v in inputs.items()}

    def col(a):
        return np.ascontiguousarray(a).reshape(D, 1)

    f = np.float32
    pos = np.arange(1, T + 1, dtype=f)[:, None]
    i = np.arange(D)
    exponent = np.where(i % 2 == 0, i, i + 1).astype(f) / f(D)
    angle = (pos / np.power(f(10000.0), exponent)).astype(f)
    pe = np.where(i % 2 == 0, np.cos(angle), np.sin(angle)).astype(f)

    a = {}
    a["idx"] = np.ascontiguousarray(g["x"].reshape(TILES, P).T)
    a["emb"] = np.ascontiguousarray(g["L0_tok_W"].T)
    a["pe"] = np.ascontiguousarray(pe.reshape(TILES, P, D).transpose(1, 0, 2)).reshape(P, T)
    r = "L0_attn_"
    a["vec"] = np.concatenate([col(g[n]) for n in (
        r + "bk", r + "bv", r + "br", r + "bcv", r + "bcr", r + "ln1_g", r + "ln1_b", r + "ln2_g", r + "ln2_b",
        r + "time_decay", r + "time_first", r + "tmk", r + "tmv", r + "tmr", r + "cmk", r + "cmr",
        "L0_ffn_bq", "L0_ffn_bk", "L0_ffn_ln1_g", "L0_ffn_ln1_b", "L1_ffn_ln_scale", "L1_ffn_ln_bias")], 1)
    a["rows"] = np.concatenate([g["L0_tok_b"], g[r + "bo"], g["L0_ffn_bv"], g["L0_ffn_bo"], g["L0_ffn_gate_b"],
                                g["L1_attn_b_out"], g["L1_ffn_shared_out_b"], g["L1_ffn_group_bias"],
                                g["L1_ffn_expert_bias"], np.arange(E0, 0, -1).astype(f),
                                np.arange(0, T, P).astype(f), np.arange(XT).astype(f)]).reshape(1, NR)
    a["w_rwkv"] = np.concatenate([g[r + n] for n in ("Wk", "Wv", "Wr", "Wo", "Wcr")], 1)
    a["w_ck"] = g[r + "Wck"]
    a["w_cv"] = np.ascontiguousarray(g[r + "Wcv"].reshape(FC, P, D).transpose(1, 0, 2))
    a["bckc"] = np.ascontiguousarray(g[r + "bck"].reshape(FC, P).T)
    q = "L0_ffn_"
    a["w_ffn"] = np.concatenate([g[q + "Wq"], g[q + "Wk"], g[q + "Wv"], g[q + "gate_W"]], 1)
    a["w_of"] = g[q + "Wo"]
    a["tri"] = np.concatenate([np.triu(np.ones((P, P), f), 1), np.ones((P, P), f)], 1)
    a["zrow"] = np.zeros((1, D), f)
    a["ident"] = np.eye(P, dtype=f)
    rr = np.arange(P)
    cc = np.arange(2 * (HD + 1))
    a["selo"] = ((rr[:, None] // 64 == cc[None, :] // (HD + 1)) & (rr[:, None] % 32 == cc[None, :] % (HD + 1))).astype(f)
    sel = np.zeros((P, 16, P), f)
    for j in range(PAIRS):
        for dst in range(P):
            src = (2 * j + dst // 64) * HD + dst % HD
            part = dst % 64 // HD
            if part < 3:
                sel[src, (4 if part == 1 else 0) + j, dst] = 1
                sel[src, (12 if part == 2 else 8) + j, dst] = 1
    a["sel"] = sel.reshape(P, 16 * P)
    kone = np.zeros((P, 1), f)
    kone[[48, 49, 112, 113]] = 1
    a["kone"] = kone
    a["b1c"] = np.ascontiguousarray(g[q + "b1"].reshape(E0, FC, P).transpose(2, 0, 1)).reshape(P, E0 * FC)
    a["b2r"] = g[q + "b2"]
    a["moe_w1"] = np.ascontiguousarray(g[q + "W1"].transpose(1, 0, 2)).reshape(P, E0 * FF)
    a["moe_w2"] = np.ascontiguousarray(g[q + "W2"].reshape(E0, FC, P, D).transpose(2, 0, 1, 3)).reshape(P, E0 * FF)
    w = g["L1_attn_w_qkv"]
    pads = np.zeros((D, 4, 4, 32), f)
    for k in range(4):
        part = w[:, (k // 2) * D:(k // 2 + 1) * D].reshape(D, 2, 4, HD)
        pads[:, k, :, :HD] = part[:, k % 2]
    a["w_l1"] = np.concatenate([pads.reshape(D, 4 * P), w[:, 2 * D:], g["L1_attn_w_out"]], 1)
    gt = g["L1_attn_gate"].reshape(2, 4, 1)
    a["gat"] = np.ascontiguousarray(np.broadcast_to(gt, (2, 4, 32)).reshape(2, P).T)
    gp = g["L1_attn_global_param"].reshape(2, 4, 1, G1 * WS)
    a["gp"] = np.ascontiguousarray(np.broadcast_to(gp, (2, 4, 32, G1 * WS))).reshape(2, P, G1 * WS)
    a["lb"] = np.ascontiguousarray(g["L1_attn_local_bias"].reshape(2, 4, WS, WS).transpose(2, 1, 0, 3)).reshape(WS, HEADS, WS)
    d = "L1_ffn_"
    a["w_in"] = np.ascontiguousarray(np.stack([g[d + "shared_in_w"].T, g[d + "expert_in_w"].T], 1))
    a["w_so"] = np.ascontiguousarray(g[d + "shared_out_w"].T.reshape(2, P, D).transpose(1, 0, 2))
    a["w_ex"] = np.ascontiguousarray(g[d + "expert_out_weight"].transpose(2, 0, 1).reshape(2, P, E1 * D).transpose(1, 0, 2)).reshape(P, 2 * E1 * D)
    a["w_g1"] = np.ascontiguousarray(np.concatenate([g[d + "group_gate_w"], g[d + "expert_gate_w"]], 0).T)
    a["eob"] = g[d + "expert_out_bias"]

    nc = bacc.Bacc("TRN2", target_bir_lowering=False, num_devices=1)
    arrays, args = {}, {}
    for n, v in a.items():
        v = np.ascontiguousarray(v)
        arrays["in_" + n] = v
        args[n] = nc.dram_tensor("in_" + n, v.shape, mybir.dt.from_np(v.dtype), kind="ExternalInput").ap()
    out = nc.dram_tensor("out_h", (T, D), mybir.dt.float32, kind="ExternalOutput").ap()
    xs = nc.dram_tensor("slots_in", (XS, D), mybir.dt.float32, kind="Internal").ap()
    ys = nc.dram_tensor("slots_out", (XS, D), mybir.dt.float32, kind="Internal").ap()
    build_tower(nc, args, out.rearrange("(t p) d -> p t d", p=P), xs, ys)
    res = run_bass_kernel_spmd(nc, [arrays], core_ids=[0])
    return res.results[0]["out_h"].reshape(1, T, D)
```

```python
import concourse.bass as bass
from concourse import mybir
from contextlib import ExitStack

T = 2048
D = 128
P = 128
TILES = T // P
CT = 512
CHUNKS = T // CT
TPC = CT // P
HEADS = 8
HD = D // HEADS
PAIRS = HEADS // 2
UNITS = CHUNKS * PAIRS
LAG = 3
AHEAD = 5
PSLOTS = 6
FF = 4 * D
FC = FF // P
E0 = 8
XT = (T + E0 * (P - 1)) // P
XS = XT * P
HSLOTS = 4
WSLOTS = 4
WS = 64
G1 = 32
KEEP = int(WS * (1.0 - 0.3))
DROP = WS - KEEP
H1 = 256
E1 = 8
EG = 4
EPS = 1e-5
NEG = -3.0e38

VECS = ["bk", "bv", "br", "bcv", "bcr", "g1", "b1", "g2", "b2", "decay", "first", "mk", "mv", "mr", "ck", "cr",
        "bq", "bkf", "gf", "bf", "ls", "lb"]
VI = {n: i for i, n in enumerate(VECS)}
NV = len(VECS)
ROWS = [("tokb", D), ("bo", D), ("bvf", D), ("bof", D), ("gateb", E0), ("bout", D), ("shb", D), ("gb", 2),
        ("eb", E1), ("prio", E0),
        ("full", TILES), ("tileno", XT)]
RO = {}
NR = 0
for _n, _w in ROWS:
    RO[_n] = (NR, NR + _w)
    NR += _w


def build_tower(nc, A, out, xs, ys):
    f32, f32r, i32 = mybir.dt.float32, mybir.dt.float32r, mybir.dt.int32
    ALU, ACT, AX = mybir.AluOpType, mybir.ActivationFunctionType, mybir.AxisListType
    ctx = ExitStack()
    with ctx:
        def sb(name, shape, dt=f32):
            return ctx.enter_context(nc.sbuf_tensor("s_" + name, shape, dt))

        def sem(name):
            return ctx.enter_context(nc.semaphore(name))

        H = sb("resid", [P, TILES, D])
        X = sb("normed", [P, TILES, D])
        SW = T + 8
        SS = sb("scratch", [P, 7 * SW])
        S = [SS[:, i * SW:(i + 1) * SW] for i in range(7)]
        V = sb("vals", [P, 4096])
        PB = sb("probs", [P, 4096])
        QHI, QLO = sb("qhi", [P, T], f32r), sb("qlo", [P, T], f32r)
        KHI, KLO = sb("khi", [P, 2, CT], f32r), sb("klo", [P, 2, CT], f32r)
        KST = sb("kstack", [P, PAIRS, T], f32r)
        SELR = sb("selr", [P, 4 * PAIRS, P], f32r)
        IDR = sb("identr", [P, P], f32r)
        QM = [sb("qmax", [P, 2, CT], f32r), KHI]
        QE = [KLO, SELR[:, 8:16, :].rearrange("p (h a) b -> p h (a b)", h=2)]
        AM = sb("amax", [P, TPC, P], f32r)
        ID = sb("ident", [P, P])
        SELO = sb("selo", [P, 2 * (HD + 1)])
        DEC = sb("dec", [P, CT])
        vec = sb("vec", [P, NV])
        drv = sb("drv", [P, 16])
        kone = sb("kone", [P, 1])
        row = sb("rows", [P, NR])
        idx = sb("idx", [P, TILES], i32)
        wrk = sb("w_rwkv", [P, 5 * D + FF])
        wr, wck = wrk[:, 0:5 * D], wrk[:, 5 * D:5 * D + FF]
        wcv = sb("w_cv", [P, FC, D])
        wf = sb("w_ffn", [P, 3 * D + E0])
        wof = sb("w_of", [P, D])
        wl = sb("w_l1", [P, 4 * D + 2 * D])
        win = sb("w_in", [P, 2, FF])
        wso = sb("w_so", [P, 2, D])
        wg1 = sb("w_g1", [P, 2 + E1])
        eob = sb("w_eob", [E1, D])
        b1c = sb("b1c", [P, E0 * FC])
        b2r = sb("b2r", [E0, D])
        bckc = sb("bckc", [P, FC])
        nh = sb("neghalf", [P, 8])
        st6 = sb("st6", [P, TILES, 6])
        MV = [sb(f"mv{i}", [P, TILES, 2]) for i in range(6)]
        RAB = sb("rab", [P, 2, TILES])
        RB = RAB[:, 1, :]
        RA = [RAB[:, 0, :]] + [sb(f"ra{i}", [P, TILES]) for i in range(1, 5)]
        VE = sb("ve", [P, 2, 2, TPC])
        mq = sb("mq", [P, 8, 4])
        nm = sb("nm", [P, 8])
        cw = sb("cw", [P, TILES, E0])
        gt = [sb(f"gt{i}", [P, TILES, E0]) for i in range(4)]
        gs = sb("gs", [P, 4, TILES])
        cT = S[4][0:E0, 0:T]
        tri = sb("tri", [P, 2 * P])
        slot = sb("slot", [P, TILES], i32)
        tex = sb("tex", [P, XT], i32)
        xmc = sb("xmc", [P, CHUNKS, WS])
        b1w = sb("b1w", [P, WSLOTS, FC])
        gpm = sb("gpm", [P, 2, WS])
        xm = sb("xm", [P, WS])
        wcvf = wcv[:, :, :].rearrange("p f d -> p (f d)")
        qm = wcvf[:, 0:2 * WS].rearrange("p (g n) -> p g n", g=2)
        km = wcvf[:, 2 * WS:4 * WS].rearrange("p (g n) -> p g n", g=2)
        gq = sb("gq", [P, 8])
        gqb = wcvf[:, 4 * WS:4 * WS + 2 * P].rearrange("p (g n) -> p g n", g=2)
        gat = sb("gat", [P, 2])
        BT = DEC[:, :].rearrange("p (h m) -> p h m", m=WS)
        t8 = wrk[:, 0:768].rearrange("p (k r e) -> p k r e", k=3, e=8)
        mn = sb("mn", [P, 32])
        oden = sb("oden", [P, 2, 16])
        gpick = sb("gpick", [P, TILES, 2])

        def sco(i):
            return S[i][:, 0:T].rearrange("p (r m) -> p r m", m=WS)

        def tokv(i):
            return S[i][:, 0:T].rearrange("p (t d) -> p t d", d=D)

        PS = ctx.enter_context(nc.psum_tensor("banks", [P, 8, CT], f32))
        B = [PS[:, i, :] for i in range(8)]

        names = """w_idx w_pe w_vec w_rwkv w_ck w_ffn w_sel w_misc w_l1
            w_d w_moe w_gp w_lb h_ready xh_ready t1_done hT_ready mix_ready
            k_done v_done r_done gate_ready wv_ready tr_ready z_ready woo_done x1_ready
            x0b_ready xh2_ready t2_done h2T_ready mix2_ready cr_done ck_done gelu_ready tc_ready vv2_done
            q_ready t3_done h1_ready xh3_ready t4_done x1T_ready q_done kk_done vt_done qhi_ready
            khi_ready qlo_ready klo_ready vals_ready ksel_done kst_ready xb_ready qsel_done qm_ready mxp_done
            mxr_done nm_ready qe_done qe_ready st_done p_ready av_done xev_ready dsum_done on_ready
            wo_done y_ready xh4_ready t5_done tT_ready gl_done cw_ready cT_done cT_ready acc0_done
            acc0_ready w1_done hid_ready w2_done acc_ready h2_ready xh5_ready t6_done x2T_ready xm_ready
            gm_done gq_ready gb_done bt_ready qk_done qk_ready v1_done v1_ready s_done ns_ready
            mn_ready e_in e_ready p1_ready pt_done pt_ready ov_done o_ready t7_done oT_ready
            pr_done h3_ready h3b_ready xh6_ready t8_done fT_ready in_done gb_copied hsw_ready sh_done
            ex_done g2_done cb_ready cn_done cn_ready fin_ready dve_step act_step pool_step st_out
            ot_done ot_ready zero_ready ln_stats ln_rstd gpm_ready ones_ready kept hx_ready rec_ready rank_done slot_ready xs_zero sc_in xs_in0 xs_in1
            wc_ready ys_out gate_sig drv_ready drv_act selr_ready c2_ready gs_ready wex_in""".split()
        s = {n: sem(n) for n in names}
        emb_in = [sem(f"emb_in{c}") for c in range(CHUNKS)]
        block = ctx.enter_context(nc.Block())

        def vc(n):
            return vec[:, VI[n]:VI[n] + 1]

        def rowv(n):
            a, b = RO[n]
            return row[:, a:b]

        def rows_over(n, k):
            a, b = RO[n]
            return row[:, a:b].unsqueeze(1).to_broadcast([P, k, b - a])

        def ch(c):
            return slice(c * CT, (c + 1) * CT)

        def tl(c):
            return slice(c * TPC, (c + 1) * TPC)

        def bt4(b):
            return B[b].rearrange("p (t d) -> p t d", d=D)

        hT = S[1]

        def ytile(j, n=1):
            return S[5 + j // TILES][:, (j % TILES) * D:(j % TILES + n) * D]

        def xT(j):
            return PB[:, j * P:(j + 1) * P]

        def hid(j):
            half = j % 2 * FC * P
            home = PB[:, XT * P:] if j % HSLOTS < 2 else S[6][:, (XT - TILES) * P:]
            return home[:, half:half + FC * P]

        def wexp(j):
            k, half = j % WSLOTS // 2, j % 2
            home = X[:, :, :].rearrange("p t d -> p (t d)") if k == 0 else S[4]
            return home[:, half * 2 * FF:(half + 1) * 2 * FF]

        @block.sync
        def _(sp):
            sp.dma_start(idx[:, :], A["idx"]).then_inc(s["w_idx"], 16)
            sp.dma_start(S[6][:, 0:T], A["pe"]).then_inc(s["w_pe"], 16)
            sp.dma_start(row[:, :], A["rows"].to_broadcast([P, NR])).then_inc(s["w_pe"], 16)
            sp.dma_start(vec[:, :], A["vec"]).then_inc(s["w_vec"], 16)
            sp.dma_start(gat[:, :], A["gat"]).then_inc(s["w_vec"], 16)
            sp.dma_start(ID[:, :], A["ident"]).then_inc(s["w_misc"], 16)
            sp.dma_start(SELO[:, :], A["selo"]).then_inc(s["w_misc"], 16)
            sp.dma_start(bckc[:, :], A["bckc"]).then_inc(s["w_misc"], 16)
            sp.dma_start(kone[:, :], A["kone"]).then_inc(s["w_misc"], 16)
            sp.dma_start(wr, A["w_rwkv"]).then_inc(s["w_rwkv"], 16)
            sp.dma_start(PB[:, 0:T], A["sel"]).then_inc(s["w_sel"], 16)
            sp.dma_start(wck, A["w_ck"]).then_inc(s["w_ck"], 16)
            sp.dma_start(wcv[:, :, :], A["w_cv"]).then_inc(s["w_ck"], 16)
            sp.dma_start(wf[:, :], A["w_ffn"]).then_inc(s["w_ffn"], 16)
            sp.dma_start(wof[:, :], A["w_of"]).then_inc(s["w_ffn"], 16)
            sp.dma_start(wl[:, :], A["w_l1"]).then_inc(s["w_l1"], 16)
            sp.dma_start(win[:, :, :], A["w_in"]).then_inc(s["w_d"], 16)
            sp.dma_start(wso[:, :, :], A["w_so"]).then_inc(s["w_d"], 16)
            sp.dma_start(wg1[:, :], A["w_g1"]).then_inc(s["w_d"], 16)
            sp.dma_start(eob[:, :], A["eob"]).then_inc(s["w_d"], 16)
            sp.dma_start(b1c[:, :], A["b1c"]).then_inc(s["w_d"], 16)
            sp.dma_start(b2r[:, :], A["b2r"]).then_inc(s["w_d"], 16)
            sp.dma_start(tri[:, :], A["tri"]).then_inc(s["w_d"], 16)
            for g in range(2):
                sp.dma_start(V[:, g * T:(g + 1) * T], A["gp"][g, :, :]).then_inc(s["w_gp"], 16)
            sp.dma_start(xs, A["zrow"].to_broadcast([XS, D])).then_inc(s["xs_zero"], 16)
            sp.wait_ge(s["z_ready"], CHUNKS)
            for half in range(2):
                sp.dma_start(BT[half * WS:(half + 1) * WS, :, :], A["lb"]).then_inc(s["w_lb"], 16)
            sp.wait_ge(s["ksel_done"], PAIRS * CHUNKS)
            sp.wait_ge(s["vals_ready"], CHUNKS)
            sp.dma_start(SS[:, 0:E0 * FF], A["moe_w1"]).then_inc(s["w_moe"], 16)
            sp.dma_start(SS[:, 2 * SW:2 * SW + E0 * FF], A["moe_w2"]).then_inc(s["w_moe"], 16)
            xsv, ysv = xs.rearrange("(j p) d -> p j d", p=P), ys.rearrange("(j p) d -> p j d", p=P)
            sp.wait_ge(s["sc_in"], 16 * TILES)
            sp.dma_start(V[:, 0:8 * D].rearrange("p (j d) -> p j d", d=D), xsv[:, 0:8, :]).then_inc(s["xs_in0"], 16)
            sp.dma_start(V[:, 8 * D:XT * D].rearrange("p (j d) -> p j d", d=D), xsv[:, 8:XT, :]).then_inc(s["xs_in1"], 16)
            for j in range(0, XT, 2):
                n = min(2, XT - j)
                sp.wait_ge(s["acc_ready"], j + n)
                sp.dma_start(ysv[:, j:j + n, :], ytile(j, n).rearrange("p (j d) -> p j d", d=D)).then_inc(s["ys_out"], 16)
            sp.wait_ge(s["ov_done"], CHUNKS)
            sp.dma_start(V[:, 0:2 * E1 * D], A["w_ex"]).then_inc(s["wex_in"], 16)
            for c in range(CHUNKS):
                sp.wait_ge(s["fin_ready"], c + 1)
                sp.dma_start(out[:, tl(c), :], H[:, tl(c), :]).then_inc(s["st_out"], 16)
            sp.wait_ge(s["st_out"], 16 * CHUNKS)

        @block.gpsimd
        def _(pool):
            n = [0]

            def step(ins):
                n[0] += 1
                ins.then_inc(s["pool_step"], 1)
                pool.wait_ge(s["pool_step"], n[0])

            def gather(c):
                for t in range(c * TPC, (c + 1) * TPC):
                    pool.indirect_dma_start(H[:, t, :], None, A["emb"],
                                            bass.IndirectOffsetOnAxis(ap=idx[:, t:t + 1], axis=0)).then_inc(emb_in[c], 16)

            def rstd(k, c, twice=False):
                pool.wait_ge(s["ln_stats"], CHUNKS * k + c + 1)
                ve, var = VE[:, c % 2, :, :], MV[k][:, tl(c), 1]
                if k != 5:
                    step(pool.tensor_scalar(ve[:, 0, :], var, EPS, None, ALU.add))
                if twice:
                    step(pool.tensor_scalar(ve[:, 1, :], var, 1.0 + EPS, EPS * EPS, ALU.mult, ALU.add))
                if k == 0:
                    pool.tensor_tensor(RAB[:, :, tl(c)], ve, nh[:, :].rearrange("p (k t) -> p k t", k=2),
                                       ALU.pow).then_inc(s["ln_rstd"], 1)
                elif k == 5:
                    pool.tensor_tensor(RB[:, tl(c)], ve[:, 1, :], nh[:, 0:TPC], ALU.pow).then_inc(s["ln_rstd"], 1)
                else:
                    pool.tensor_tensor(RA[k][:, tl(c)], ve[:, 0, :], nh[:, 0:TPC], ALU.pow).then_inc(s["ln_rstd"], 1)

            step(pool.memset(nh[:, :], -0.5))
            pool.wait_ge(s["w_idx"], 16)
            for c in range(3):
                gather(c)
            rstd(0, 0, True)
            gather(3)
            for c in range(1, CHUNKS):
                rstd(0, c, True)
            pool.wait_ge(s["ln_rstd"], CHUNKS)
            step(pool.memset(QM[0][64:128, 0, :].bitcast(f32), 0.0))
            pool.memset(QM[0][0:64, 1, :].bitcast(f32), 0.0).then_inc(s["zero_ready"], 1)
            pool.wait_ge(s["zero_ready"], 1)
            step(pool.tensor_scalar(rowv("bo"), rowv("bo"), 0.5, None, ALU.mult))
            for c in range(CHUNKS):
                for t in range(c * TPC, (c + 1) * TPC):
                    ins = pool.tensor_scalar(X[:, t, :], H[:, t, :], MV[0][:, t, 0:1], RA[0][:, t:t + 1],
                                             ALU.subtract, ALU.mult)
                step(ins)
                pool.tensor_tensor(X[:, tl(c), :], X[:, tl(c), :], rows_over("bo", TPC), ALU.add).then_inc(s["x0b_ready"], 1)
            for c in range(CHUNKS):
                pool.wait_ge(s["rec_ready"], c + 1)
                pool.wait_ge(s["tr_ready"], c + 1)
                pool.tensor_tensor(S[0][:, ch(c)], S[3][:, ch(c)], S[4][:, ch(c)], ALU.mult).then_inc(s["z_ready"], 1)
            for c in range(CHUNKS):
                rstd(1, c)
            for c in range(CHUNKS):
                pool.wait_ge(s["x1_ready"], c + 1)
                pool.tensor_tensor(H[:, tl(c), :], H[:, tl(c), :], X[:, tl(c), :], ALU.add).then_inc(s["hx_ready"], 1)
            pool.wait_ge(s["gpm_ready"], 1)
            pool.memset(V[:, :], 1.0).then_inc(s["ones_ready"], 1)
            pool.wait_ge(s["ones_ready"], 1)
            for c in range(CHUNKS):
                rstd(2, c)
            pool.wait_ge(s["ksel_done"], CHUNKS * PAIRS)
            for i, stack in enumerate((QM[1], QE[0], QE[1])):
                step(pool.memset(stack[64:128, 0, :].bitcast(f32), 0.0))
                pool.memset(stack[0:64, 1, :].bitcast(f32), 0.0).then_inc(s["zero_ready"], 1)
                pool.wait_ge(s["zero_ready"], 2 + i)
            for c in range(CHUNKS):
                pool.wait_ge(s["xh3_ready"], c + 1)
                pool.wait_ge(s["t4_done"], c + 1)
                pool.tensor_tensor(X[:, tl(c), :], X[:, tl(c), :], rows_over("bof", TPC), ALU.add).then_inc(s["xb_ready"], 1)
            for c in range(CHUNKS):
                rstd(3, c)
            pool.wait_ge(s["xs_zero"], 16)
            pool.wait_ge(s["slot_ready"], 1)
            for t in range(TILES):
                pool.indirect_dma_start(xs, bass.IndirectOffsetOnAxis(ap=slot[:, t:t + 1], axis=0), X[:, t, :],
                                        None).then_inc(s["sc_in"], 16)
            pool.wait_ge(s["ys_out"], 16 * ((XT + 1) // 2))
            for c in range(CHUNKS):
                for t in range(c * TPC, (c + 1) * TPC):
                    pool.indirect_dma_start(V[:, t * D:(t + 1) * D], None, ys,
                                            bass.IndirectOffsetOnAxis(ap=slot[:, t:t + 1], axis=0)).then_inc(emb_in[c], 16)
                if c >= 1:
                    rstd(4, c - 1)
            rstd(4, CHUNKS - 1)
            for c in range(CHUNKS):
                pool.wait_ge(s["xh5_ready"], c + 1)
                pool.tensor_tensor(H[:, tl(c), :], H[:, tl(c), :], rows_over("bout", TPC), ALU.add).then_inc(s["h3b_ready"], 1)
            def distance(c):
                pool.wait_ge(s["mn_ready"], c + 1)
                if c >= 2:
                    pool.wait_ge(s["t7_done"], c - 1)
                pool.tensor_tensor(sco(4 + 2 * (c % 2)), sco(2 + c % 2),
                                   mn[:, :].unsqueeze(2).to_broadcast([P, 32, WS]), ALU.subtract).then_inc(s["e_in"], 1)

            def gated(c):
                for k in range(4):
                    pool.wait_ge(s["gb_copied"], 4 * c + k + 1)
                    sl = S[c][:, k * CT:(k + 1) * CT]
                    pool.tensor_tensor(sl, sl, PB[:, k * CT:(k + 1) * CT], ALU.mult).then_inc(s["hsw_ready"], 1)

            def keep(c):
                ex = sco(4 + 2 * (c % 2))
                pool.wait_ge(s["kept"], c + 1)
                pool.wait_ge(s["e_ready"], c + 1)
                pool.tensor_tensor(ex, ex, sco(2 + c % 2), ALU.mult).then_inc(s["p1_ready"], 1)

            distance(0)
            keep(0)
            distance(1)
            keep(1)
            distance(2)
            rstd(5, 0, True)
            keep(2)
            distance(3)
            rstd(5, 1, True)
            gated(0)
            gated(1)
            rstd(5, 2, True)
            rstd(5, 3, True)
            gated(2)
            gated(3)

        G = PB[:, :].rearrange("p (k f t) -> p k f t", k=2, f=FC)

        def prob(m):
            k = m % PSLOTS
            home = PB[:, k * 2 * CT:(k + 1) * 2 * CT] if k < 4 else S[k + 1][:, 2 * CT:4 * CT]
            return home.rearrange("p (h q) -> p h q", h=2)

        def val(c):
            return V[:, :].rearrange("p (t h d) -> p t h d", h=HEADS, d=32)[:, tl(c), :, :]

        def valh(k, h):
            return V[:, (k * HEADS + h) * 32:(k * HEADS + h + 1) * 32]

        def vwin(c, k):
            return V[:, :].rearrange("p (c k t h d) -> p c k t h d", c=2, k=2, h=HEADS, d=32)[:, c % 2, k, :, :, :]

        def sco2(i):
            return S[i][:, 0:T]

        @block.scalar
        def _(act):
            n = [0]

            def step(ins):
                n[0] += 1
                ins.then_inc(s["act_step"], 1)
                act.wait_ge(s["act_step"], n[0])

            act.wait_ge(s["w_vec"], 32)
            act.activation(drv[:, 0:1], vc("decay"), ACT.Sigmoid).then_inc(s["act_step"], 1)
            act.activation(gat[:, :], gat[:, :], ACT.Sigmoid).then_inc(s["gate_sig"], 1)
            act.activation(drv[:, 1:2], vc("first"), ACT.Tanh).then_inc(s["drv_act"], 1)
            n[0] = 1
            act.wait_ge(s["drv_ready"], 1)
            for c in range(CHUNKS):
                act.wait_ge(s["t1_done"], c + 1)
                act.activation(hT[:, 1 + c * CT:1 + (c + 1) * CT], B[c], ACT.Identity, bias=vc("b1"),
                               scale=vc("g1")).then_inc(s["hT_ready"], 1)
            for c in range(CHUNKS):
                act.wait_ge(s["k_done"], c + 1)
                act.activation(S[5][:, ch(c)], B[4 + c % 2], ACT.Sigmoid, bias=drv[:, 2:3]).then_inc(s["gate_ready"], 1)
                act.wait_ge(s["v_done"], c + 1)
                act.activation(S[3][:, ch(c)], B[6 + c % 2], ACT.Identity, bias=vc("bv"))
                act.activation(S[2][:, ch(c)], B[6 + c % 2], ACT.Identity, bias=drv[:, 4:5],
                               scale=drv[:, 3:4]).then_inc(s["wv_ready"], 1)
                act.wait_ge(s["r_done"], c + 1)
                act.activation(S[4][:, ch(c)], B[c], ACT.Tanh, bias=vc("br")).then_inc(s["tr_ready"], 1)
            for c in range(CHUNKS):
                act.wait_ge(s["t2_done"], c + 1)
                act.activation(hT[:, 1 + c * CT:1 + (c + 1) * CT], B[4 + c], ACT.Identity, bias=vc("b2"),
                               scale=vc("g2")).then_inc(s["h2T_ready"], 1)
            for c in range(CHUNKS):
                for f in range(FC):
                    act.wait_ge(s["ck_done"], FC * c + f + 1)
                    if c >= 2:
                        act.wait_ge(s["vv2_done"], c - 1)
                    act.activation(G[:, c % 2, f, :], B[4 + f], ACT.Gelu, bias=bckc[:, f:f + 1]).then_inc(s["gelu_ready"], 1)
                act.wait_ge(s["cr_done"], c + 1)
                act.activation(S[2][:, ch(c)], B[c], ACT.Tanh, bias=vc("bcr")).then_inc(s["tc_ready"], 1)
            for c in range(CHUNKS):
                act.wait_ge(s["t4_done"], c + 1)
                act.activation(S[0][:, ch(c)], B[c], ACT.Copy).then_inc(s["x1T_ready"], 1)
            def filled(dst, done):
                act.activation(dst[0:64, 0, :], B[7][0:64, :], ACT.Copy)
                act.activation(dst[64:128, 1, :], B[7][64:128, :], ACT.Copy).then_inc(done, 1)

            for c in range(CHUNKS):
                act.wait_ge(s["q_done"], c + 1)
                act.activation(QHI[:, ch(c)], B[4], ACT.Identity, bias=vc("bq")).then_inc(s["qhi_ready"], 1)
                act.wait_ge(s["kk_done"], c + 1)
                if c >= 2:
                    act.wait_ge(s["ksel_done"], PAIRS * (c - 1))
                act.activation(KHI[:, c % 2, :], B[5], ACT.Identity, bias=vc("bkf")).then_inc(s["khi_ready"], 1)
                for j in range(PAIRS):
                    act.wait_ge(s["ksel_done"], PAIRS * c + j + 1)
                    act.activation(KST[:, j, ch(c)], B[6 + j % 2], ACT.Identity, bias=kone[:, 0:1]).then_inc(s["kst_ready"], 1)
                if c == 0:
                    act.wait_ge(s["qsel_done"], 1)
                    filled(QM[0], s["qm_ready"])

            def weighed(u):
                act.wait_ge(s["av_done"], 8 * (u + 1))
                if u >= 1:
                    act.wait_ge(s["dsum_done"], u)
                act.activation(S[5][:, 0:CT], B[6], ACT.Copy).then_inc(s["xev_ready"], 1)

            def attended(q):
                act.wait_ge(s["ot_done"], q + 1)
                act.activation(S[5][:, CT:2 * CT], B[7], ACT.Copy).then_inc(s["ot_ready"], 1)

            act.wait_ge(s["qe_done"], 1)
            filled(QE[0], s["qe_ready"])
            act.wait_ge(s["qsel_done"], 2)
            filled(QM[1], s["qm_ready"])
            for u in range(UNITS):
                for k in range(TILES):
                    m = u * TILES + k
                    if m >= PSLOTS:
                        act.wait_ge(s["av_done"], (m - PSLOTS) // 2 + 1)
                    for h in range(2):
                        act.wait_ge(s["st_done"], 2 * m + h + 1)
                        act.activation(prob(m)[:, h, :], B[3 + (2 * m + h) % 3], ACT.Exp, scale=HD ** -0.5).then_inc(s["p_ready"], 1)
                    if k == 1 and u >= 1:
                        weighed(u - 1)
                    if k == 5 and u >= 1 and u % PAIRS == 0:
                        attended(u // PAIRS - 1)
                    if k == 9 and u + 2 < UNITS:
                        act.wait_ge(s["qsel_done"], u + 3)
                        filled(QM[u % 2], s["qm_ready"])
                    if k == 13 and u + 1 < UNITS:
                        act.wait_ge(s["qe_done"], u + 2)
                        filled(QE[(u + 1) % 2], s["qe_ready"])
            weighed(UNITS - 1)
            attended(CHUNKS - 1)

            act.wait_ge(s["wo_done"], CHUNKS)
            for c in range(CHUNKS):
                act.wait_ge(s["t5_done"], c + 1)
                act.activation(S[5][:, ch(c)], B[c], ACT.Identity, bias=vc("bf"), scale=vc("gf")).then_inc(s["tT_ready"], 1)
            act.wait_ge(s["gs_ready"], 1)
            act.activation(gt[1][:, :, :], gt[0][:, :, :], ACT.Exp).then_inc(s["gs_ready"], 1)
            act.wait_ge(s["cT_done"], 1)
            for k in range(4):
                ins = act.activation(cT[:, ch(k)], B[k][0:E0, :], ACT.Copy)
            ins.then_inc(s["cT_ready"], 1)
            def slots_out(g):
                n = min(4, XT - 4 * g)
                act.wait_ge(s["t5_done"], CHUNKS + g + 1)
                act.activation(PB[:, 4 * g * P:(4 * g + n) * P], B[6 + g % 2][:, 0:n * P], ACT.Identity, bias=vc("bf"),
                               scale=vc("gf")).then_inc(s["tT_ready"], 1)

            def result_out(j):
                act.wait_ge(s["w2_done"], j + 1)
                act.activation(ytile(j), B[j % 2][:, 0:D], ACT.Copy).then_inc(s["acc_ready"], 1)

            slots_out(0)
            for j in range(XT):
                act.wait_ge(s["w1_done"], j + 1)
                if j >= HSLOTS:
                    act.wait_ge(s["w2_done"], j - HSLOTS + 1)
                for f in range(FC):
                    act.activation(hid(j)[:, f * P:(f + 1) * P], B[3 + j % 3][:, f * P:(f + 1) * P],
                                   ACT.Gelu_apprx_tanh, bias=b1w[:, j % WSLOTS, f:f + 1]).then_inc(s["hid_ready"], 1)
                if j % 4 == 1 and 4 * (j // 4 + 1) < XT:
                    slots_out(j // 4 + 1)
                if j >= 1:
                    result_out(j - 1)
            result_out(XT - 1)

            for c in range(CHUNKS):
                act.wait_ge(s["t6_done"], c + 1)
                act.activation(S[5][:, ch(c)], B[c], ACT.Copy).then_inc(s["x2T_ready"], 1)

            def qkv_out(c):
                for k in range(4):
                    act.wait_ge(s["qk_done"], 4 * c + k + 1)
                    act.activation(S[c % 2][:, k * CT:(k + 1) * CT], B[4 + k % 2], ACT.Copy).then_inc(s["qk_ready"], 1)
                for k in range(2):
                    act.wait_ge(s["v1_done"], 2 * c + k + 1)
                    act.activation(vwin(c, k)[:, :, :, 0:HD], B[4 + k].rearrange("p (t h d) -> p t h d", t=TPC, d=HD),
                                   ACT.Copy).then_inc(s["v1_ready"], 1)

            def exp_out(c):
                act.wait_ge(s["e_in"], c + 1)
                act.activation(sco(4 + 2 * (c % 2)), sco(4 + 2 * (c % 2)), ACT.Exp, scale=-1.0).then_inc(s["e_ready"], 1)

            def normed_out(c):
                act.wait_ge(s["t8_done"], c + 1)
                act.activation(S[5][:, ch(c)], B[c], ACT.Identity, bias=vc("lb"), scale=vc("ls")).then_inc(s["fT_ready"], 1)

            def gates_out(c):
                for k in range(4):
                    act.wait_ge(s["in_done"], 4 * c + k + 1)
                    act.activation(S[c][:, k * CT:(k + 1) * CT], B[2 * (k % 2)], ACT.Silu)
                    if c >= 1:
                        act.wait_ge(s["hsw_ready"], 4 * (c - 1) + k + 1)
                    act.activation(PB[:, k * CT:(k + 1) * CT], B[2 * (k % 2) + 1], ACT.Copy).then_inc(s["gb_copied"], 1)

            qkv_out(0)
            qkv_out(1)
            exp_out(0)
            for c in range(CHUNKS):
                for k in range(4):
                    act.wait_ge(s["pt_done"], 4 * c + k + 1)
                    act.activation(PB[:, (c % 2) * T + k * CT:(c % 2) * T + (k + 1) * CT], B[4 + k % 2],
                                   ACT.Copy).then_inc(s["pt_ready"], 1)
                if c + 2 < CHUNKS:
                    qkv_out(c + 2)
                if c + 1 < CHUNKS:
                    exp_out(c + 1)
                if c == 2:
                    normed_out(0)
                    normed_out(1)
                    gates_out(0)
                    gates_out(1)
                act.wait_ge(s["t7_done"], c + 1)
                act.activation(S[5][:, ch(c)], B[4], ACT.Copy).then_inc(s["oT_ready"], 1)

            normed_out(2)
            normed_out(3)
            act.wait_ge(s["gs_ready"], 3)
            act.activation(gt[1][:, :, 0:EG], gt[0][:, :, 0:EG], ACT.Exp).then_inc(s["gs_ready"], 1)
            gates_out(2)
            act.wait_ge(s["cn_done"], 1)
            for k in range(4):
                ins = act.activation(cT[:, ch(k)], B[4 + k][0:E1, :], ACT.Copy)
            ins.then_inc(s["cn_ready"], 1)
            gates_out(3)

        @block.vector
        def _(dve):
            n = [0]

            def did(ins):
                n[0] += 1
                ins.then_inc(s["dve_step"], 1)
                return n[0]

            def settle(back=0):
                dve.wait_ge(s["dve_step"], n[0] - back)

            def step(ins):
                did(ins)
                settle()

            step(dve.memset(S[1][:, 0:1], 0.0))
            step(dve.memset(S[6][:, T:T + 1], 0.0))
            step(dve.memset(DEC[:, :], 0.0))
            step(dve.memset(AM[:, :, :].bitcast(f32), 0.0))
            dve.wait_ge(s["w_vec"], 32)
            a, b = VI["mk"], VI["cr"] + 1
            step(dve.tensor_scalar(vec[:, a:b], vec[:, a:b], 0.0, 1.0, ALU.max, ALU.min))
            dve.wait_ge(s["drv_act"], 1)
            step(dve.tensor_scalar(drv[:, 2:3], vc("bk"), drv[:, 1:2], None, ALU.add))
            step(dve.tensor_scalar(drv[:, 3:4], drv[:, 0:1], -1.0, 1.0, ALU.mult, ALU.add))
            step(dve.tensor_scalar(DEC[:, :], DEC[:, :], drv[:, 0:1], None, ALU.add))
            dve.tensor_scalar(drv[:, 4:5], vc("bv"), drv[:, 3:4], None, ALU.mult).then_inc(s["drv_ready"], 1)

            def stats(k, c, src):
                for t in range(c * TPC, (c + 1) * TPC):
                    did(dve.bn_stats(st6[:, t, :], src[:, t, :]))
                settle()
                for t in range(c * TPC, (c + 1) * TPC):
                    ins = dve.bn_aggr(MV[k][:, t, :], st6[:, t, :])
                ins.then_inc(s["ln_stats"], 1)

            def normed(k, c, dst, src, r, sem_=None):
                for t in range(c * TPC, (c + 1) * TPC):
                    ins = dve.tensor_scalar(dst[:, t, :], src[:, t, :], MV[k][:, t, 0:1], r[:, t:t + 1],
                                            ALU.subtract, ALU.mult)
                    if sem_ and t == (c + 1) * TPC - 1:
                        ins.then_inc(sem_, 1)
                    else:
                        did(ins)

            for c in range(CHUNKS):
                if c == 0:
                    dve.wait_ge(s["w_pe"], 32)
                step(dve.tensor_tensor(tokv(6)[:, tl(c), :], tokv(6)[:, tl(c), :], rows_over("tokb", TPC), ALU.add))
                dve.wait_ge(emb_in[c], 16 * TPC)
                dve.tensor_tensor(H[:, tl(c), :], H[:, tl(c), :], tokv(6)[:, tl(c), :], ALU.add).then_inc(s["h_ready"], 1)
                dve.wait_ge(s["h_ready"], c + 1)
                stats(0, c, H)
            dve.wait_ge(s["w_sel"], 16)
            step(dve.tensor_copy(SELR[:, 0:8, :], PB[:, 0:1024].rearrange("p (a b) -> p a b", b=P)))
            dve.wait_ge(s["w_misc"], 64)
            dve.wait_ge(s["w_sel"], 16)
            step(dve.tensor_copy(SELR[:, 8:16, :], PB[:, 1024:2048].rearrange("p (a b) -> p a b", b=P)))
            dve.tensor_copy(IDR[:, :], ID[:, :]).then_inc(s["selr_ready"], 1)
            for c in range(CHUNKS):
                dve.wait_ge(s["ln_rstd"], c + 1)
                normed(0, c, tokv(0), H, RB, s["xh_ready"])
            for c in range(CHUNKS):
                dve.wait_ge(s["hT_ready"], c + 1)
                now, before = hT[:, 1 + c * CT:1 + (c + 1) * CT], hT[:, ch(c)]
                step(dve.tensor_tensor(S[0][:, ch(c)], now, before, ALU.subtract))
                for i, m in ((2, "mk"), (3, "mv"), (4, "mr")):
                    ins = dve.scalar_tensor_tensor(S[i][:, ch(c)], S[0][:, ch(c)], vc(m), before, ALU.mult, ALU.add)
                    if i < 4:
                        did(ins)
                ins.then_inc(s["mix_ready"], 1)
            dve.wait_ge(s["h_ready"], CHUNKS)
            step(dve.memset(S[6][:, 0:1], 0.0))
            for c in range(CHUNKS):
                dve.wait_ge(s["wv_ready"], c + 1)
                step(dve.tensor_tensor_scan(S[6][:, 1 + c * CT:1 + (c + 1) * CT], DEC[:, :], S[2][:, ch(c)],
                                            S[6][:, c * CT:c * CT + 1], ALU.mult, ALU.add))
                v = S[3][:, ch(c)]
                step(dve.tensor_tensor(v, v, S[6][:, ch(c)], ALU.subtract))
                step(dve.tensor_tensor(v, v, S[5][:, ch(c)], ALU.mult))
                dve.tensor_tensor(v, v, S[6][:, ch(c)], ALU.add).then_inc(s["rec_ready"], 1)
            for c in range(CHUNKS):
                dve.wait_ge(s["woo_done"], c + 1)
                dve.wait_ge(s["x0b_ready"], c + 1)
                dve.scalar_tensor_tensor(X[:, tl(c), :], bt4(c), 0.5, X[:, tl(c), :], ALU.mult, ALU.add).then_inc(s["x1_ready"], 1)
                dve.wait_ge(s["x1_ready"], c + 1)
                stats(1, c, X)
            for c in range(CHUNKS):
                dve.wait_ge(s["ln_rstd"], 1 * CHUNKS + c + 1)
                normed(1, c, tokv(5), X, RA[1], s["xh2_ready"])
            for c in range(CHUNKS):
                dve.wait_ge(s["h2T_ready"], c + 1)
                now, before = hT[:, 1 + c * CT:1 + (c + 1) * CT], hT[:, ch(c)]
                step(dve.tensor_tensor(S[0][:, ch(c)], now, before, ALU.subtract))
                did(dve.scalar_tensor_tensor(S[4][:, ch(c)], S[0][:, ch(c)], vc("cr"), before, ALU.mult, ALU.add))
                dve.scalar_tensor_tensor(S[3][:, ch(c)], S[0][:, ch(c)], vc("ck"), before, ALU.mult,
                                         ALU.add).then_inc(s["mix2_ready"], 1)
            dve.wait_ge(s["w_gp"], 32)
            for g in range(2):
                did(dve.tensor_reduce(gpm[:, g, :], V[:, g * T:(g + 1) * T].rearrange("p (g n) -> p n g", n=WS), AX.X, ALU.add))
            settle()
            dve.tensor_scalar(gpm[:, :, :], gpm[:, :, :], 1.0 / G1, None, ALU.mult).then_inc(s["gpm_ready"], 1)
            for c in range(CHUNKS):
                dve.wait_ge(s["vv2_done"], c + 1)
                dve.wait_ge(s["tc_ready"], c + 1)
                dve.scalar_tensor_tensor(S[6][:, ch(c)], B[c], vc("bcv"), S[2][:, ch(c)], ALU.add,
                                         ALU.mult).then_inc(s["q_ready"], 1)
            for c in range(CHUNKS):
                dve.wait_ge(s["t3_done"], c + 1)
                dve.wait_ge(s["hx_ready"], c + 1)
                dve.scalar_tensor_tensor(H[:, tl(c), :], bt4(4 + c), 0.5, H[:, tl(c), :], ALU.mult, ALU.add).then_inc(s["h1_ready"], 1)
                dve.wait_ge(s["h1_ready"], c + 1)
                stats(2, c, H)
            for c in range(CHUNKS):
                dve.wait_ge(s["ln_rstd"], 2 * CHUNKS + c + 1)
                normed(2, c, X, H, RA[2], s["xh3_ready"])
            def maxes(u, a, b):
                for i in range(a, b):
                    for h in range(2):
                        m = u * 32 + 2 * i + h
                        dve.wait_ge(s["mxp_done"], m + 1)
                        kq, t = divmod(i, TPC)
                        dve.tensor_reduce(mq[:, 2 * t + h, kq:kq + 1], B[m % 3], AX.X,
                                          ALU.max).then_inc(s["mxr_done"], 1)

            for c in range(CHUNKS):
                dve.wait_ge(s["qhi_ready"], c + 1)
                dve.scalar_tensor_tensor(QLO[:, ch(c)], B[4], vc("bq"), QHI[:, ch(c)].bitcast(f32), ALU.add,
                                         ALU.subtract).then_inc(s["qlo_ready"], 1)
                dve.wait_ge(s["khi_ready"], c + 1)
                dve.scalar_tensor_tensor(KLO[:, c % 2, :], B[5], vc("bkf"), KHI[:, c % 2, :].bitcast(f32), ALU.add,
                                         ALU.subtract).then_inc(s["klo_ready"], 1)
                dve.wait_ge(s["vt_done"], c + 1)
                if c == 0:
                    dve.wait_ge(s["ones_ready"], 1)
                dve.tensor_tensor(val(c)[:, :, :, 0:HD], B[3].rearrange("p (t h d) -> p t h d", t=TPC, d=HD),
                                  rowv("bvf").rearrange("p (h d) -> p h d", d=HD).unsqueeze(1).to_broadcast([P, TPC, HEADS, HD]),
                                  ALU.add).then_inc(s["vals_ready"], 1)
                if c >= 1:
                    maxes(0, (c - 1) * TPC, c * TPC)
            maxes(0, (CHUNKS - 1) * TPC, CHUNKS * TPC)

            ON = tokv(6)

            def negated(u):
                dve.wait_ge(s["mxr_done"], 32 * (u + 1))
                step(dve.tensor_reduce(nm[:, :], mq[:, :, :], AX.X, ALU.max, negate=True))
                if u >= 1:
                    dve.wait_ge(s["qe_done"], u)
                nmv = nm[:, :].rearrange("p (t h) -> p t h", h=2)
                step(dve.tensor_copy(AM[:, :, 48::64], nmv))
                dve.tensor_tensor(AM[:, :, 49::64], nmv, AM[:, :, 48::64].bitcast(f32), ALU.subtract).then_inc(s["nm_ready"], 1)

            def normalize(u):
                dve.wait_ge(s["dsum_done"], u + 1)
                o = B[7][:, 0:TPC * 2 * (HD + 1)].rearrange("p (t h e) -> p t h e", t=TPC, h=2)
                den = oden[:, 0, 0:2 * TPC].rearrange("p (t h) -> p t h", h=2)
                step(dve.reciprocal(den, o[:, :, :, HD]))
                j = u % PAIRS
                dve.tensor_tensor(ON[:, 0:TPC, 2 * j * HD:2 * (j + 1) * HD].rearrange("p t (h d) -> p t h d", h=2),
                                  o[:, :, :, 0:HD], den.unsqueeze(3).to_broadcast([P, TPC, 2, HD]),
                                  ALU.mult).then_inc(s["on_ready"], 1)

            def projected(q):
                dve.wait_ge(s["wo_done"], q + 1)
                dve.wait_ge(s["xb_ready"], q + 1)
                dve.tensor_tensor(tokv(4)[:, tl(q), :], bt4(7), X[:, tl(q), :], ALU.add).then_inc(s["y_ready"], 1)

            def stats3(q):
                dve.wait_ge(s["y_ready"], q + 1)
                stats(3, q, tokv(4))

            def normed3(q):
                dve.wait_ge(s["ln_rstd"], 3 * CHUNKS + q + 1)
                normed(3, q, X, tokv(4), RA[3], s["xh4_ready"])

            negated(0)
            maxes(1, 0, AHEAD)
            for u in range(UNITS):
                more = u + 1 < UNITS
                if more:
                    maxes(u + 1, AHEAD, AHEAD + 3)
                if u >= 1:
                    normalize(u - 1)
                if more:
                    maxes(u + 1, AHEAD + 3, AHEAD + 8)
                if u >= 1 and u % PAIRS == 0:
                    projected(u // PAIRS - 1)
                if u >= PAIRS and u % PAIRS == 1:
                    stats3(u // PAIRS - 1)
                if u >= PAIRS and u % PAIRS == 2:
                    normed3(u // PAIRS - 1)
                if more:
                    maxes(u + 1, AHEAD + 8, 16)
                    negated(u + 1)
                if u + 2 < UNITS:
                    maxes(u + 2, 0, AHEAD)
            normalize(UNITS - 1)
            projected(CHUNKS - 1)
            stats3(CHUNKS - 1)
            normed3(CHUNKS - 1)

            def over(x, k):
                return x.unsqueeze(2).to_broadcast([P, TILES, k])

            def prio(k):
                a0, _ = RO["prio"]
                return row[:, a0 + E0 - k:a0 + E0].unsqueeze(1).to_broadcast([P, TILES, k])

            def first_max(dst, src, mx, k, tmp):
                step(dve.tensor_reduce(mx, src, AX.X, ALU.max))
                step(dve.tensor_tensor(tmp, src, over(mx, k), ALU.is_equal))
                step(dve.tensor_tensor(tmp, tmp, prio(k), ALU.mult))
                step(dve.tensor_reduce(gs[:, 3, :], tmp, AX.X, ALU.max))
                step(dve.tensor_tensor(dst, tmp, over(gs[:, 3, :], k), ALU.is_equal))

            def softmaxed(src, k, ready, back):
                step(dve.tensor_reduce(gs[:, 0, :], src, AX.X, ALU.max))
                dve.tensor_tensor(gt[0][:, :, 0:k], src, over(gs[:, 0, :], k), ALU.subtract).then_inc(ready, 1)
                dve.wait_ge(ready, back)
                step(dve.tensor_reduce(gs[:, 1, :], gt[1][:, :, 0:k], AX.X, ALU.add))
                step(dve.reciprocal(gs[:, 1, :], gs[:, 1, :]))
                step(dve.tensor_tensor(gt[1][:, :, 0:k], gt[1][:, :, 0:k], over(gs[:, 1, :], k), ALU.mult))

            dve.wait_ge(s["gl_done"], 1)
            step(dve.tensor_tensor(gt[2][:, :, :], B[4][:, 0:TILES * E0].rearrange("p (t e) -> p t e", e=E0),
                                   rows_over("gateb", TILES), ALU.add))
            softmaxed(gt[2][:, :, :], E0, s["gs_ready"], 2)
            first_max(cw[:, :, :], gt[1][:, :, :], gs[:, 0, :], E0, gt[3][:, :, :])
            dve.tensor_copy(RA[3][:, :], gs[:, 0, :]).then_inc(s["cw_ready"], 1)
            dve.wait_ge(s["cw_ready"], 1)
            dve.tensor_tensor(gt[0][:, :, :], cw[:, :, :], over(gs[:, 0, :], E0), ALU.mult).then_inc(s["cw_ready"], 1)
            before = B[5][:, 0:TILES * E0].rearrange("p (t e) -> p t e", e=E0)
            count = B[5][:, TILES * E0:2 * TILES * E0].rearrange("p (t e) -> p t e", e=E0)
            dve.wait_ge(s["rank_done"], 1)
            step(dve.tensor_copy(gt[1][:, :, :], count))
            a, b = gt[1], gt[2]
            for k in (1, 2, 4, 8):
                did(dve.tensor_copy(b[:, 0:k, :], a[:, 0:k, :]))
                step(dve.tensor_tensor(b[:, k:TILES, :], a[:, k:TILES, :], a[:, 0:TILES - k, :], ALU.add))
                a, b = b, a
            total = a[:, TILES - 1, :]
            need, run, tmp = nm[:, 0:E0], mn[:, 0:E0], mn[:, E0:2 * E0]
            full = gt[3][:, :, :].rearrange("p t e -> p (t e)").rearrange("p (e k) -> p e k", k=TILES)
            step(dve.tensor_tensor(full, total.unsqueeze(2).to_broadcast([P, E0, TILES]),
                                   rowv("full").unsqueeze(1).to_broadcast([P, E0, TILES]), ALU.is_gt))
            step(dve.tensor_reduce(need, full, AX.X, ALU.add))
            step(dve.tensor_tensor(a[:, :, :], a[:, :, :], count, ALU.subtract))
            did(dve.tensor_tensor(a[:, :, :], a[:, :, :], before, ALU.add))
            step(dve.tensor_copy(run, need))
            for k in (1, 2, 4):
                did(dve.tensor_copy(tmp[:, 0:k], run[:, 0:k]))
                step(dve.tensor_tensor(tmp[:, k:E0], run[:, k:E0], run[:, 0:E0 - k], ALU.add))
                run, tmp = tmp, run
            step(dve.tensor_tensor(tmp, run, need, ALU.subtract))
            step(dve.tensor_scalar(tmp, tmp, float(P), None, ALU.mult))
            step(dve.tensor_tensor(a[:, :, :], a[:, :, :], tmp.unsqueeze(1).to_broadcast([P, TILES, E0]), ALU.add))
            step(dve.tensor_tensor(a[:, :, :], a[:, :, :], cw[:, :, :], ALU.mult))
            step(dve.tensor_reduce(gs[:, 1, :], a[:, :, :], AX.X, ALU.add))
            dve.tensor_copy(slot[:, :], gs[:, 1, :]).then_inc(s["slot_ready"], 1)
            ends = xm[:, 0:XT]
            past = S[6][:, 0:XT * E0].rearrange("p (j e) -> p j e", e=E0)
            step(dve.tensor_tensor(past, rowv("tileno").unsqueeze(2).to_broadcast([P, XT, E0]),
                                   run.unsqueeze(1).to_broadcast([P, XT, E0]), ALU.is_ge))
            step(dve.tensor_reduce(ends, past, AX.X, ALU.add))
            step(dve.tensor_scalar(ends, ends, float(E0 - 1), None, ALU.min))
            step(dve.tensor_copy(tex[:, :], ends))
            for c in range(CHUNKS):
                dve.wait_ge(s["acc0_done"], c + 1)
                dve.tensor_tensor(H[:, tl(c), :], H[:, tl(c), :], bt4(c), ALU.add).then_inc(s["acc0_ready"], 1)
            dve.wait_ge(s["w_moe"], 32)
            dve.wait_ge(s["sc_in"], 16 * TILES)
            for j in range(XT):
                e = dve.value_load(tex[0:1, j:j + 1], min_val=0, max_val=E0 - 1)
                if j >= WSLOTS:
                    dve.wait_ge(s["w2_done"], j - WSLOTS + 1)
                did(dve.tensor_copy(wexp(j)[:, 0:FF], SS[:, bass.ds(e * FF, FF)]))
                did(dve.tensor_copy(wexp(j)[:, FF:2 * FF], SS[:, bass.ds(e * FF + 2 * SW, FF)]))
                settle()
                dve.tensor_copy(b1w[:, j % WSLOTS, :], b1c[:, bass.ds(e * FC, FC)]).then_inc(s["wc_ready"], 1)
            for c in range(CHUNKS):
                dve.wait_ge(emb_in[c], 2 * 16 * TPC)
                dve.wait_ge(s["acc0_ready"], CHUNKS)
                for t in range(c * TPC, (c + 1) * TPC):
                    ins = dve.scalar_tensor_tensor(H[:, t, :], V[:, t * D:(t + 1) * D], RA[3][:, t:t + 1], H[:, t, :],
                                                   ALU.mult, ALU.add)
                    if t < (c + 1) * TPC - 1:
                        did(ins)
                ins.then_inc(s["h2_ready"], 1)
                dve.wait_ge(s["h2_ready"], c + 1)
                settle()
                stats(4, c, H)
                if c >= 1:
                    dve.wait_ge(s["ln_rstd"], 4 * CHUNKS + c)
                    normed(4, c - 1, X, H, RA[4], s["xh5_ready"])
            dve.wait_ge(s["ln_rstd"], 5 * CHUNKS)
            normed(4, CHUNKS - 1, X, H, RA[4], s["xh5_ready"])

            did(dve.memset(V[:, :].rearrange("p (x d) -> p x d", d=32)[:, :, HD:HD + 1], 1.0))
            for c in range(CHUNKS):
                dve.wait_ge(s["x2T_ready"], c + 1)
                did(dve.tensor_reduce(xmc[:, c, :], S[5][:, ch(c)].rearrange("p (w n) -> p n w", n=WS), AX.X, ALU.add))
            settle()
            dve.tensor_reduce(xm[:, :], xmc[:, :, :].rearrange("p c n -> p n c"), AX.X, ALU.add).then_inc(s["xm_ready"], 1)
            dve.wait_ge(s["gm_done"], 1)
            did(dve.tensor_scalar(qm[:, :, :], B[6][:, 0:2 * WS].rearrange("p (g n) -> p g n", g=2), WS / T, None, ALU.mult))
            step(dve.tensor_scalar(km[:, :, :], B[6][:, 2 * WS:4 * WS].rearrange("p (g n) -> p g n", g=2), WS / T, None, ALU.mult))
            step(dve.tensor_tensor(qm[:, :, :], qm[:, :, :], gpm[:, :, :], ALU.mult))
            step(dve.tensor_reduce(gq[:, 0:2], qm[:, :, :], AX.X, ALU.add))
            dve.wait_ge(s["gate_sig"], 1)
            step(dve.scalar_tensor_tensor(gq[:, 2:4], gq[:, 0:2], D ** -0.5, gat[:, :], ALU.mult, ALU.mult))
            dve.tensor_copy(gqb[:, :, :], gq[:, 2:4].unsqueeze(2).to_broadcast([P, 2, P])).then_inc(s["gq_ready"], 1)
            dve.wait_ge(s["gb_done"], 1)
            btv = BT[:, :, :].rearrange("p h m -> p (h m)")
            dve.wait_ge(s["w_lb"], 32)
            for j in range(4):
                ins = dve.tensor_tensor(btv[:, j * P:(j + 1) * P], btv[:, j * P:(j + 1) * P], B[j][:, 0:P], ALU.add)
                if j < 3:
                    did(ins)
            ins.then_inc(s["bt_ready"], 1)
            dve.wait_ge(s["bt_ready"], 1)

            W = X[:, :, :].rearrange("p t d -> p (t d)").rearrange("p (r m) -> p r m", m=WS)

            def window_out(c):
                dve.wait_ge(s["ov_done"], c + 1)
                ob = tokv(4 + 2 * (c % 2))[:, 0:TPC, :].rearrange("p t (g j d) -> p t g j d", g=2, d=HD)
                for g in range(2):
                    o = B[6 + g].rearrange("p (t j e) -> p t j e", t=TPC, j=4)
                    den = oden[:, g, :].rearrange("p (t j) -> p t j", j=4)
                    step(dve.reciprocal(den, o[:, :, :, HD]))
                    ins = dve.tensor_tensor(ob[:, :, g, :, :], o[:, :, :, 0:HD],
                                            den.unsqueeze(3).to_broadcast([P, TPC, 4, HD]), ALU.mult)
                    if g == 0:
                        did(ins)
                ins.then_inc(s["o_ready"], 1)

            def residual3(c):
                dve.wait_ge(s["pr_done"], c + 1)
                dve.wait_ge(s["h3b_ready"], c + 1)
                dve.tensor_tensor(H[:, tl(c), :], H[:, tl(c), :], bt4(5), ALU.add).then_inc(s["h3_ready"], 1)
                dve.wait_ge(s["h3_ready"], c + 1)
                stats(5, c, H)

            def normed5(c):
                dve.wait_ge(s["ln_rstd"], 5 * CHUNKS + c + 1)
                normed(5, c, tokv(5), H, RB, s["xh6_ready"])

            for c in range(CHUNKS):
                ns = sco(2 + c % 2)
                for j in range(4):
                    dve.wait_ge(s["s_done"], 4 * c + j + 1)
                    if c >= 2:
                        dve.wait_ge(s["p1_ready"], c - 1)
                    ins = dve.scalar_tensor_tensor(S[2 + c % 2][:, j * CT:(j + 1) * CT].rearrange("p (t x) -> p t x", t=TPC),
                                                   B[j].rearrange("p (t x) -> p t x", t=TPC), -(D ** -0.5),
                                                   btv[:, j * P:(j + 1) * P].unsqueeze(1).to_broadcast([P, TPC, P]),
                                                   ALU.mult, ALU.subtract)
                    ins.then_inc(s["ns_ready"], 1)
                dve.wait_ge(s["ns_ready"], 4 * (c + 1))
                if c >= 1:
                    dve.wait_ge(s["e_in"], c)
                dve.tensor_reduce(mn[:, :], ns, AX.X, ALU.min).then_inc(s["mn_ready"], 1)
                if c >= 2:
                    residual3(c - 2)
                for r in range(32):
                    did(dve.max(t8[:, 0, r, :], ns[:, r, :]))
                if c >= 2:
                    normed5(c - 2)
                settle()
                for r in range(32):
                    did(dve.match_replace(W[:, r, :], t8[:, 0, r, :], ns[:, r, :], NEG))
                for r in range(32):
                    settle(31)
                    did(dve.max(t8[:, 1, r, :], W[:, r, :]))
                for r in range(32):
                    settle(31)
                    did(dve.match_replace(W[:, r, :], t8[:, 1, r, :], W[:, r, :], NEG))
                for r in range(32):
                    settle(31)
                    did(dve.max(t8[:, 2, r, :], W[:, r, :]))
                settle()
                if c >= 1:
                    window_out(c - 1)
                dve.wait_ge(s["e_in"], c + 1)
                kept = dve.tensor_tensor(ns, ns, t8[:, 2, :, DROP - 16:DROP - 15].to_broadcast([P, 32, WS]), ALU.is_le)
                if c < CHUNKS - 1:
                    kept.then_inc(s["kept"], 1)
                else:
                    step(kept)
                    dve.wait_ge(s["e_ready"], CHUNKS)
                    ex = sco(4 + 2 * (c % 2))
                    dve.tensor_tensor(ex, ex, ns, ALU.mult).then_inc(s["p1_ready"], 1)
            residual3(CHUNKS - 2)
            window_out(CHUNKS - 1)
            residual3(CHUNKS - 1)

            normed5(2)
            normed5(3)
            dve.wait_ge(s["g2_done"], 1)
            g2 = B[5][:, 0:TILES * (2 + E1)].rearrange("p (t e) -> p t e", e=2 + E1)
            step(dve.tensor_tensor(gt[2][:, :, 0:2], g2[:, :, 0:2], rows_over("gb", TILES), ALU.add))
            step(dve.tensor_tensor(gt[3][:, :, :], g2[:, :, 2:2 + E1], rows_over("eb", TILES), ALU.add))
            v = gs[:, 2, :]
            step(dve.tensor_tensor(v, gt[2][:, :, 1], gt[2][:, :, 0], ALU.is_gt))
            grp = gpick
            step(dve.tensor_copy(grp[:, :, 1], v))
            step(dve.tensor_scalar(grp[:, :, 0], v, -1.0, 1.0, ALU.mult, ALU.add))
            did(dve.tensor_tensor(gt[3][:, :, 0:EG], gt[3][:, :, 0:EG], over(grp[:, :, 0], EG), ALU.mult))
            step(dve.tensor_tensor(gt[3][:, :, EG:E1], gt[3][:, :, EG:E1], over(grp[:, :, 1], EG), ALU.mult))
            step(dve.tensor_tensor(gt[2][:, :, 0:EG], gt[3][:, :, 0:EG], gt[3][:, :, EG:E1], ALU.add))
            softmaxed(gt[2][:, :, 0:EG], EG, s["gs_ready"], 4)
            pr, o1, o2, tmp = gt[1][:, :, 0:EG], gt[2][:, :, 0:EG], gt[2][:, :, EG:E1], gt[3][:, :, 0:EG]
            first_max(o1, pr, gs[:, 0, :], EG, tmp)
            step(dve.scalar_tensor_tensor(pr, o1, -4.0, pr, ALU.mult, ALU.add))
            first_max(o2, pr, gs[:, 1, :], EG, tmp)
            step(dve.tensor_tensor(gs[:, 2, :], gs[:, 0, :], gs[:, 1, :], ALU.add))
            step(dve.tensor_scalar(gs[:, 2, :], gs[:, 2, :], 1e-8, None, ALU.add))
            step(dve.reciprocal(gs[:, 2, :], gs[:, 2, :]))
            did(dve.tensor_tensor(gs[:, 0, :], gs[:, 0, :], gs[:, 2, :], ALU.mult))
            step(dve.tensor_tensor(gs[:, 1, :], gs[:, 1, :], gs[:, 2, :], ALU.mult))
            did(dve.tensor_tensor(tmp, o1, over(gs[:, 0, :], EG), ALU.mult))
            did(dve.tensor_tensor(pr, o2, over(gs[:, 1, :], EG), ALU.mult))
            step(dve.tensor_tensor(o1, o1, o2, ALU.add))
            step(dve.tensor_tensor(tmp, tmp, pr, ALU.add))
            for g in range(2):
                did(dve.tensor_tensor(gt[0][:, :, g * EG:(g + 1) * EG], o1, over(grp[:, :, g], EG), ALU.mult))
                ins = dve.tensor_tensor(cw[:, :, g * EG:(g + 1) * EG], tmp, over(grp[:, :, g], EG), ALU.mult)
                if g == 0:
                    did(ins)
            ins.then_inc(s["c2_ready"], 1)
            dve.wait_ge(s["c2_ready"], 1)
            OA, OBB = tokv(6)[:, 0:TPC, :], tokv(6)[:, TPC:2 * TPC, :]
            for c in range(CHUNKS):
                dve.wait_ge(s["sh_done"], c + 1)
                step(dve.tensor_tensor(H[:, tl(c), :], H[:, tl(c), :], rows_over("shb", TPC), ALU.add))
                dve.tensor_tensor(H[:, tl(c), :], H[:, tl(c), :], bt4(4), ALU.add).then_inc(s["xev_ready"], 1)
                dve.wait_ge(s["xev_ready"], UNITS + c + 1)
                for t in range(TPC):
                    g = c * TPC + t
                    dve.wait_ge(s["ex_done"], g + 1)
                    b0 = 6 if t % 2 == 0 else 2
                    for e in range(E1):
                        dst = (OA if e % 2 == 0 else OBB)[:, t, :]
                        src = PS[:, b0 + e // 4, (e % 4) * D:(e % 4 + 1) * D]
                        if e < 2:
                            did(dve.tensor_scalar(dst, src, cw[:, g, e:e + 1], None, ALU.mult))
                            continue
                        settle(1)
                        ins = dve.scalar_tensor_tensor(dst, src, cw[:, g, e:e + 1], dst, ALU.mult, ALU.add)
                        if e < E1 - 1:
                            did(ins)
                    ins.then_inc(s["cb_ready"], 1)
                    dve.wait_ge(s["cb_ready"], g + 1)
                step(dve.tensor_tensor(OA, OA, OBB, ALU.add))
                dve.tensor_tensor(H[:, tl(c), :], H[:, tl(c), :], OA, ALU.add).then_inc(s["fin_ready"], 1)

        @block.tensor
        def _(pe):
            def transposes(dst, src, done):
                for t in range(TPC):
                    ins = pe.transpose(dst[:, t * P:(t + 1) * P], src(t), ID[:, :])
                ins.then_inc(done, 1)

            def w(i):
                return wr[:, i * D:(i + 1) * D]

            pe.wait_ge(s["w_misc"], 64)
            for c in range(CHUNKS):
                pe.wait_ge(s["xh_ready"], c + 1)
                transposes(B[c], lambda t: tokv(0)[:, c * TPC + t, :], s["t1_done"])
            pe.wait_ge(s["w_rwkv"], 16)
            for c in range(CHUNKS):
                pe.wait_ge(s["mix_ready"], c + 1)
                if c >= 2:
                    pe.wait_ge(s["gate_ready"], c - 1)
                pe.matmul(B[4 + c % 2], w(0), S[2][:, ch(c)], start=True, stop=True).then_inc(s["k_done"], 1)
                if c >= 2:
                    pe.wait_ge(s["wv_ready"], c - 1)
                pe.matmul(B[6 + c % 2], w(1), S[3][:, ch(c)], start=True, stop=True).then_inc(s["v_done"], 1)
                pe.matmul(B[c], w(2), S[4][:, ch(c)], start=True, stop=True).then_inc(s["r_done"], 1)
            for c in range(CHUNKS):
                pe.wait_ge(s["z_ready"], c + 1)
                for t in range(TPC):
                    g = (c * TPC + t) * P
                    ins = pe.matmul(B[c][:, t * D:(t + 1) * D], S[0][:, g:g + P], w(3), start=True, stop=True)
                ins.then_inc(s["woo_done"], 1)
            for c in range(CHUNKS):
                pe.wait_ge(s["xh2_ready"], c + 1)
                transposes(B[4 + c], lambda t: tokv(5)[:, c * TPC + t, :], s["t2_done"])
            pe.wait_ge(s["w_ck"], 32)

            def ckr(c):
                pe.wait_ge(s["mix2_ready"], c + 1)
                if c == 0:
                    pe.wait_ge(s["h2T_ready"], CHUNKS)
                for f in range(FC):
                    if c >= 1:
                        pe.wait_ge(s["gelu_ready"], FC * (c - 1) + f + 1)
                    pe.matmul(B[4 + f], wck[:, f * P:(f + 1) * P], S[3][:, ch(c)], start=True, stop=True).then_inc(s["ck_done"], 1)
                pe.wait_ge(s["x1_ready"], c + 1)
                pe.matmul(B[c], w(4), S[4][:, ch(c)], start=True, stop=True).then_inc(s["cr_done"], 1)

            ckr(0)
            for c in range(CHUNKS):
                if c + 1 < CHUNKS:
                    ckr(c + 1)
                pe.wait_ge(s["gelu_ready"], FC * (c + 1))
                pe.wait_ge(s["tc_ready"], c + 1)
                for f in range(FC):
                    ins = pe.matmul(B[c], wcv[:, f, :], G[:, c % 2, f, :], start=f == 0, stop=f == FC - 1)
                ins.then_inc(s["vv2_done"], 1)
            for c in range(CHUNKS):
                pe.wait_ge(s["q_ready"], c + 1)
                transposes(B[4 + c], lambda t: S[6][:, (c * TPC + t) * P:(c * TPC + t + 1) * P], s["t3_done"])
            for c in range(CHUNKS):
                pe.wait_ge(s["xh3_ready"], c + 1)
                transposes(B[c], lambda t: X[:, c * TPC + t, :], s["t4_done"])
            def qsel(u, last):
                q, j = divmod(u, PAIRS)
                pe.matmul(B[7], SELR[:, j, :], QHI[:, ch(q)], start=True, stop=False)
                return pe.matmul(B[7], SELR[:, 4 + j, :], QLO[:, ch(q)], start=False, stop=last)

            def maxes(u, i, heads=(0, 1)):
                j = u % PAIRS
                kq, t = divmod(i, TPC)
                for h in heads:
                    m = 32 * u + 2 * i + h
                    if m >= 3:
                        pe.wait_ge(s["mxr_done"], m - 2)
                    pe.matmul(B[m % 3], QM[u % 2][:, h, t * P:(t + 1) * P], KST[:, j, kq * CT:(kq + 1) * CT],
                              start=True, stop=True).then_inc(s["mxp_done"], 1)

            pe.wait_ge(s["w_ffn"], 32)
            pe.wait_ge(s["selr_ready"], 1)
            pe.wait_ge(s["h1_ready"], CHUNKS)
            for c in range(CHUNKS):
                pe.wait_ge(s["x1T_ready"], c + 1)
                if c >= 1:
                    pe.wait_ge(s["qlo_ready"], c)
                pe.matmul(B[4], wf[:, 0:D], S[0][:, ch(c)], start=True, stop=True).then_inc(s["q_done"], 1)
                if c >= 1:
                    pe.wait_ge(s["klo_ready"], c)
                pe.matmul(B[5], wf[:, D:2 * D], S[0][:, ch(c)], start=True, stop=True).then_inc(s["kk_done"], 1)
                if c == 0:
                    pe.wait_ge(s["x1T_ready"], CHUNKS)
                else:
                    pe.wait_ge(s["vals_ready"], c)
                for t in range(TPC):
                    g = (c * TPC + t) * P
                    ins = pe.matmul(B[3][:, t * D:(t + 1) * D], S[0][:, g:g + P], wf[:, 2 * D:3 * D], start=True, stop=True)
                ins.then_inc(s["vt_done"], 1)
                if c >= 1:
                    pe.wait_ge(s["kst_ready"], PAIRS * c)
                    for i in ((c - 1) * TPC, (c - 1) * TPC + 1):
                        maxes(0, i)
                pe.wait_ge(s["klo_ready"], c + 1)
                for j in range(PAIRS):
                    i = PAIRS * c + j
                    if i >= 2:
                        pe.wait_ge(s["kst_ready"], i - 1)
                    pe.matmul(B[6 + j % 2], SELR[:, 8 + j, :], KHI[:, c % 2, :], start=True, stop=False)
                    pe.matmul(B[6 + j % 2], SELR[:, 12 + j, :], KLO[:, c % 2, :], start=False, stop=True).then_inc(s["ksel_done"], 1)
                if c == 0:
                    pe.wait_ge(s["kst_ready"], PAIRS)
                    pe.wait_ge(s["qlo_ready"], 1)
                    qsel(0, True).then_inc(s["qsel_done"], 1)
                    pe.wait_ge(s["zero_ready"], 1)
                    pe.wait_ge(s["qm_ready"], 1)
                else:
                    for i in ((c - 1) * TPC + 2, (c - 1) * TPC + 3):
                        maxes(0, i)
            pe.wait_ge(s["kst_ready"], PAIRS * CHUNKS)
            for i in range((CHUNKS - 1) * TPC, CHUNKS * TPC):
                maxes(0, i)

            def scores(u, k, heads=(0, 1)):
                m, j = u * TILES + k, u % PAIRS
                for h in heads:
                    b = 2 * m + h
                    if b >= 3:
                        pe.wait_ge(s["p_ready"], b - 2)
                    pe.matmul(B[3 + b % 3], KST[:, j, k * P:(k + 1) * P], QE[u % 2][:, h, :], start=True,
                              stop=True).then_inc(s["st_done"], 1)

            def weigh(u, kp):
                j = u % PAIRS
                pe.wait_ge(s["p_ready"], 2 * (u * TILES + 2 * kp + 2))
                if kp == 0 and u >= 1:
                    pe.wait_ge(s["xev_ready"], u)
                for h in range(2):
                    for par in range(2):
                        k = 2 * kp + par
                        q = 32 * (2 * h + par)
                        ins = pe.matmul(B[6][q:q + 32, :], valh(k, 2 * j + h), prob(u * TILES + k)[:, h, :],
                                        start=kp == 0, stop=kp == TILES // 2 - 1, tile_position=(0, q))
                ins.then_inc(s["av_done"], 1)

            def attended(q):
                pe.wait_ge(s["on_ready"], PAIRS * (q + 1))
                transposes(B[7], lambda t: tokv(6)[:, t, :], s["ot_done"])

            def project(q):
                pe.wait_ge(s["ot_ready"], q + 1)
                for t in range(TPC):
                    ins = pe.matmul(B[7][:, t * D:(t + 1) * D], S[5][:, CT + t * P:CT + (t + 1) * P], wof[:, :],
                                    start=True, stop=True)
                ins.then_inc(s["wo_done"], 1)

            def dsum(u):
                pe.wait_ge(s["xev_ready"], u + 1)
                n = 2 * (HD + 1)
                for t in range(TPC):
                    ins = pe.matmul(B[7][:, t * n:(t + 1) * n], S[5][:, t * P:(t + 1) * P], SELO[:, :], start=True, stop=True)
                ins.then_inc(s["dsum_done"], 1)

            def with_max(u):
                pe.wait_ge(s["nm_ready"], u + 1)
                qsel(u, False)
                for t in range(TPC):
                    ins = pe.matmul(B[7][:, t * P:(t + 1) * P], AM[:, t, :], IDR[:, :], start=False, stop=t == TPC - 1)
                ins.then_inc(s["qe_done"], 1)

            pe.wait_ge(s["vals_ready"], CHUNKS)
            pe.wait_ge(s["kst_ready"], CHUNKS * PAIRS)
            pe.wait_ge(s["qlo_ready"], CHUNKS)
            pe.wait_ge(s["zero_ready"], 4)
            with_max(0)
            pe.wait_ge(s["qe_ready"], 1)
            qsel(1, True).then_inc(s["qsel_done"], 1)
            pe.wait_ge(s["qm_ready"], 2)
            for i in range(AHEAD):
                maxes(1, i)
            for u in range(UNITS):
                q = u // PAIRS
                for k in range(TILES):
                    v, i = divmod(16 * (u + 1) + k + AHEAD, 16)
                    if v < UNITS and i == 0:
                        pe.wait_ge(s["qm_ready"], v + 1)
                    for h in range(2):
                        scores(u, k, (h,))
                        if v < UNITS:
                            maxes(v, i, (h,))
                    if k == 2 and u >= 1:
                        dsum(u - 1)
                    if k == 5 and u >= 1 and u % PAIRS == 0:
                        attended(q - 1)
                    if k == 7 and u >= 1 and u % PAIRS == 0:
                        project(q - 1)
                    if k == 9:
                        if u >= 1:
                            pe.wait_ge(s["on_ready"], u)
                        if u >= 1 and u % PAIRS == 0:
                            pe.wait_ge(s["y_ready"], q)
                        if u + 2 < UNITS:
                            qsel(u + 2, True).then_inc(s["qsel_done"], 1)
                    if k == 13 and u + 1 < UNITS:
                        if u + 2 < UNITS:
                            pe.wait_ge(s["qm_ready"], u + 3)
                        with_max(u + 1)
                    if k % 2 == 1:
                        v, kp = divmod(u * (TILES // 2) + (k - LAG) // 2, TILES // 2)
                        if v >= 0:
                            weigh(v, kp)
                if u + 1 < UNITS:
                    pe.wait_ge(s["qe_ready"], u + 2)
            def channels3(c):
                pe.wait_ge(s["xh4_ready"], c + 1)
                transposes(B[c], lambda t: X[:, c * TPC + t, :], s["t5_done"])

            def gate_logits(c):
                for t in range(c * TPC, (c + 1) * TPC):
                    ins = pe.matmul(B[4][:, t * E0:(t + 1) * E0], S[5][:, t * P:(t + 1) * P], wf[:, 3 * D:3 * D + E0],
                                    start=True, stop=True)
                return ins

            pe.wait_ge(s["mxr_done"], 2 * TILES * UNITS)
            for c in range(CHUNKS - 1):
                channels3(c)
            weigh(UNITS - 1, TILES // 2 - 1)
            pe.wait_ge(s["on_ready"], UNITS - 1)
            dsum(UNITS - 1)
            attended(CHUNKS - 1)
            project(CHUNKS - 1)

            for c in range(CHUNKS - 1):
                pe.wait_ge(s["tT_ready"], c + 1)
                gate_logits(c)
            channels3(CHUNKS - 1)
            pe.wait_ge(s["tT_ready"], CHUNKS)
            gate_logits(CHUNKS - 1).then_inc(s["gl_done"], 1)
            pe.wait_ge(s["w_d"], 112)
            pe.wait_ge(s["cw_ready"], 1)
            chosen = cw[:, :, :].rearrange("p t e -> p (t e)")
            for k in range(2):
                ins = pe.matmul(B[5][:, k * TILES * E0:(k + 1) * TILES * E0], tri[:, k * P:(k + 1) * P], chosen,
                                start=True, stop=True)
            ins.then_inc(s["rank_done"], 1)
            pe.wait_ge(s["cw_ready"], 2)
            for t in range(TILES):
                ins = pe.transpose(B[t // TPC][0:E0, (t % TPC) * P:(t % TPC + 1) * P], gt[0][:, t, :], ID[:, :])
            ins.then_inc(s["cT_done"], 1)
            pe.wait_ge(s["cT_ready"], 1)
            for c in range(CHUNKS):
                for t in range(TPC):
                    ins = pe.matmul(B[c][:, t * D:(t + 1) * D], cT[:, (c * TPC + t) * P:(c * TPC + t + 1) * P], b2r[:, :],
                                    start=True, stop=True)
                ins.then_inc(s["acc0_done"], 1)

            def slots_over(g):
                n = min(4, XT - 4 * g)
                if g == 0:
                    pe.wait_ge(s["xs_in0"], 16)
                if g == 2:
                    pe.wait_ge(s["xs_in1"], 16)
                if g >= 2:
                    pe.wait_ge(s["tT_ready"], CHUNKS + g - 1)
                for t in range(n):
                    j = 4 * g + t
                    ins = pe.transpose(B[6 + g % 2][:, t * P:(t + 1) * P], V[:, j * D:(j + 1) * D], ID[:, :])
                ins.then_inc(s["t5_done"], 1)

            def up(j):
                pe.wait_ge(s["wc_ready"], j + 1)
                pe.wait_ge(s["tT_ready"], CHUNKS + j // 4 + 1)
                if j >= 3:
                    pe.wait_ge(s["hid_ready"], FC * (j - 2))
                for f in range(FC):
                    ins = pe.matmul(B[3 + j % 3][:, f * P:(f + 1) * P], wexp(j)[:, f * P:(f + 1) * P], xT(j), start=True,
                                    stop=True)
                ins.then_inc(s["w1_done"], 1)

            def down(j):
                if j >= 2:
                    pe.wait_ge(s["acc_ready"], j - 1)
                for f in range(FC):
                    pe.wait_ge(s["hid_ready"], FC * j + f + 1)
                    ins = pe.matmul(B[j % 2][:, 0:D], hid(j)[:, f * P:(f + 1) * P], wexp(j)[:, FF + f * D:FF + (f + 1) * D],
                                    start=f == 0, stop=f == FC - 1)
                ins.then_inc(s["w2_done"], 1)

            pe.wait_ge(s["acc0_ready"], CHUNKS)
            slots_over(0)
            up(0)
            up(1)
            for j in range(XT):
                if j % 4 == 0 and 4 * (j // 4 + 1) < XT:
                    slots_over(j // 4 + 1)
                if j + 2 < XT:
                    up(j + 2)
                down(j)

            for c in range(CHUNKS):
                pe.wait_ge(s["xh5_ready"], c + 1)
                transposes(B[c], lambda t: X[:, c * TPC + t, :], s["t6_done"])
            pe.wait_ge(s["w_l1"], 16)
            def projections(c):
                pe.wait_ge(s["x2T_ready"], c + 1)
                for k in range(4):
                    if k < 2:
                        if c >= 1:
                            pe.wait_ge(s["v1_ready"], 2 * (c - 1) + k + 1)
                        if c >= 2:
                            pe.wait_ge(s["pt_ready"], 4 * (c - 2) + 4)
                    else:
                        pe.wait_ge(s["qk_ready"], 4 * c + k - 1)
                    pe.matmul(B[4 + k % 2], wl[:, k * P:(k + 1) * P], S[5][:, ch(c)], start=True, stop=True).then_inc(s["qk_done"], 1)
                wv = wl[:, 4 * P:5 * P]
                pe.wait_ge(s["qk_ready"], 4 * c + 3)
                for t in range(TPC):
                    g = (c * TPC + t) * P
                    ins = pe.matmul(B[4][:, t * D:(t + 1) * D], S[5][:, g:g + P], wv, start=True, stop=True)
                ins.then_inc(s["v1_done"], 1)
                pe.wait_ge(s["qk_ready"], 4 * c + 4)
                for t in range(TPC):
                    for par in range(2):
                        g = (c * TPC + t) * P + WS * par
                        o = WS * (1 - par)
                        ins = pe.matmul(B[5][o:o + WS, t * D:(t + 1) * D], S[5][:, g:g + WS], wv, start=True, stop=True,
                                        tile_position=(0, o))
                ins.then_inc(s["v1_done"], 1)

            def window_scores(c):
                pe.wait_ge(s["qk_ready"], 4 * c + 4)
                for j in range(4):
                    if c == 0:
                        pe.wait_ge(s["bt_ready"], 1)
                    else:
                        pe.wait_ge(s["ns_ready"], 4 * (c - 1) + j + 1)
                for j in range(4):
                    r = slice(32 * j, 32 * j + 32)
                    for t in range(TPC):
                        for g in range(2):
                            for par in range(2):
                                x = t * P + WS * par
                                o = (2 * t + g) * WS
                                ins = pe.matmul(B[j][WS * par:WS * par + WS, o:o + WS],
                                                S[c % 2][r, g * CT + x:g * CT + x + WS],
                                                S[c % 2][r, (2 + g) * CT + x:(2 + g) * CT + x + WS],
                                                start=True, stop=True, tile_position=(32 * j, WS * par))
                    ins.then_inc(s["s_done"], 1)

            def channels(c):
                pe.wait_ge(s["xh6_ready"], c + 1)
                transposes(B[c], lambda t: tokv(5)[:, c * TPC + t, :], s["t8_done"])

            def gates_in(c):
                pe.wait_ge(s["fT_ready"], min(CHUNKS, 2 * (c // 2) + 2))
                for k in range(4):
                    m, half = divmod(k, 2)
                    if 4 * c + k >= 2:
                        pe.wait_ge(s["gb_copied"], 4 * c + k - 1)
                    x = S[5][:, ch(c)]
                    b0 = 2 * (k % 2)
                    pe.matmul(B[b0], win[:, m, half * P:(half + 1) * P], x, start=True, stop=True)
                    pe.matmul(B[b0 + 1], win[:, m, H1 + half * P:H1 + (half + 1) * P], x, start=True,
                              stop=True).then_inc(s["in_done"], 1)

            projections(0)
            pe.wait_ge(s["xm_ready"], 1)
            for k in range(4):
                ins = pe.matmul(B[6][:, k * WS:(k + 1) * WS], wl[:, k * P:(k + 1) * P], xm[:, :], start=True, stop=True)
            ins.then_inc(s["gm_done"], 1)
            projections(1)
            pe.wait_ge(s["gq_ready"], 1)
            for g in range(2):
                for j in range(4):
                    r = slice(32 * j, 32 * j + 32)
                    ins = pe.matmul(B[j][:, g * WS:(g + 1) * WS], gqb[r, g, :], km[r, g, :], start=True, stop=True,
                                    tile_position=(32 * j, 0))
            ins.then_inc(s["gb_done"], 1)

            window_scores(0)
            window_scores(1)
            for c in range(CHUNKS):
                pe.wait_ge(s["p1_ready"], c + 1)
                for k in range(4):
                    if k < 2:
                        pe.wait_ge(s["v1_ready"], 2 * min(c + 2, CHUNKS))
                        if c >= 1:
                            pe.wait_ge(s["oT_ready"] if k == 0 else s["h3_ready"], c)
                    else:
                        pe.wait_ge(s["pt_ready"], 4 * c + k - 1)
                    transposes(B[4 + k % 2], lambda t: sco2(4 + 2 * (c % 2))[:, (k * TPC + t) * P:(k * TPC + t + 1) * P], s["pt_done"])
                pe.wait_ge(s["pt_ready"], 4 * (c + 1))
                if c >= 1:
                    pe.wait_ge(s["o_ready"], c)
                for g in range(2):
                    r = slice(WS * g, WS * g + WS)
                    for t in range(TPC):
                        for j in range(4):
                            for par in range(2):
                                o = (c % 2) * T + (j * TPC + t) * P + WS * par
                                ins = pe.matmul(B[6 + g][WS * par:WS * par + WS, (t * 4 + j) * 32:(t * 4 + j + 1) * 32],
                                                PB[r, o:o + WS], vwin(c, 0 if g == par else 1)[r, t, 4 * g + j, :],
                                                start=True, stop=True, tile_position=(WS * g, WS * par))
                ins.then_inc(s["ov_done"], 1)
                if c + 2 < CHUNKS:
                    projections(c + 2)
                    window_scores(c + 2)
                if c == 2:
                    pe.wait_ge(s["ns_ready"], 4 * CHUNKS)
                    channels(0)
                    channels(1)
                    gates_in(0)
                    gates_in(1)
                pe.wait_ge(s["o_ready"], c + 1)
                if c + 2 < CHUNKS:
                    pe.wait_ge(s["v1_ready"], 2 * (c + 3))
                transposes(B[4], lambda t: tokv(4 + 2 * (c % 2))[:, t, :], s["t7_done"])
                pe.wait_ge(s["oT_ready"], c + 1)
                for t in range(TPC):
                    g = (c * TPC + t) * P
                    ins = pe.matmul(B[5][:, t * D:(t + 1) * D], S[5][:, g:g + P], wl[:, 5 * P:6 * P], start=True, stop=True)
                ins.then_inc(s["pr_done"], 1)

            pe.wait_ge(s["gb_copied"], 8)
            channels(2)
            channels(3)
            pe.wait_ge(s["fT_ready"], CHUNKS)
            pe.wait_ge(s["h3_ready"], CHUNKS)
            for t in range(TILES):
                ins = pe.matmul(B[5][:, t * (2 + E1):(t + 1) * (2 + E1)], S[5][:, t * P:(t + 1) * P], wg1[:, :],
                                start=True, stop=True)
            ins.then_inc(s["g2_done"], 1)
            gates_in(2)
            pe.wait_ge(s["c2_ready"], 1)
            for t in range(TILES):
                ins = pe.transpose(B[4 + t // TPC][0:E1, (t % TPC) * P:(t % TPC + 1) * P], gt[0][:, t, :], ID[:, :])
            ins.then_inc(s["cn_done"], 1)
            gates_in(3)
            pe.wait_ge(s["gb_copied"], 16)
            pe.wait_ge(s["cn_ready"], 1)
            pe.wait_ge(s["wex_in"], 16)
            wex = V[:, 0:2 * E1 * D].rearrange("p (k n) -> p k n", k=2)
            for c in range(CHUNKS):
                pe.wait_ge(s["hsw_ready"], 4 * c + 4)
                if c >= 1:
                    pe.wait_ge(s["xev_ready"], UNITS + c)
                for t in range(TPC):
                    dst = B[4][:, t * D:(t + 1) * D]
                    for k in range(2):
                        pe.matmul(dst, S[c][:, k * CT + t * P:k * CT + (t + 1) * P], wso[:, k, :], start=k == 0, stop=False)
                    ins = pe.matmul(dst, cT[:, (c * TPC + t) * P:(c * TPC + t + 1) * P], eob[:, :], start=False, stop=True)
                ins.then_inc(s["sh_done"], 1)
                for t in range(TPC):
                    g = c * TPC + t
                    b0 = 6 if t % 2 == 0 else 2
                    if g >= 2:
                        pe.wait_ge(s["cb_ready"], g - 1)
                    for half in range(2):
                        for k in range(2):
                            ins = pe.matmul(B[b0 + half], S[c][:, (2 + k) * CT + t * P:(2 + k) * CT + (t + 1) * P],
                                            wex[:, k, half * CT:(half + 1) * CT], start=k == 0, stop=k == 1)
                    ins.then_inc(s["ex_done"], 1)


def kernel(**inputs):
    import numpy as np
    import concourse.bacc as bacc
    from concourse.bass_utils import run_bass_kernel_spmd

    g = {k: np.asarray(v) for k, v in inputs.items()}

    def col(a):
        return np.ascontiguousarray(a).reshape(D, 1)

    f = np.float32
    pos = np.arange(1, T + 1, dtype=f)[:, None]
    i = np.arange(D)
    exponent = np.where(i % 2 == 0, i, i + 1).astype(f) / f(D)
    angle = (pos / np.power(f(10000.0), exponent)).astype(f)
    pe = np.where(i % 2 == 0, np.cos(angle), np.sin(angle)).astype(f)

    a = {}
    a["idx"] = np.ascontiguousarray(g["x"].reshape(TILES, P).T)
    a["emb"] = np.ascontiguousarray(g["L0_tok_W"].T)
    a["pe"] = np.ascontiguousarray(pe.reshape(TILES, P, D).transpose(1, 0, 2)).reshape(P, T)
    r = "L0_attn_"
    a["vec"] = np.concatenate([col(g[n]) for n in (
        r + "bk", r + "bv", r + "br", r + "bcv", r + "bcr", r + "ln1_g", r + "ln1_b", r + "ln2_g", r + "ln2_b",
        r + "time_decay", r + "time_first", r + "tmk", r + "tmv", r + "tmr", r + "cmk", r + "cmr",
        "L0_ffn_bq", "L0_ffn_bk", "L0_ffn_ln1_g", "L0_ffn_ln1_b", "L1_ffn_ln_scale", "L1_ffn_ln_bias")], 1)
    a["rows"] = np.concatenate([g["L0_tok_b"], g[r + "bo"], g["L0_ffn_bv"], g["L0_ffn_bo"], g["L0_ffn_gate_b"],
                                g["L1_attn_b_out"], g["L1_ffn_shared_out_b"], g["L1_ffn_group_bias"],
                                g["L1_ffn_expert_bias"], np.arange(E0, 0, -1).astype(f),
                                np.arange(0, T, P).astype(f), np.arange(XT).astype(f)]).reshape(1, NR)
    a["w_rwkv"] = np.concatenate([g[r + n] for n in ("Wk", "Wv", "Wr", "Wo", "Wcr")], 1)
    a["w_ck"] = g[r + "Wck"]
    a["w_cv"] = np.ascontiguousarray(g[r + "Wcv"].reshape(FC, P, D).transpose(1, 0, 2))
    a["bckc"] = np.ascontiguousarray(g[r + "bck"].reshape(FC, P).T)
    q = "L0_ffn_"
    a["w_ffn"] = np.concatenate([g[q + "Wq"], g[q + "Wk"], g[q + "Wv"], g[q + "gate_W"]], 1)
    a["w_of"] = g[q + "Wo"]
    a["tri"] = np.concatenate([np.triu(np.ones((P, P), f), 1), np.ones((P, P), f)], 1)
    a["zrow"] = np.zeros((1, D), f)
    a["ident"] = np.eye(P, dtype=f)
    rr = np.arange(P)
    cc = np.arange(2 * (HD + 1))
    a["selo"] = ((rr[:, None] // 64 == cc[None, :] // (HD + 1)) & (rr[:, None] % 32 == cc[None, :] % (HD + 1))).astype(f)
    sel = np.zeros((P, 16, P), f)
    for j in range(PAIRS):
        for dst in range(P):
            src = (2 * j + dst // 64) * HD + dst % HD
            part = dst % 64 // HD
            if part < 3:
                sel[src, (4 if part == 1 else 0) + j, dst] = 1
                sel[src, (12 if part == 2 else 8) + j, dst] = 1
    a["sel"] = sel.reshape(P, 16 * P)
    kone = np.zeros((P, 1), f)
    kone[[48, 49, 112, 113]] = 1
    a["kone"] = kone
    a["b1c"] = np.ascontiguousarray(g[q + "b1"].reshape(E0, FC, P).transpose(2, 0, 1)).reshape(P, E0 * FC)
    a["b2r"] = g[q + "b2"]
    a["moe_w1"] = np.ascontiguousarray(g[q + "W1"].transpose(1, 0, 2)).reshape(P, E0 * FF)
    a["moe_w2"] = np.ascontiguousarray(g[q + "W2"].reshape(E0, FC, P, D).transpose(2, 0, 1, 3)).reshape(P, E0 * FF)
    w = g["L1_attn_w_qkv"]
    pads = np.zeros((D, 4, 4, 32), f)
    for k in range(4):
        part = w[:, (k // 2) * D:(k // 2 + 1) * D].reshape(D, 2, 4, HD)
        pads[:, k, :, :HD] = part[:, k % 2]
    a["w_l1"] = np.concatenate([pads.reshape(D, 4 * P), w[:, 2 * D:], g["L1_attn_w_out"]], 1)
    gt = g["L1_attn_gate"].reshape(2, 4, 1)
    a["gat"] = np.ascontiguousarray(np.broadcast_to(gt, (2, 4, 32)).reshape(2, P).T)
    gp = g["L1_attn_global_param"].reshape(2, 4, 1, G1 * WS)
    a["gp"] = np.ascontiguousarray(np.broadcast_to(gp, (2, 4, 32, G1 * WS))).reshape(2, P, G1 * WS)
    a["lb"] = np.ascontiguousarray(g["L1_attn_local_bias"].reshape(2, 4, WS, WS).transpose(2, 1, 0, 3)).reshape(WS, HEADS, WS)
    d = "L1_ffn_"
    a["w_in"] = np.ascontiguousarray(np.stack([g[d + "shared_in_w"].T, g[d + "expert_in_w"].T], 1))
    a["w_so"] = np.ascontiguousarray(g[d + "shared_out_w"].T.reshape(2, P, D).transpose(1, 0, 2))
    a["w_ex"] = np.ascontiguousarray(g[d + "expert_out_weight"].transpose(2, 0, 1).reshape(2, P, E1 * D).transpose(1, 0, 2)).reshape(P, 2 * E1 * D)
    a["w_g1"] = np.ascontiguousarray(np.concatenate([g[d + "group_gate_w"], g[d + "expert_gate_w"]], 0).T)
    a["eob"] = g[d + "expert_out_bias"]

    nc = bacc.Bacc("TRN2", target_bir_lowering=False, num_devices=1)
    arrays, args = {}, {}
    for n, v in a.items():
        v = np.ascontiguousarray(v)
        arrays["in_" + n] = v
        args[n] = nc.dram_tensor("in_" + n, v.shape, mybir.dt.from_np(v.dtype), kind="ExternalInput").ap()
    out = nc.dram_tensor("out_h", (T, D), mybir.dt.float32, kind="ExternalOutput").ap()
    xs = nc.dram_tensor("slots_in", (XS, D), mybir.dt.float32, kind="Internal").ap()
    ys = nc.dram_tensor("slots_out", (XS, D), mybir.dt.float32, kind="Internal").ap()
    build_tower(nc, args, out.rearrange("(t p) d -> p t d", p=P), xs, ys)
    res = run_bass_kernel_spmd(nc, [arrays], core_ids=[0])
    return res.results[0]["out_h"].reshape(1, T, D)
```
